# Optimizing a Trainium2 kernel written in Bass

```python
import numpy as np
import jax
import jax.numpy as jnp

def _softmax(x, axis=-1):
    return jax.nn.softmax(x, axis=axis)

def _gelu(x):
    return jax.nn.gelu(x, approximate=True)

def _silu(x):
    return jax.nn.silu(x)

def _sigmoid(x):
    return jax.nn.sigmoid(x)

def _layernorm(x, axis=-1, eps=1e-05):
    m = jnp.mean(x, axis=axis, keepdims=True)
    v = jnp.var(x, axis=axis, keepdims=True)
    return (x - m) / jnp.sqrt(v + eps)

def _scatter_add(tgt, idx, src, axis=0):
    return tgt.at[idx].add(src)

def _segment_sum(src, seg, n):
    return jax.ops.segment_sum(src, seg, n)
kernel_name = 'mk_gnn_ffn_d1_gnn_r8_b2c252'

def setup_inputs(seed: int=0):
    np.random.seed(seed)
    _w = jnp.asarray

    def _rec_inputs():
        import jax
        import jax.numpy as jnp
        _gk = jax.random.key(seed)
        x = -0.0003713 + 1 * jax.random.normal(jax.random.fold_in(_gk, 1), (6250, 256), jnp.float32)
        src = jax.random.randint(jax.random.fold_in(_gk, 2), (200000,), 0, 6250, jnp.int32)
        dst = jnp.minimum((6250 * jax.random.uniform(jax.random.fold_in(_gk, 3), (200000,)) ** 2.0).astype(jnp.int32), 49999)
        _o = jnp.argsort(dst, stable=True)
        src = src[_o]
        dst = dst[_o]
        return (x, src, dst)
    x, src, dst = _rec_inputs()

    def _L0_gnn_setup():
        import jax, jax.numpy as jnp
        import numpy as np
        N_NODES = 6250
        N_EDGES = 100000
        IN_DIM = 256
        HEADS = 4
        HEAD_DIM = 64
        NEG_SLOPE = 0.2
        EPS = 1e-16
        key = jax.random.key(seed)
        k1, k2, k3, k4, k5 = jax.random.split(key, 5)
        x = jax.random.normal(k1, (N_NODES, IN_DIM), dtype=jnp.float32)
        edge_index = jax.random.randint(k2, (2, N_EDGES), 0, N_NODES, dtype=jnp.int64)
        W = jax.random.normal(k3, (IN_DIM, HEADS * HEAD_DIM), dtype=jnp.float32) * (1.0 / np.sqrt(IN_DIM))
        att_src = jax.random.normal(k4, (HEADS, HEAD_DIM), dtype=jnp.float32) * 0.1
        att_dst = jax.random.normal(k5, (HEADS, HEAD_DIM), dtype=jnp.float32) * 0.1
        bias = jnp.zeros((HEADS * HEAD_DIM,), dtype=jnp.float32)
        return {'x': x, 'edge_index': edge_index, 'W': W, 'att_src': att_src, 'att_dst': att_dst, 'bias': bias}
    _L0_gnn_all = _L0_gnn_setup()
    _L0_gnn_in = {k: v for k, v in _L0_gnn_all.items() if k in ('W', 'att_src', 'att_dst', 'bias')}
    del _L0_gnn_all

    def _L0_ffn_setup():
        import jax, jax.numpy as jnp
        import numpy as np
        E, D, H, TOP_K = (6, 256, 256, 2)
        ROUTER_H = D // 2
        key = jax.random.key(seed)
        ks = jax.random.split(key, 12)
        s = 1.0 / np.sqrt(D)
        sh = 1.0 / np.sqrt(H)
        sr = 1.0 / np.sqrt(ROUTER_H)
        return {'features': jax.random.normal(ks[0], (8, 512, D), dtype=jnp.float32), 'router_w1': jax.random.uniform(ks[1], (D, ROUTER_H), jnp.float32, -s, s), 'router_b1': jnp.zeros((ROUTER_H,), jnp.float32), 'router_w2': jax.random.uniform(ks[2], (ROUTER_H, E), jnp.float32, -sr, sr), 'router_b2': jnp.zeros((E,), jnp.float32), 'expert_w1': jax.random.uniform(ks[3], (E, D, H), jnp.float32, -s, s), 'expert_b1': jnp.zeros((E, H), jnp.float32), 'expert_w2': jax.random.uniform(ks[4], (E, H, H), jnp.float32, -sh, sh), 'expert_b2': jnp.zeros((E, H), jnp.float32), 'expert_w3': jax.random.uniform(ks[5], (E, H, D), jnp.float32, -sh, sh), 'expert_b3': jnp.zeros((E, D), jnp.float32)}
    _L0_ffn_all = _L0_ffn_setup()
    _L0_ffn_in = {k: v for k, v in _L0_ffn_all.items() if k in ('router_w1', 'router_b1', 'router_w2', 'router_b2', 'expert_w1', 'expert_b1', 'expert_w2', 'expert_b2', 'expert_w3', 'expert_b3')}
    del _L0_ffn_all
    return {'x': x, 'src': src, 'dst': dst, 'L0_gnn_W': _L0_gnn_in['W'], 'L0_gnn_att_src': _L0_gnn_in['att_src'], 'L0_gnn_att_dst': _L0_gnn_in['att_dst'], 'L0_gnn_bias': _L0_gnn_in['bias'], 'L0_ffn_router_w1': _L0_ffn_in['router_w1'], 'L0_ffn_router_b1': _L0_ffn_in['router_b1'], 'L0_ffn_router_w2': _L0_ffn_in['router_w2'], 'L0_ffn_router_b2': _L0_ffn_in['router_b2'], 'L0_ffn_expert_w1': _L0_ffn_in['expert_w1'], 'L0_ffn_expert_b1': _L0_ffn_in['expert_b1'], 'L0_ffn_expert_w2': _L0_ffn_in['expert_w2'], 'L0_ffn_expert_b2': _L0_ffn_in['expert_b2'], 'L0_ffn_expert_w3': _L0_ffn_in['expert_w3'], 'L0_ffn_expert_b3': _L0_ffn_in['expert_b3']}

def reference(x, src, dst, L0_gnn_W, L0_gnn_att_src, L0_gnn_att_dst, L0_gnn_bias, L0_ffn_router_w1, L0_ffn_router_b1, L0_ffn_router_w2, L0_ffn_router_b2, L0_ffn_expert_w1, L0_ffn_expert_b1, L0_ffn_expert_w2, L0_ffn_expert_b2, L0_ffn_expert_w3, L0_ffn_expert_b3):
    import jax
    import jax.numpy as jnp

    def _L0_gnn_ref(x, edge_index, W, att_src, att_dst, bias):
        import jax, jax.numpy as jnp
        import numpy as np
        N_NODES = 6250
        N_EDGES = 100000
        IN_DIM = 256
        HEADS = 4
        HEAD_DIM = 64
        NEG_SLOPE = 0.2
        EPS = 1e-16
        N = x.shape[0]
        loops = jnp.arange(N, dtype=edge_index.dtype)
        src = jnp.concatenate([edge_index[0], loops])
        dst = jnp.concatenate([edge_index[1], loops])
        h = (x @ W).reshape(N, HEADS, HEAD_DIM)
        alpha_s = jnp.einsum('nhc,hc->nh', h, att_src)
        alpha_d = jnp.einsum('nhc,hc->nh', h, att_dst)
        e = alpha_s[src] + alpha_d[dst]
        e = jax.nn.leaky_relu(e, negative_slope=NEG_SLOPE)
        m = jax.ops.segment_max(e, dst, num_segments=N)
        ex = jnp.exp(e - m[dst])
        s = jax.ops.segment_sum(ex, dst, num_segments=N)
        alpha = ex / (s[dst] + EPS)
        msg = h[src] * alpha[:, :, None]
        out = jax.ops.segment_sum(msg, dst, num_segments=N)
        return out.reshape(N, HEADS * HEAD_DIM) + bias

    def _L0_ffn_ref(features, router_w1, router_b1, router_w2, router_b2, expert_w1, expert_b1, expert_w2, expert_b2, expert_w3, expert_b3):
        import jax, jax.numpy as jnp
        import numpy as np
        E, D, H, TOP_K = (6, 256, 256, 2)
        ROUTER_H = D // 2
        rh = jax.nn.relu(features @ router_w1 + router_b1)
        expert_logits = jax.nn.softmax(rh @ router_w2 + router_b2, axis=-1)
        top_w, top_i = jax.lax.top_k(expert_logits, TOP_K)
        routing_weights = jax.nn.softmax(top_w, axis=-1)
        h1 = jax.nn.relu(jnp.einsum('bsd,edh->bseh', features, expert_w1) + expert_b1)
        h2 = jax.nn.relu(jnp.einsum('bseh,ehf->bsef', h1, expert_w2) + expert_b2)
        expert_out = jnp.einsum('bsef,efo->bseo', h2, expert_w3) + expert_b3
        sel = jnp.take_along_axis(expert_out, top_i[:, :, :, None], axis=2)
        combined = jnp.sum(sel * routing_weights[..., None], axis=2)
        return combined
    edge_index = jnp.stack([src, dst])
    x = x + _L0_gnn_ref(_layernorm(x, axis=-1), edge_index, L0_gnn_W, L0_gnn_att_src, L0_gnn_att_dst, L0_gnn_bias)
    x = x + _L0_ffn_ref(_layernorm(x, axis=-1)[None], L0_ffn_router_w1, L0_ffn_router_b1, L0_ffn_router_w2, L0_ffn_router_b2, L0_ffn_expert_w1, L0_ffn_expert_b1, L0_ffn_expert_w2, L0_ffn_expert_b2, L0_ffn_expert_w3, L0_ffn_expert_b3)[0]
    return x

_drawn_inputs = setup_inputs


def setup_inputs(seed=0):
    import zlib

    import numpy as np

    out = dict(_drawn_inputs(seed))
    spreads = {'L0_gnn_bias': (0.0, 0.1),
     'L0_ffn_router_b1': (0.0, 0.1),
     'L0_ffn_router_b2': (0.0, 0.1),
     'L0_ffn_expert_b1': (0.0, 0.706),
     'L0_ffn_expert_b2': (0.0, 0.299),
     'L0_ffn_expert_b3': (0.0, 0.1)}
    factors = {}
    for name, (base, spread) in spreads.items():
        noise = np.random.default_rng([zlib.crc32(name.encode()), seed]).standard_normal(out[name].shape)
        drawn = base * np.exp(spread * noise) if base else spread * noise
        out[name] = jnp.asarray(drawn.astype(out[name].dtype))
    for name, factor in factors.items():
        out[name] = (out[name] * factor).astype(out[name].dtype)
    return out
```

```python
from contextlib import ExitStack

import concourse.bass as bass
from concourse import mybir

N_NODES, DIM, N_EDGES = 6250, 256, 200000
HEADS, HEAD_DIM = 4, 64
EXPERTS, ROUTER_H = 6, 128
SLOPE, LN_EPS, SUM_EPS = 0.2, 1e-5, 1e-16
P = 128

NW = -(-N_NODES // P)
LAST_ROWS = N_NODES - (NW - 1) * P
TILES = 4
GE = TILES * P
NG = -(-N_EDGES // GE)
UNROLL = 6
STEPS = -(-(NG + NW - 1) // UNROLL) * UNROLL
CHUNKS = 4
assert STEPS <= CHUNKS * P and NG <= CHUNKS * P
HC = HEAD_DIM + 1
ROW = HEADS * HC
BIG = 1.0e30
PAD_DST = 1 << 20
BW = 7
NB = NW // BW
BN = BW * P
HALF = BN // 2


STAGES = NB * EXPERTS


def phase3_order():
    order = [("front", 0), ("h1", 0)]
    for s in range(STAGES):
        if s % EXPERTS == 2 and s // EXPERTS + 1 < NB:
            order.append(("front", s // EXPERTS + 1))
        if s + 1 < STAGES:
            order.append(("h1", s + 1))
        order.append(("h2", s))
        if s:
            order.append(("out", s - 1))
    return order + [("out", STAGES - 1)]


hidden_done = {}
for _part in phase3_order():
    if _part[0] in ("h1", "h2"):
        hidden_done[_part] = 4 * (len(hidden_done) + 1)


def gnn_moe_program(nc, x, src, dst, gat_w, att_src, att_dst, gat_bias, r_w1, r_b1, r_w2, r_b2,
                    e_w1, e_b1, e_w2, e_b2, e_w3, e_b3, out):
    f32, i32 = mybir.dt.float32, mybir.dt.int32
    ALU, ACT, AX = mybir.AluOpType, mybir.ActivationFunctionType, mybir.AxisListType

    src_pad = nc.dram_tensor("src_pad", [NG + 1, GE], i32, kind="Internal").ap()
    dst_pad = nc.dram_tensor("dst_pad", [NG + 1, GE], i32, kind="Internal").ap()
    node_rows = nc.dram_tensor("node_rows", [NW * P, ROW], f32, kind="Internal").ap()
    flag_rows = nc.dram_tensor("flag_rows", [CHUNKS * P, TILES, HEADS, P], f32, kind="Internal").ap()
    window_list = nc.dram_tensor("window_list", [CHUNKS * P], i32, kind="Internal").ap()

    with ExitStack() as ctx:
        def sb(name, cols, dt=f32, parts=P):
            return ctx.enter_context(nc.sbuf_tensor(name, [parts, cols], dt))

        def sem(name):
            return ctx.enter_context(nc.semaphore(name))

        def sems(name, n):
            return [sem(f"{name}{i}") for i in range(n)]

        acc = sb("acc", NW * ROW)
        state = sb("state", NW * 8)
        ident = sb("ident", P)
        iota_row = sb("iota_row", P)
        waug = sb("waug", 2 * (ROW + HEADS))
        ew1, ew2, ew3 = (sb(f"ew{i}", EXPERTS * 2 * 256) for i in (1, 2, 3))
        eb1, eb2 = (sb(f"eb{i}", EXPERTS * 2) for i in (1, 2))
        eb3 = sb("eb3", EXPERTS * DIM)
        rw1, rb1, rw2, rb2 = sb("rw1", 2 * ROUTER_H), sb("rb1", 1), sb("rw2", EXPERTS), sb("rb2", EXPERTS)
        gbias = sb("gbias", DIM)
        eps = sb("eps", 1)

        arena = sb("arena", UNROLL * (TILES * ROW + 2 * TILES * P))
        rows_at, oh_at = 0, UNROLL * TILES * ROW
        oht_at = oh_at + UNROLL * TILES * P
        column_data = sb("column_data", 3 * CHUNKS * P * TILES)
        rel_col = column_data[:, 0:2048].rearrange("p (s j) -> p s j", j=TILES)
        end_col = column_data[:, 2048:4096].rearrange("p (s j) -> p s j", j=TILES)
        src_col = column_data[:, 4096:6144].rearrange("p (s j) -> p s j", j=TILES)
        flag_ring = sb("flag_ring", UNROLL * P, parts=16)
        scan_ring = sb("scan_ring", UNROLL * P, parts=16)
        idx_ring = sb("idx_ring", UNROLL * TILES, i32)
        seg_ring = sb("seg_ring", UNROLL * TILES * 5)
        node_ring = sb("node_ring", UNROLL * 12)
        cand = sb("cand", 16)
        absent = sb("absent", TILES)
        top = sb("top", HEADS)
        top_e = sb("top_e", HEADS)
        fall = sb("fall", UNROLL * HEADS)
        keep = sb("keep", UNROLL * HEADS)
        zsum = sb("zsum", 16)
        zlr = sb("zlr", 16)
        zexp = sb("zexp", UNROLL * 16)
        wexp = sb("wexp", UNROLL * 16)
        windows = sb("windows", CHUNKS * P, i32, parts=1)

        def rows(u):
            return arena[:, rows_at + u * TILES * ROW:rows_at + (u + 1) * TILES * ROW]

        def onehot(u):
            return arena[:, oh_at + u * TILES * P:oh_at + (u + 1) * TILES * P]

        def onehot_t(u):
            return arena[:, oht_at + u * TILES * P:oht_at + (u + 1) * TILES * P]

        dst_i = arena[:, 0:2048].bitcast(i32)
        src_i = arena[:, 2048:4096].bitcast(i32)
        rel_q = arena[:, 4096:6144]
        change = arena[:, 6144:8192 + 4]
        end_q = arena[:, 8200:10248]
        src_f = arena[:, 10248:12296]
        before = column_data[:, 0:2048]
        iota_step = column_data[:, 2048:2560]
        tri = column_data[:, 2560:2688]
        ones = column_data[:, 2688:2816]
        small = sb("small", 96)
        step_no = small[:, 0:4]
        width = small[:, 4:12].rearrange("p (c two) -> p c two", two=2)
        shifted = small[:, 12:16]
        cum = small[:, 16:20]
        found = small[:, 20:28]
        win_f = small[:, 28:32]
        neg_w = small[:, 32:36]
        prev_f = small[:, 36:44]
        ints = sb("ints", 40, i32)
        prev_first, prev_last = ints[:, 0:4], ints[:, 4:8]
        prev_first_w, prev_last_w = ints[:, 8:12], ints[:, 12:16]
        group_no, win_i, first_w = ints[:, 16:20], ints[:, 20:24], ints[:, 24:28]
        pads = sb("pads", 2 * GE, i32, parts=1)

        xin, xn0, xnt0 = arena[:, 4096:5120], arena[:, 5120:5632], arena[:, 5632:6144]
        attb, att_prod = arena[:, 6144:6656], arena[:, 6656:6912]
        stats0 = sb("stats0", 2 * 12)
        ynt = [arena[:, i * 2 * BN:(i + 1) * 2 * BN] for i in (0, 1)]
        h1t = [arena[:, (2 + i) * 2 * BN:(3 + i) * 2 * BN] for i in (0, 1)]
        h2t = [arena[:, (4 + i) * 2 * BN:(5 + i) * 2 * BN] for i in (0, 1)]
        xblk = [column_data[:, i * BW * DIM:(i + 1) * BW * DIM] for i in (0, 1)]
        y = [sb(f"y{i}", BW * DIM) for i in (0, 1)]
        yn = column_data[:, 2 * BW * DIM:3 * BW * DIM]
        rht = arena[:, 12 * BN:13 * BN]
        stats3 = sb("stats3", BW * 6)
        mv3 = sb("mv3", BW * 2)
        rsum = sb("rsum", 2 * BW)
        rsum28 = sb("rsum28", BW * HEADS)
        gate = [sb(f"gate{i}", BW * EXPERTS) for i in (0, 1)]
        rt = sb("rt", 12 * BW * EXPERTS)
        rev = sb("rev", BW * EXPERTS)

        bank = [ctx.enter_context(nc.psum_tensor(f"bank{i}", [P, 512], f32)) for i in range(8)]

        gat_in, bounds_ready = sem("gat_in"), sem("bounds_ready")
        weights_in, xblk_in = sem("weights_in"), sems("xblk_in", 2)
        consts = sem("consts")
        const_step = sem("const_step")
        dve_link, act_prep = sem("dve_link"), sem("act_prep")
        pads_set = sem("pads_set")
        edges_copied, bounds_in = sem("edges_copied"), sem("bounds_in")
        cum_ps, before_set, found_ps, groups_set = sem("cum_ps"), sem("before_set"), sem("found_ps"), sem("groups_set")
        group_rows_in = sem("group_rows_in")
        sched_set, flags_out, windows_out, windows_in = sem("sched_set"), sem("flags_out"), sem("windows_out"), sem("windows_in")
        col_ps, col_copied = sem("col_ps"), sem("col_copied")
        x_in = sems("x_in", 4)
        p1_stats, p1_mv, p1_std, p1_rstd, p1_mean, p1_xn = (sem(f"p1_{n}") for n in ("stats", "mv", "std", "rstd", "mean", "xn"))
        p1_xt_ps, p1_xt, p1_h, p1_acc, p1_ad = (sem(f"p1_{n}") for n in ("xt_ps", "xt", "h", "acc", "ad"))
        node_rows_out, waug_set, init_set = sem("node_rows_out"), sem("waug_set"), sem("init_set")

        idx_ready = sem("idx_ready")
        rows_in = sems("rows_in", UNROLL)
        flags_in = sems("flags_in", UNROLL)
        (onehot_set, oht_ps, oht_set, score_ps, scanned, scan_ps, seg_set, endcol_set, px_ps, cur_set, absent_set,
         cand_set, top_set, tope_set, lr_set, newmax_set, fall_set, keep_set, max_stored, ex_ps, zsum_set, zlr_set,
         z_set, wexp_set, w_set, msg_set, agg_ps, scaled, added) = (
            sem(n) for n in ("onehot_set oht_ps oht_set score_ps scanned scan_ps seg_set endcol_set px_ps cur_set "
                             "absent_set cand_set top_set tope_set lr_set newmax_set fall_set keep_set max_stored "
                             "ex_ps zsum_set zlr_set z_set wexp_set w_set msg_set agg_ps scaled added").split())
        p3_link = sem("p3_link")
        p3_var, p3_std, p3_yn, p3_yt_ps, p3_yt, p3_rh_ps, p3_rh, p3_lg_ps = (
            sem(f"p3_{n}") for n in ("var", "std", "yn", "yt_ps", "yt", "rh_ps", "rh", "lg_ps"))
        p3_ex_in, p3_ex_out, p3_e2_in, p3_e2_out = (sem(f"p3_{n}") for n in ("ex_in", "ex_out", "e2_in", "e2_out"))
        h_ps, h_set, o_ps, o_used = sem("h_ps"), sem("h_set"), sem("o_ps"), sem("o_used")
        block_done, out_sem = sem("block_done"), sem("out_sem")

        block = ctx.enter_context(nc.Block())

        N_BOUNDS = 8
        N_WEIGHTS = 4 + 3 * EXPERTS + 3 + 1

        @block.sync
        def _(sp):
            sp.wait_ge(pads_set, 2)
            flat_s = src_pad.rearrange("g e -> (g e)")
            flat_d = dst_pad.rearrange("g e -> (g e)")
            sp.dma_start(flat_d[GE:GE + N_EDGES], dst).then_inc(edges_copied, 16)
            sp.dma_start(flat_s[GE:GE + N_EDGES], src).then_inc(edges_copied, 16)
            tail = (NG + 1) * GE - GE - N_EDGES
            sp.dma_start(flat_d[0:GE].unsqueeze(0), pads[0:1, 0:GE]).then_inc(edges_copied, 16)
            sp.dma_start(flat_d[GE + N_EDGES:(NG + 1) * GE].unsqueeze(0), pads[0:1, GE:GE + tail]).then_inc(edges_copied, 16)
            sp.dma_start(flat_s[0:GE].unsqueeze(0), pads[0:1, 0:GE]).then_inc(edges_copied, 16)
            sp.dma_start(flat_s[GE + N_EDGES:(NG + 1) * GE].unsqueeze(0), pads[0:1, 0:tail]).then_inc(edges_copied, 16)
            for k in range(2):
                o = k * (ROW + HEADS)
                sp.dma_start(waug[:, o:o + ROW].rearrange("p (h c) -> p h c", c=HC)[:, :, 0:HEAD_DIM],
                             gat_w[k * P:(k + 1) * P, :].rearrange("p (h c) -> p h c", c=HEAD_DIM)).then_inc(gat_in, 16)
            sp.dma_start(attb[:, 0:DIM], att_src.rearrange("h c -> (h c)").partition_broadcast(P)).then_inc(gat_in, 16)
            sp.dma_start(attb[:, DIM:2 * DIM], att_dst.rearrange("h c -> (h c)").partition_broadcast(P)).then_inc(gat_in, 16)
            sp.dma_start(gbias[:, :], gat_bias.partition_broadcast(P)).then_inc(gat_in, 16)

            def load_x(t, slot, n):
                sp.dma_start(xin[0:n, slot * DIM:(slot + 1) * DIM], x[bass.ds(t * P, n), :]).then_inc(x_in[slot], 16)

            for t in range(4):
                load_x(t, t, P)
            sp.wait_ge(edges_copied, 96)
            sp.wait_ge(bounds_ready, 1)
            with nc.allow_non_contiguous_dma(reason="one word per group"):
                for c in range(CHUNKS):
                    n = min(P, NG - c * P)
                    sp.dma_start(prev_first[0:n, c:c + 1], dst_pad[c * P:c * P + n, 0:1]).then_inc(bounds_in, 16)
                    sp.dma_start(prev_last[0:n, c:c + 1], dst_pad[c * P:c * P + n, GE - 1:GE]).then_inc(bounds_in, 16)

            def store_node_rows(t):
                sp.wait_ge(p1_acc, t + 1)
                sp.dma_start(node_rows[bass.ds(t * P, P), :], acc[:, bass.ds(t * ROW, ROW)]).then_inc(node_rows_out, 16)

            with sp.Fori(1, NW // 4) as it:
                for q in range(4):
                    sp.wait_ge(p1_xn, it * 4 + (q - 3))
                    load_x(it * 4 + q, q, P)
                    store_node_rows(it * 4 + (q - 4))
            for t in range(NW - NW % 4, NW):
                sp.wait_ge(p1_xn, t - 3)
                load_x(t, t % 4, P if t < NW - 1 else LAST_ROWS)
            for t in range(NW // 4 * 4 - 4, NW):
                store_node_rows(t)
            for k in range(2):
                sp.dma_start(rw1[:, k * ROUTER_H:(k + 1) * ROUTER_H], r_w1[k * P:(k + 1) * P, :]).then_inc(weights_in, 16)
            sp.dma_start(rw2[:, :], r_w2).then_inc(weights_in, 16)
            sp.dma_start(rb2[:, :], r_b2.partition_broadcast(P)).then_inc(weights_in, 16)
            for e in range(EXPERTS):
                for w, d in ((ew1, e_w1), (ew2, e_w2), (ew3, e_w3)):
                    sp.dma_start(w[:, e * 512:(e + 1) * 512].rearrange("p (k n) -> p k n", k=2),
                                 d[e, :, :].rearrange("(k p) n -> p k n", p=P)).then_inc(weights_in, 16)
            with nc.allow_non_contiguous_dma(reason="biases one word per partition"):
                sp.dma_start(rb1[:, :], r_b1.rearrange("(p o) -> p o", o=1)).then_inc(weights_in, 16)
                sp.dma_start(eb1[:, :].rearrange("p (e m) -> p e m", m=2), e_b1.rearrange("e (m p) -> p e m", p=P)).then_inc(weights_in, 16)
                sp.dma_start(eb2[:, :].rearrange("p (e m) -> p e m", m=2), e_b2.rearrange("e (m p) -> p e m", p=P)).then_inc(weights_in, 16)
            sp.dma_start(eb3[:, :], e_b3.rearrange("e d -> (e d)").partition_broadcast(P)).then_inc(weights_in, 16)
            sp.wait_ge(sched_set, 1)
            for q in range(CHUNKS):
                for h in range(HEADS):
                    sp.dma_start(flag_rows[q * P:(q + 1) * P, :, h, :],
                                 change[:, q * GE:(q + 1) * GE].rearrange("p (j e) -> p j e", j=TILES)).then_inc(flags_out, 16)
            with nc.allow_non_contiguous_dma(reason="one word per step"):
                sp.dma_start(window_list.rearrange("(q p) -> p q", p=P), win_i).then_inc(windows_out, 16)
            sp.wait_ge(windows_out, 16)
            sp.dma_start(windows[0:1, :], window_list.unsqueeze(0)).then_inc(windows_in, 16)
            sp.wait_ge(flags_out, 16 * CHUNKS * HEADS)

            def load_flags(s, u):
                sp.dma_start(flag_ring[:, u * P:(u + 1) * P],
                             flag_rows[bass.ds(s, 1), :, :, :].rearrange("s j h e -> (s j h) e")).then_inc(flags_in[u], 16)

            for s in range(UNROLL):
                load_flags(s, s)
            with sp.Fori(1, STEPS // UNROLL) as it:
                for u in range(UNROLL):
                    sp.wait_ge(scanned, it * UNROLL + (u - UNROLL + 1))
                    load_flags(it * UNROLL + u, u)

            def load_block(b):
                full = BW if b < NB - 1 else BW - 1
                sp.dma_start(xblk[b % 2][:, 0:full * DIM].rearrange("p (t d) -> p t d", d=DIM),
                             x[b * BN:b * BN + full * P, :].rearrange("(t p) d -> p t d", p=P)).then_inc(xblk_in[b % 2], 16)
                if full < BW:
                    sp.dma_start(xblk[b % 2][0:LAST_ROWS, full * DIM:BW * DIM],
                                 x[(NW - 1) * P:N_NODES, :]).then_inc(xblk_in[b % 2], 16)

            sp.wait_ge(onehot_set, STEPS)
            sp.wait_ge(endcol_set, STEPS)
            sp.wait_ge(seg_set, STEPS)
            sp.wait_ge(idx_ready, STEPS)
            load_block(0)
            load_block(1)
            for b in range(NB):
                sp.wait_ge(block_done, b + 1)
                full = BW if b < NB - 1 else BW - 1
                sp.dma_start(out[b * BN:b * BN + full * P, :].rearrange("(t p) d -> p t d", p=P),
                             y[b % 2][:, 0:full * DIM].rearrange("p (t d) -> p t d", d=DIM)).then_inc(out_sem, 16)
                if full < BW:
                    sp.dma_start(out[(NW - 1) * P:N_NODES, :], y[b % 2][0:LAST_ROWS, full * DIM:BW * DIM]).then_inc(out_sem, 16)
                if b + 2 < NB:
                    load_block(b + 2)
            sp.wait_ge(out_sem, 16 * (NB + 1))

        @block.gpsimd
        def _(pool):
            pool.memset(pads[0:1, 0:GE], 0).then_inc(pads_set, 1)
            pool.memset(pads[0:1, GE:2 * GE], PAD_DST).then_inc(pads_set, 1)
            pool.memset(ident[:, :], 0.0).then_inc(const_step, 1)
            pool.memset(tri, 1.0).then_inc(const_step, 1)
            pool.wait_ge(const_step, 2)
            pool.affine_select(out=ident[:, :], in_=ident[:, :], compare_op=ALU.not_equal, fill=1.0,
                               base=0, pattern=[[-1, P]], channel_multiplier=1).then_inc(consts, 1)
            pool.affine_select(out=tri, in_=tri, compare_op=ALU.is_ge, fill=0.0,
                               base=0, pattern=[[1, P]], channel_multiplier=-1).then_inc(consts, 1)
            pool.iota(iota_row[:, :], [[1, P]], base=0, channel_multiplier=0,
                      allow_small_or_imprecise_dtypes=True).then_inc(consts, 1)
            pool.iota(iota_step, [[1, CHUNKS * P]], base=1, channel_multiplier=0,
                      allow_small_or_imprecise_dtypes=True).then_inc(consts, 1)
            pool.iota(step_no, [[P, CHUNKS]], base=1, channel_multiplier=1,
                      allow_small_or_imprecise_dtypes=True).then_inc(consts, 1)
            pool.iota(rev[:, :], [[0, BW], [-1, EXPERTS]], base=EXPERTS, channel_multiplier=0,
                      allow_small_or_imprecise_dtypes=True).then_inc(consts, 1)
            pool.memset(ones, 1.0).then_inc(consts, 1)
            pool.memset(eps[:, :], LN_EPS).then_inc(consts, 1)
            pool.wait_ge(groups_set, 1)
            for q in range(CHUNKS):
                for to, table in ((dst_i, dst_pad), (src_i, src_pad)):
                    pool.indirect_dma_start(to[:, q * GE:(q + 1) * GE], None, table,
                                            bass.IndirectOffsetOnAxis(ap=group_no[:, q:q + 1], axis=0)).then_inc(group_rows_in, 16)
            pool.wait_ge(node_rows_out, 16 * NW)

            def gather(u):
                for j in range(TILES):
                    pool.indirect_dma_start(rows(u)[:, j * ROW:(j + 1) * ROW], None, node_rows,
                                            bass.IndirectOffsetOnAxis(ap=idx_ring[:, u * TILES + j:u * TILES + j + 1], axis=0)
                                            ).then_inc(rows_in[u], 16)

            for u in range(UNROLL):
                pool.wait_ge(idx_ready, u + 1)
                gather(u)
            with pool.Fori(1, STEPS // UNROLL) as it:
                for u in range(UNROLL):
                    pool.wait_ge(idx_ready, it * UNROLL + (u + 1))
                    pool.wait_ge(agg_ps, it * UNROLL + (u - UNROLL + 1))
                    pool.nop(nofuse=True)
                    gather(u)

        FIRST_IT, LAST_IT = 2, STEPS // UNROLL - 1

        def iterate(eng, body):
            for k in range(-1, FIRST_IT * UNROLL):
                body(k // UNROLL, k % UNROLL, lambda off: 0 <= k + off < STEPS)
            with eng.Fori(FIRST_IT, LAST_IT) as it:
                for u in range(UNROLL):
                    body(it, u, lambda off: True)
            for k in range(LAST_IT * UNROLL, STEPS + 2):
                body(k // UNROLL, k % UNROLL, lambda off: 0 <= k + off < STEPS)

        @block.scalar
        def _(act):
            def p1_act(t, s):
                act.wait_ge(p1_mv, t + 1)
                act.activation(stats0[:, s * 12 + 8:s * 12 + 9], stats0[:, s * 12 + 7:s * 12 + 8], ACT.Sqrt,
                               bias=eps[:, 0:1]).then_inc(p1_std, 1)
                act.wait_ge(p1_xt_ps, t + 1)
                act.activation(xnt0[:, s * DIM:(s + 1) * DIM], bank[s][:, 0:DIM], ACT.Copy).then_inc(p1_xt, 1)

            act.wait_ge(consts, 8)
            with act.Fori(0, NW // 2) as it:
                for s in range(2):
                    p1_act(it * 2 + s, s)
            p1_act(NW - 1, 0)
            n = 0
            for q in range(CHUNKS):
                for to in (rel_col, end_col, src_col):
                    act.wait_ge(col_ps, n + 1)
                    act.activation(to[:, q * P:(q + 1) * P, :].rearrange("p s j -> p j s"),
                                   bank[4 + n % 2][:, :].rearrange("p (j s) -> p j s", j=TILES), ACT.Copy).then_inc(col_copied, 1)
                    n += 1
            act.wait_ge(col_copied, n)
            act.wait_ge(flags_out, 16 * CHUNKS * HEADS)

            def stage_index(it, u):
                act.activation(idx_ring[:, u * TILES:(u + 1) * TILES], src_col[:, bass.ds(it * UNROLL + u, 1), :].rearrange("p s j -> p (s j)"),
                               ACT.Copy).then_inc(idx_ready, 1)

            for u in range(2):
                stage_index(0, u)

            def act_iter(it, u, on):
                k = it * UNROLL + u
                if on(3):
                    it3, u3 = it + (u + 3) // UNROLL, (u + 3) % UNROLL
                    if not isinstance(it3, int) or it3 > 0:
                        act.wait_ge(rows_in[u3], it3 * (16 * TILES))
                    stage_index(it3, u3)
                if on(-1):
                    v = (u - 1) % UNROLL
                    act.wait_ge(z_set, k)
                    act.activation(wexp[:, v * 16:v * 16 + 16], zexp[:, v * 16:v * 16 + 16], ACT.Exp).then_inc(wexp_set, 1)
                if on(1):
                    v = (u + 1) % UNROLL
                    act.wait_ge(oht_ps, k + 2)
                    act.activation(onehot_t(v), bank[v % 2][:, :], ACT.Copy).then_inc(oht_set, 1)
                    act.activation(seg_ring[:, v * 20:v * 20 + 20].rearrange("p (j c) -> p j c", c=5)[:, :, 4:5],
                                   end_col[:, bass.ds(k + 1, 1), :].rearrange("p s j -> p j s"), ACT.Copy).then_inc(endcol_set, 1)
                if on(0):
                    act.wait_ge(fall_set, k + 1)
                    act.activation(keep[:, u * HEADS:(u + 1) * HEADS], fall[:, u * HEADS:(u + 1) * HEADS], ACT.Exp).then_inc(keep_set, 1)

            iterate(act, act_iter)

            act.wait_ge(weights_in, 16 * N_WEIGHTS)
            nh = [0]

            def front_act(b):
                act.wait_ge(p3_var, b + 1)
                act.activation(rsum[:, 0:BW], mv3[:, :].rearrange("p (t two) -> p t two", two=2)[:, :, 1:2].rearrange("p t o -> p (t o)"),
                               ACT.Sqrt, bias=eps[:, 0:1]).then_inc(p3_std, 1)
                for g in range(4):
                    nt = 4 if g < 3 else 2
                    act.wait_ge(p3_yt_ps, 4 * b + g + 1)
                    for i in range(nt):
                        tk = 4 * g + i
                        t, kk = tk // 2, tk % 2
                        last = act.activation(ynt[b % 2][:, kk * BN + t * P:kk * BN + (t + 1) * P],
                                              bank[6 + g % 2][:, i * P:(i + 1) * P], ACT.Copy)
                    last.then_inc(p3_yt, 1)
                for half in range(2):
                    act.wait_ge(p3_rh_ps, 2 * b + half + 1)
                    act.activation(rht[:, half * HALF:(half + 1) * HALF], bank[6 + half][:, 0:HALF], ACT.Relu,
                                   bias=rb1[:, 0:1]).then_inc(p3_rh, 1)
                act.wait_ge(p3_ex_in, b + 1)
                act.activation(rt[:, 42:84], rt[:, 0:42], ACT.Exp).then_inc(p3_ex_out, 1)
                act.wait_ge(p3_e2_in, b + 1)
                act.activation(rt[:, 7 * 42 + 7:7 * 42 + 14], rt[:, 7 * 42:7 * 42 + 7], ACT.Exp).then_inc(p3_e2_out, 1)

            def hidden_act(s, layer):
                e = s % EXPERTS
                to = (h1t, h2t)[layer][s % 2]
                bias = (eb1, eb2)[layer]
                for m in range(2):
                    for half in range(2):
                        act.wait_ge(h_ps, nh[0] + 1)
                        act.activation(to[:, m * BN + half * HALF:m * BN + (half + 1) * HALF], bank[nh[0] % 4][:, 0:HALF],
                                       ACT.Relu, bias=bias[:, 2 * e + m:2 * e + m + 1]).then_inc(h_set, 1)
                        nh[0] += 1

            for kind, arg in phase3_order():
                if kind == "front":
                    front_act(arg)
                elif kind != "out":
                    hidden_act(arg, 0 if kind == "h1" else 1)

        @block.tensor
        def _(pe):
            pe.wait_ge(consts, 8)
            pe.wait_ge(before_set, 1)
            pe.matmul(bank[6][:, 0:CHUNKS], tri, width[:, :, 1:2].rearrange("p c o -> p (c o)"), start=True, stop=False)
            pe.matmul(bank[6][:, 0:CHUNKS], ones, shifted, start=False, stop=True).then_inc(cum_ps, 1)
            pe.wait_ge(before_set, 2)
            for q in range(CHUNKS):
                for c in range(CHUNKS):
                    last = pe.matmul(bank[7][:, 2 * q:2 * q + 2], before[:, c * 512 + q * P:c * 512 + (q + 1) * P],
                                     width[:, c, :], start=(c == 0), stop=(c == CHUNKS - 1))
            last.then_inc(found_ps, 1)

            def p1_pe(t, s, lag):
                pe.wait_ge(p1_xn, t + 1)
                if lag:
                    pe.wait_ge(p1_xt, t - 1)
                for kk in range(2):
                    last = pe.transpose(bank[s][:, kk * P:(kk + 1) * P], xn0[:, s * DIM + kk * P:s * DIM + (kk + 1) * P], ident[:, :])
                last.then_inc(p1_xt_ps, 1)
                pe.wait_ge(p1_xt, t + 1)
                if lag:
                    pe.wait_ge(p1_ad, t - 1)
                for kk in range(2):
                    last = pe.matmul(bank[2 + s][:, 0:ROW + HEADS], xnt0[:, s * DIM + kk * P:s * DIM + (kk + 1) * P],
                                     waug[:, kk * (ROW + HEADS):(kk + 1) * (ROW + HEADS)], start=(kk == 0), stop=(kk == 1))
                last.then_inc(p1_h, 1)

            pe.wait_ge(waug_set, 1)
            p1_pe(0, 0, False)
            p1_pe(1, 1, False)
            with pe.Fori(1, NW // 2) as it:
                for s in range(2):
                    p1_pe(it * 2 + s, s, True)
            p1_pe(NW - 1, 0, True)
            pe.wait_ge(sched_set, 1)
            n = 0
            for q in range(CHUNKS):
                for of in (rel_q, end_q, src_f):
                    if n >= 2:
                        pe.wait_ge(col_copied, n - 1)
                    for j in range(TILES):
                        last = pe.transpose(bank[4 + n % 2][:, j * P:(j + 1) * P], of[:, q * GE + j * P:q * GE + (j + 1) * P], ident[:, :])
                    last.then_inc(col_ps, 1)
                    n += 1

            def pe_iter(it, u, on):
                k = it * UNROLL + u
                if on(0):
                    pe.wait_ge(scanned, k + 1)
                    pe.nop(nofuse=True)
                    pe.transpose(bank[3][:, 0:16], scan_ring[:, u * P:(u + 1) * P], ident[0:16, 0:16]).then_inc(scan_ps, 1)
                if on(1):
                    v = (u + 1) % UNROLL
                    pe.wait_ge(onehot_set, k + 2)
                    if on(-1):
                        pe.wait_ge(oht_set, k)
                    for j in range(TILES):
                        last = pe.transpose(bank[v % 2][:, j * P:(j + 1) * P], onehot(v)[:, j * P:(j + 1) * P], ident[:, :])
                    last.then_inc(oht_ps, 1)
                if on(0):
                    pe.wait_ge(endcol_set, k + 1)
                    pe.wait_ge(seg_set, k + 1)
                    for j in range(TILES):
                        last = pe.matmul(bank[4][:, j * 5:j * 5 + 5], onehot(u)[:, j * P:(j + 1) * P],
                                         seg_ring[:, u * 20 + j * 5:u * 20 + j * 5 + 5], start=True, stop=True)
                    last.then_inc(px_ps, 1)
                if on(-1):
                    v = (u - 1) % UNROLL
                    pe.wait_ge(msg_set, k)
                    for j in range(TILES):
                        last = pe.matmul(bank[6 + v % 2][:, 0:ROW], onehot(v)[:, j * P:(j + 1) * P],
                                         rows(v)[:, j * ROW:(j + 1) * ROW], start=(j == 0), stop=(j == TILES - 1))
                    last.then_inc(agg_ps, 1)
                if on(0):
                    pe.wait_ge(oht_set, k + 1)
                    pe.wait_ge(newmax_set, k + 1)
                    for j in range(TILES):
                        last = pe.matmul(bank[5][:, j * 8:j * 8 + 8], onehot_t(u)[:, j * P:(j + 1) * P],
                                         node_ring[:, u * 12 + 4:u * 12 + 12], start=True, stop=True)
                    last.then_inc(ex_ps, 1)
                if on(1):
                    v = (u + 1) % UNROLL
                    pe.wait_ge(rows_in[v], (it + (u + 1) // UNROLL + 1) * (16 * TILES))
                    scores = rows(v).rearrange("p (r c) -> p r c", c=HC)[:, :, HEAD_DIM:HC].rearrange("p r o -> p (r o)")
                    pe.transpose(bank[2][0:16, 0:P], scores, ident[:, :]).then_inc(score_ps, 1)

            iterate(pe, pe_iter)

            pe.wait_ge(weights_in, 16 * N_WEIGHTS)
            nh, no = [0], [0]

            def front_pe(b):
                pe.wait_ge(p3_yn, b + 1)
                for g in range(4):
                    nt = 4 if g < 3 else 2
                    if g >= 2:
                        pe.wait_ge(p3_yt, 4 * b + g - 1)
                    elif b > 0:
                        pe.wait_ge(p3_rh, 2 * b)
                        if g == 0:
                            pe.wait_ge(p3_ex_in, b)
                    for i in range(nt):
                        tk = 4 * g + i
                        t, kk = tk // 2, tk % 2
                        last = pe.transpose(bank[6 + g % 2][:, i * P:(i + 1) * P],
                                            yn[:, t * DIM + kk * P:t * DIM + (kk + 1) * P], ident[:, :])
                    last.then_inc(p3_yt_ps, 1)
                pe.wait_ge(p3_yt, 4 * b + 4)
                for half in range(2):
                    for kk in range(2):
                        last = pe.matmul(bank[6 + half][:, 0:HALF], rw1[:, kk * ROUTER_H:(kk + 1) * ROUTER_H],
                                         ynt[b % 2][:, kk * BN + half * HALF:kk * BN + (half + 1) * HALF],
                                         start=(kk == 0), stop=(kk == 1))
                    last.then_inc(p3_rh_ps, 1)
                pe.wait_ge(p3_rh, 2 * b + 2)
                for t in range(BW):
                    last = pe.matmul(bank[6][:, t * EXPERTS:(t + 1) * EXPERTS], rht[:, t * P:(t + 1) * P], rw2[:, :],
                                     start=True, stop=True)
                last.then_inc(p3_lg_ps, 1)

            def hidden_pe(s, layer):
                b, e = s // EXPERTS, s % EXPERTS
                frm = ynt[b % 2] if layer == 0 else h1t[s % 2]
                w = (ew1, ew2)[layer]
                if layer == 1:
                    pe.wait_ge(h_set, hidden_done[("h1", s)])
                for m in range(2):
                    for half in range(2):
                        if nh[0] >= 4:
                            pe.wait_ge(h_set, nh[0] - 3)
                        for kk in range(2):
                            last = pe.matmul(bank[nh[0] % 4][:, 0:HALF], w[:, e * 512 + kk * 256 + m * P:e * 512 + kk * 256 + (m + 1) * P],
                                             frm[:, kk * BN + half * HALF:kk * BN + (half + 1) * HALF],
                                             start=(kk == 0), stop=(kk == 1))
                        last.then_inc(h_ps, 1)
                        nh[0] += 1

            def out_pe(s):
                e = s % EXPERTS
                pe.wait_ge(h_set, hidden_done[("h2", s)])
                for t in range(BW):
                    if no[0] >= 2:
                        pe.wait_ge(o_used, no[0] - 1)
                    for kk in range(2):
                        last = pe.matmul(bank[4 + no[0] % 2][:, 0:DIM], h2t[s % 2][:, kk * BN + t * P:kk * BN + (t + 1) * P],
                                         ew3[:, e * 512 + kk * 256:e * 512 + (kk + 1) * 256], start=(kk == 0), stop=(kk == 1))
                    last.then_inc(o_ps, 1)
                    no[0] += 1

            for kind, arg in phase3_order():
                if kind == "front":
                    front_pe(arg)
                elif kind == "out":
                    out_pe(arg)
                else:
                    hidden_pe(arg, 0 if kind == "h1" else 1)

        @block.vector
        def _(dve):
            links = [0]

            def link(ins):
                links[0] += 1
                ins.then_inc(dve_link, 1)
                dve.wait_ge(dve_link, links[0])

            dve.wait_ge(gat_in, 16 * 5)
            for kk in range(2):
                o = kk * (ROW + HEADS)
                feats = waug[:, o:o + ROW].rearrange("p (h c) -> p h c", c=HC)
                for which in range(2):
                    link(dve.tensor_tensor(att_prod[:, :].rearrange("p (h c) -> p h c", h=HEADS), feats[:, :, 0:HEAD_DIM],
                                           attb[:, which * DIM:(which + 1) * DIM].rearrange("p (h c) -> p h c", h=HEADS), ALU.mult))
                    to = feats[:, :, HEAD_DIM:HC] if which == 0 else waug[:, o + ROW:o + ROW + HEADS].unsqueeze(2)
                    link(dve.tensor_reduce(to, att_prod[:, :].rearrange("p (h c) -> p h c", h=HEADS), AX.X, ALU.add))
            dve.memset(small[:, 59:60], 0.0).then_inc(waug_set, 1)

            link(dve.memset(ints[:, 3:4], 0))
            link(dve.memset(ints[:, 7:8], P * 1000))
            dve.memset(small[:, 60:61], 0.0).then_inc(bounds_ready, 1)
            dve.wait_ge(consts, 8)
            dve.wait_ge(bounds_in, 16 * N_BOUNDS)
            link(dve.tensor_single_scalar(ints[:, 8:16], ints[:, 0:8], 7, ALU.arith_shift_right))
            link(dve.tensor_copy(prev_f, ints[:, 8:16]))
            link(dve.memset(width, 1.0))
            link(dve.scalar_tensor_tensor(width[:, :, 1:2].rearrange("p c o -> p (c o)"), prev_f[:, 4:8], 1.0, prev_f[:, 0:4], ALU.add, ALU.subtract))
            link(dve.memset(shifted, 0.0))
            for c in range(1, CHUNKS):
                link(dve.tensor_tensor(shifted[:, c:c + 1], shifted[:, c - 1:c], width[:, c - 1, 1:2], ALU.add))
            dve.memset(small[:, 61:62], 0.0).then_inc(before_set, 1)
            dve.wait_ge(cum_ps, 1)
            link(dve.tensor_copy(cum, bank[6][:, 0:CHUNKS]))
            for c in range(CHUNKS):
                link(dve.tensor_scalar(before[:, c * 512:(c + 1) * 512], iota_step, cum[:, c:c + 1], None, ALU.is_ge))
            dve.memset(small[:, 61:62], 0.0).then_inc(before_set, 1)
            dve.wait_ge(found_ps, 1)
            link(dve.tensor_copy(found, bank[7][:, 0:2 * CHUNKS]))
            counts = found.rearrange("p (q two) -> p q two", two=2)
            dve.tensor_copy(group_no, counts[:, :, 0:1].rearrange("p q o -> p (q o)")).then_inc(groups_set, 1)

            def p1_norm(t, xs, s):
                st = stats0[:, s * 12:(s + 1) * 12]
                dve.bn_stats(st[:, 0:6], xin[:, xs * DIM:(xs + 1) * DIM]).then_inc(p1_stats, 1)
                dve.wait_ge(p1_stats, t + 1)
                dve.nop(nofuse=True)
                dve.bn_aggr(st[:, 6:8], st[:, 0:6]).then_inc(p1_mv, 1)

            def p1_apply(t, xs, s):
                st = stats0[:, s * 12:(s + 1) * 12]
                dve.wait_ge(p1_std, t + 1)
                dve.reciprocal(st[:, 9:10], st[:, 8:9]).then_inc(p1_rstd, 1)
                dve.wait_ge(p1_rstd, t + 1)
                dve.tensor_scalar(xn0[:, s * DIM:(s + 1) * DIM], xin[:, xs * DIM:(xs + 1) * DIM], st[:, 6:7], st[:, 9:10],
                                  ALU.subtract, ALU.mult).then_inc(p1_xn, 1)

            def p1_take(t, s):
                dve.wait_ge(p1_h, t + 1)
                dve.tensor_copy(acc[:, bass.ds(t * ROW, ROW)], bank[2 + s][:, 0:ROW]).then_inc(p1_acc, 1)
                dve.tensor_copy(state[:, bass.ds(t * 8 + 4, 4)], bank[2 + s][:, ROW:ROW + HEADS]).then_inc(p1_ad, 1)

            dve.wait_ge(x_in[0], 16)
            p1_norm(0, 0, 0)
            p1_apply(0, 0, 0)
            for t in range(1, 4):
                dve.wait_ge(x_in[t], 16)
                p1_norm(t, t, t % 2)
                p1_take(t - 1, (t - 1) % 2)
                p1_apply(t, t, t % 2)
            with dve.Fori(1, NW // 4) as it:
                for q in range(4):
                    dve.wait_ge(x_in[q], (it + 1) * 16)
                    p1_norm(it * 4 + q, q, q % 2)
                    p1_take(it * 4 + (q - 1), (q - 1) % 2)
                    p1_apply(it * 4 + q, q, q % 2)
            for t in range(NW - 1, NW):
                dve.wait_ge(x_in[t % 4], (t // 4 + 1) * 16)
                p1_norm(t, t % 4, t % 2)
                p1_take(t - 1, (t - 1) % 2)
                p1_apply(t, t % 4, t % 2)
            p1_take(NW - 1, (NW - 1) % 2)
            acc_all = acc[:, :].rearrange("p (t h c) -> p t h c", h=HEADS, c=HC)
            st_all = state[:, :].rearrange("p (t c) -> p t c", c=8)
            dve.wait_ge(p1_ad, NW)
            link(dve.tensor_tensor(st_all[:, :, 0:4], acc_all[:, :, :, HEAD_DIM:HC].rearrange("p t h o -> p t (h o)"),
                                   st_all[:, :, 4:8], ALU.add))
            link(dve.scalar_tensor_tensor(st_all[:, :, 0:4], st_all[:, :, 0:4], SLOPE, st_all[:, :, 0:4], ALU.mult, ALU.max))
            dve.wait_ge(node_rows_out, 16 * NW)
            link(dve.memset(acc_all[:, :, :, HEAD_DIM:HC].rearrange("p t h o -> p (t h o)"), 1.0))

            dve.wait_ge(group_rows_in, 16 * 2 * CHUNKS)
            dst_q = dst_i.rearrange("p (q e) -> p q e", e=GE)
            link(dve.tensor_single_scalar(first_w, dst_q[:, :, 0:1].rearrange("p q o -> p (q o)"), 7, ALU.arith_shift_right))
            link(dve.tensor_copy(win_f, first_w))
            link(dve.tensor_tensor(win_f, win_f, step_no, ALU.add))
            link(dve.tensor_tensor(win_f, win_f, counts[:, :, 1:2].rearrange("p q o -> p (q o)"), ALU.subtract))
            link(dve.tensor_single_scalar(neg_w, win_f, -float(P), ALU.mult))
            link(dve.tensor_single_scalar(win_i, win_f, float(NW - 1), ALU.min))
            for q in range(CHUNKS):
                link(dve.tensor_scalar(rel_q[:, q * GE:(q + 1) * GE], dst_i[:, q * GE:(q + 1) * GE], neg_w[:, q:q + 1], None, ALU.add))
            rel3 = rel_q.rearrange("p (q e) -> p q e", e=GE)
            chg3 = change[:, 0:CHUNKS * GE].rearrange("p (q e) -> p q e", e=GE)
            link(dve.memset(chg3[:, :, 0:1], 0.0))
            link(dve.tensor_tensor(chg3[:, :, 1:GE], rel3[:, :, 1:GE], rel3[:, :, 0:GE - 1], ALU.not_equal))
            end3 = end_q.rearrange("p (r e) -> p r e", e=P)
            chr3 = change[:, 0:CHUNKS * GE].rearrange("p (r e) -> p r e", e=P)
            link(dve.tensor_copy(end3[:, :, 0:P - 1], chr3[:, :, 1:P]))
            link(dve.memset(end3[:, :, P - 1:P], 1.0))
            link(dve.tensor_single_scalar(change[:, 0:CHUNKS * GE], change[:, 0:CHUNKS * GE], -BIG, ALU.mult))
            link(dve.tensor_copy(src_f, src_i))
            dve.memset(small[:, 63:64], 0.0).then_inc(sched_set, 1)

            dve.wait_ge(windows_in, 16)
            dve.wait_ge(col_copied, 3 * CHUNKS)
            dve.wait_ge(flags_out, 16 * CHUNKS * HEADS)

            wreg = {}

            def window_of(it, u):
                return dve.value_load(windows[0:1, bass.ds(it * UNROLL + u, 1)], min_val=0, max_val=NW - 1)

            def dve_iter(it, u, on):
                k = it * UNROLL + u
                v = (u - 1) % UNROLL
                if on(0):
                    dve.wait_ge(flags_in[u], (it + 1) * 16)
                    dve.wait_ge(score_ps, k + 1)
                    dve.tensor_tensor_scan(scan_ring[:, u * P:(u + 1) * P], flag_ring[:, u * P:(u + 1) * P],
                                           bank[2][0:16, 0:P], -BIG, ALU.add, ALU.max).then_inc(scanned, 1)
                if on(-1):
                    dve.wait_ge(ex_ps, k)
                    scores = rows(v).rearrange("p (j h c) -> p j h c", h=HEADS, c=HC)[:, :, :, HEAD_DIM:HC].rearrange("p j h o -> p j (h o)")
                    ex = bank[5][:, 0:32].rearrange("p (j c) -> p j c", c=8)
                    z3 = zsum[:, :].rearrange("p (j h) -> p j h", h=HEADS)
                    dve.tensor_tensor(z3, scores, ex[:, :, 0:4], ALU.add).then_inc(zsum_set, 1)
                    dve.wait_ge(zsum_set, k)
                    dve.scalar_tensor_tensor(zlr[:, :], zsum[:, :], SLOPE, zsum[:, :], ALU.mult, ALU.max).then_inc(zlr_set, 1)
                    dve.wait_ge(zlr_set, k)
                    dve.tensor_tensor(zexp[:, v * 16:v * 16 + 16].rearrange("p (j h) -> p j h", h=HEADS),
                                      zlr[:, :].rearrange("p (j h) -> p j h", h=HEADS), ex[:, :, 4:8], ALU.subtract).then_inc(z_set, 1)
                if on(1):
                    n = (u + 1) % UNROLL
                    dve.tensor_tensor(onehot(n).rearrange("p (j d) -> p j d", d=P),
                                      iota_row[:, :].unsqueeze(1).to_broadcast([P, TILES, P]),
                                      rel_col[:, bass.ds(k + 1, 1), :].rearrange("p s j -> p j s").to_broadcast([P, TILES, P]),
                                      ALU.is_equal).then_inc(onehot_set, 1)
                if on(0):
                    dve.wait_ge(scan_ps, k + 1)
                    dve.tensor_tensor(seg_ring[:, u * 20:u * 20 + 20].rearrange("p (j c) -> p j c", c=5)[:, :, 0:4],
                                      bank[3][:, 0:16].rearrange("p (j h) -> p j h", h=HEADS),
                                      end_col[:, bass.ds(k, 1), :].rearrange("p s j -> p j s").to_broadcast([P, TILES, HEADS]),
                                      ALU.mult).then_inc(seg_set, 1)
                if on(-1):
                    dve.wait_ge(wexp_set, k)
                    parts = rows(v).rearrange("p (r c) -> p r c", c=HC)
                    dve.tensor_single_scalar(parts[:, :, HEAD_DIM:HC], wexp[:, v * 16:v * 16 + 16].unsqueeze(2), 1.0, ALU.min).then_inc(w_set, 1)
                    dve.wait_ge(w_set, k)
                    dve.tensor_tensor(parts[:, :, 0:HEAD_DIM], parts[:, :, 0:HEAD_DIM],
                                      parts[:, :, HEAD_DIM:HC].to_broadcast([P, 16, HEAD_DIM]), ALU.mult).then_inc(msg_set, 1)
                if on(0):
                    w = wreg[u] = window_of(it, u)
                    nr = node_ring[:, u * 12:u * 12 + 12]
                    if on(-1):
                        dve.wait_ge(max_stored, k)
                    dve.tensor_copy(nr[:, 0:8], state[:, bass.ds(w * 8, 8)]).then_inc(cur_set, 1)
                    dve.wait_ge(px_ps, k + 1)
                    px = bank[4][:, 0:20].rearrange("p (j c) -> p j c", c=5)
                    dve.tensor_scalar(absent[:, :].unsqueeze(2), px[:, :, 4:5], BIG, -BIG, ALU.mult, ALU.add).then_inc(absent_set, 1)
                    dve.wait_ge(absent_set, k + 1)
                    dve.tensor_tensor(cand[:, :].rearrange("p (h j) -> p j h", j=TILES), px[:, :, 0:4],
                                      absent[:, :].unsqueeze(2).to_broadcast([P, TILES, HEADS]), ALU.add).then_inc(cand_set, 1)
                    dve.wait_ge(cand_set, k + 1)
                    dve.tensor_reduce(top[:, :], cand[:, :].rearrange("p (h j) -> p h j", j=TILES), AX.X, ALU.max).then_inc(top_set, 1)
                    dve.wait_ge(top_set, k + 1)
                    dve.tensor_tensor(top_e[:, :], top[:, :], nr[:, 4:8], ALU.add).then_inc(tope_set, 1)
                    dve.wait_ge(tope_set, k + 1)
                    dve.scalar_tensor_tensor(top[:, :], top_e[:, :], SLOPE, top_e[:, :], ALU.mult, ALU.max).then_inc(lr_set, 1)
                    dve.wait_ge(lr_set, k + 1)
                    dve.tensor_tensor(nr[:, 8:12], top[:, :], nr[:, 0:4], ALU.max).then_inc(newmax_set, 1)
                    dve.wait_ge(newmax_set, k + 1)
                    dve.tensor_tensor(fall[:, u * HEADS:(u + 1) * HEADS], nr[:, 0:4], nr[:, 8:12], ALU.subtract).then_inc(fall_set, 1)
                    dve.tensor_copy(state[:, bass.ds(w * 8, 4)], nr[:, 8:12]).then_inc(max_stored, 1)
                if on(-2):
                    u2 = (u - 2) % UNROLL
                    w2 = window_of(it + (u - 2) // UNROLL, u2) if u < 2 else wreg[u2]
                    here = acc[:, bass.ds(w2 * ROW, ROW)]
                    dve.wait_ge(keep_set, k - 1)
                    if on(-3):
                        dve.wait_ge(added, k - 2)
                    dve.tensor_tensor(here.rearrange("p (h c) -> p h c", c=HC), here.rearrange("p (h c) -> p h c", c=HC),
                                      keep[:, u2 * HEADS:(u2 + 1) * HEADS].unsqueeze(2).to_broadcast([P, HEADS, HC]),
                                      ALU.mult).then_inc(scaled, 1)
                    dve.wait_ge(scaled, k - 1)
                    dve.wait_ge(agg_ps, k - 1)
                    dve.tensor_tensor(here, here, bank[6 + u2 % 2][:, 0:ROW], ALU.add).then_inc(added, 1)

            iterate(dve, dve_iter)

            dve.wait_ge(weights_in, 16 * N_WEIGHTS)
            dve.wait_ge(added, STEPS)
            plinks = [0]

            def plink(ins):
                plinks[0] += 1
                ins.then_inc(p3_link, 1)
                dve.wait_ge(p3_link, plinks[0])

            acc_all = acc[:, :].rearrange("p (t h c) -> p t h c", h=HEADS, c=HC)

            def front_dve(b):
                yb = y[b % 2]
                if b >= 2:
                    dve.wait_ge(out_sem, 16 * (b - 1))
                ab = acc[:, b * BW * ROW:(b + 1) * BW * ROW].rearrange("p (r c) -> p r c", c=HC)
                plink(dve.tensor_scalar_add(rsum28[:, :].unsqueeze(2), ab[:, :, HEAD_DIM:HC], SUM_EPS))
                plink(dve.reciprocal(rsum28[:, :], rsum28[:, :]))
                plink(dve.tensor_tensor(yb[:, :].rearrange("p (r c) -> p r c", c=HEAD_DIM), ab[:, :, 0:HEAD_DIM],
                                        rsum28[:, :].unsqueeze(2).to_broadcast([P, BW * HEADS, HEAD_DIM]), ALU.mult))
                plink(dve.tensor_tensor(yb[:, :].rearrange("p (t d) -> p t d", d=DIM), yb[:, :].rearrange("p (t d) -> p t d", d=DIM),
                                        gbias[:, :].unsqueeze(1).to_broadcast([P, BW, DIM]), ALU.add))
                dve.wait_ge(xblk_in[b % 2], 16 * (b // 2 + 1) + (16 if b == NB - 1 else 0))
                full = BW if b < NB - 1 else BW - 1
                plink(dve.tensor_tensor(yb[:, 0:full * DIM], yb[:, 0:full * DIM], xblk[b % 2][:, 0:full * DIM], ALU.add))
                if full < BW:
                    plink(dve.tensor_tensor(yb[0:LAST_ROWS, full * DIM:], yb[0:LAST_ROWS, full * DIM:],
                                            xblk[b % 2][0:LAST_ROWS, full * DIM:BW * DIM], ALU.add))
                for t in range(BW):
                    plink(dve.bn_stats(stats3[:, t * 6:(t + 1) * 6], yb[:, t * DIM:(t + 1) * DIM]))
                    ins = dve.bn_aggr(mv3[:, 2 * t:2 * t + 2], stats3[:, t * 6:(t + 1) * 6])
                    if t < BW - 1:
                        plink(ins)
                ins.then_inc(p3_var, 1)
                dve.wait_ge(p3_std, b + 1)
                plink(dve.reciprocal(rsum[:, BW:2 * BW], rsum[:, 0:BW]))
                for t in range(BW):
                    ins = dve.tensor_scalar(yn[:, t * DIM:(t + 1) * DIM], yb[:, t * DIM:(t + 1) * DIM], mv3[:, 2 * t:2 * t + 1],
                                            rsum[:, BW + t:BW + t + 1], ALU.subtract, ALU.mult)
                ins.then_inc(p3_yn, 1)
                T = [rt[:, i * 42:(i + 1) * 42] for i in range(12)]
                C = [T[i].rearrange("p (t e) -> p t e", e=EXPERTS) for i in range(12)]

                def one(i):
                    return rt[:, 10 * 42 + i * 7:10 * 42 + (i + 1) * 7].unsqueeze(2)

                def wide(i):
                    return one(i).to_broadcast([P, BW, EXPERTS])

                REV = rev[:, :].rearrange("p (t e) -> p t e", e=EXPERTS)
                dve.wait_ge(p3_lg_ps, b + 1)
                plink(dve.tensor_tensor(C[2], bank[6][:, 0:42].rearrange("p (t e) -> p t e", e=EXPERTS),
                                        rb2[:, :].unsqueeze(1).to_broadcast([P, BW, EXPERTS]), ALU.add))
                plink(dve.tensor_reduce(one(0), C[2], AX.X, ALU.max))
                dve.tensor_tensor(C[0], C[2], wide(0), ALU.subtract).then_inc(p3_ex_in, 1)
                dve.wait_ge(p3_ex_out, b + 1)
                plink(dve.tensor_reduce(one(1), C[1], AX.X, ALU.add))
                plink(dve.reciprocal(one(2), one(1)))
                plink(dve.tensor_tensor(C[3], C[1], wide(2), ALU.mult))
                for r in range(2):
                    prob, hot = C[3 + r], C[5 + r]
                    plink(dve.tensor_reduce(one(3 + r), prob, AX.X, ALU.max))
                    plink(dve.tensor_tensor(C[8], prob, wide(3 + r), ALU.is_equal))
                    plink(dve.tensor_tensor(C[8], C[8], REV, ALU.mult))
                    plink(dve.tensor_reduce(one(5), C[8], AX.X, ALU.max))
                    plink(dve.tensor_tensor(hot, REV, wide(5), ALU.is_equal))
                    if r == 0:
                        plink(dve.scalar_tensor_tensor(T[4], T[5], -2.0, T[3], ALU.mult, ALU.add))
                e2 = rt[:, 7 * 42 + 7:7 * 42 + 14]
                dve.tensor_tensor(rt[:, 7 * 42:7 * 42 + 7].unsqueeze(2), one(4), one(3), ALU.subtract).then_inc(p3_e2_in, 1)
                dve.wait_ge(p3_e2_out, b + 1)
                plink(dve.tensor_scalar_add(one(6), e2.unsqueeze(2), 1.0))
                plink(dve.reciprocal(one(7), one(6)))
                plink(dve.tensor_tensor(one(8), one(7), e2.unsqueeze(2), ALU.mult))
                plink(dve.tensor_tensor(C[5], C[5], wide(7), ALU.mult))
                plink(dve.tensor_tensor(C[6], C[6], wide(8), ALU.mult))
                plink(dve.tensor_tensor(gate[b % 2][:, :].rearrange("p (t e) -> p t e", e=EXPERTS), C[5], C[6], ALU.add))
                for e in range(EXPERTS):
                    for t in range(BW):
                        ins = dve.scalar_tensor_tensor(yb[:, t * DIM:(t + 1) * DIM], eb3[:, e * DIM:(e + 1) * DIM],
                                                       gate[b % 2][:, t * EXPERTS + e:t * EXPERTS + e + 1],
                                                       yb[:, t * DIM:(t + 1) * DIM], ALU.mult, ALU.add)
                        if t < BW - 1:
                            ins.then_inc(p3_link, 1)
                            plinks[0] += 1
                        else:
                            plink(ins)

            no = [0]

            def out_dve(s):
                b, e = s // EXPERTS, s % EXPERTS
                yb = y[b % 2]
                for t in range(BW):
                    dve.wait_ge(o_ps, no[0] + 1)
                    if no[0] >= BW:
                        dve.wait_ge(o_used, no[0] - BW + 1)
                    ins = dve.scalar_tensor_tensor(yb[:, t * DIM:(t + 1) * DIM], bank[4 + no[0] % 2][:, 0:DIM],
                                                   gate[b % 2][:, t * EXPERTS + e:t * EXPERTS + e + 1],
                                                   yb[:, t * DIM:(t + 1) * DIM], ALU.mult, ALU.add)
                    ins.then_inc(o_used, 1)
                    no[0] += 1
                if e == EXPERTS - 1:
                    dve.wait_ge(o_used, no[0])
                    dve.memset(small[:, 64:65], 0.0).then_inc(block_done, 1)

            for kind, arg in phase3_order():
                if kind == "front":
                    front_dve(arg)
                elif kind == "out":
                    out_dve(arg)


_INS = ["x", "src", "dst", "L0_gnn_W", "L0_gnn_att_src", "L0_gnn_att_dst", "L0_gnn_bias", "L0_ffn_router_w1",
        "L0_ffn_router_b1", "L0_ffn_router_w2", "L0_ffn_router_b2", "L0_ffn_expert_w1", "L0_ffn_expert_b1",
        "L0_ffn_expert_w2", "L0_ffn_expert_b2", "L0_ffn_expert_w3", "L0_ffn_expert_b3"]


def kernel(**inputs):
    import numpy as _np
    import concourse.bacc as _bacc
    from concourse import mybir as _mybir
    from concourse.bass_utils import run_bass_kernel_spmd as _run

    nc = _bacc.Bacc("TRN2", target_bir_lowering=False, num_devices=1)
    arrays, args = {}, []
    for name in _INS:
        a = _np.ascontiguousarray(inputs[name])
        arrays[f"in_{name}"] = a
        args.append(nc.dram_tensor(f"in_{name}", a.shape, _mybir.dt.from_np(a.dtype), kind="ExternalInput").ap())
    args.append(nc.dram_tensor("out_dram", (N_NODES, DIM), _mybir.dt.float32, kind="ExternalOutput").ap())
    gnn_moe_program(nc, *args)
    r = _run(nc, [arrays], core_ids=[0])
    return r.results[0]["out_dram"]
```

```python
from contextlib import ExitStack

import concourse.bass as bass
from concourse import mybir

N_NODES, DIM, N_EDGES = 6250, 256, 200000
HEADS, HEAD_DIM = 4, 64
EXPERTS, ROUTER_H = 6, 128
SLOPE, LN_EPS, SUM_EPS = 0.2, 1e-5, 1e-16
P = 128

NW = -(-N_NODES // P)
LAST_ROWS = N_NODES - (NW - 1) * P
TILES = 4
GE = TILES * P
NG = -(-N_EDGES // GE)
UNROLL = 6
FILL = 2
STEPS = -(-(NG + NW - 1) // UNROLL) * UNROLL
CHUNKS = 4
assert STEPS <= CHUNKS * P and NG <= CHUNKS * P
SORT_P = 125
SORT_T = N_EDGES // SORT_P
assert SORT_P * SORT_T == N_EDGES
HC = HEAD_DIM + 1
ROW = HEADS * HC
BIG = 1.0e30
CAP = 1.0e18
PAD_DST = 1 << 20
BW = 7
NB = NW // BW
BN = BW * P
HALF = BN // 2




def block_parts(has_next):
    order = []
    for e in range(EXPERTS):
        if has_next and e >= 2:
            order.append((("sum", "norm", "turn", "route")[e - 2], None))
        if has_next or e + 1 < EXPERTS:
            order.append(("h1", e + 1))
        order.append(("h2", e))
        if e:
            order.append(("out", e - 1))
    return order + [("out", EXPERTS - 1)]


def order_edges(nc, block, ctx, src, dst, src_pad, dst_pad, arena, pads, pads_set, edges_copied, bank, load_first_x):
    f32, i32 = mybir.dt.float32, mybir.dt.int32
    ALU, AX = mybir.AluOpType, mybir.AxisListType
    E = SORT_P
    flat_s = src_pad.rearrange("g e -> (g e)")
    flat_d = dst_pad.rearrange("g e -> (g e)")

    def sem(name):
        return ctx.enter_context(nc.semaphore(name))

    limit_set, dst_in, src_in, odd_count, odd_sum, order_known = (
        sem(n) for n in ("limit_set", "dst_in", "src_in", "odd_count", "odd_sum", "order_known"))
    sort_ones, sort_consts, sort_step, sort_onehot, sort_prod, sort_turned, sort_looked, sort_pos, sort_free, sort_stored, sort_base = (
        sem(f"sort_{n}") for n in ("ones", "consts", "step", "onehot", "prod", "turned", "looked", "pos", "free", "stored", "base"))

    used = [0]

    def part(cols, parts=E):
        at = used[0]
        used[0] += cols
        return arena[0:parts, at:at + cols]

    dst_next = part(SORT_T + 1).bitcast(i32)
    edge_i = part(2 * SORT_T).bitcast(i32).rearrange("p (t c) -> p t c", c=2)
    edge_f = part(2 * SORT_T).rearrange("p (t c) -> p t c", c=2)
    temp = part(SORT_T)
    temp_i = temp.bitcast(i32)
    src_raw = edge_f.rearrange("p t c -> p (t c)")[:, 0:SORT_T].bitcast(i32)
    ones, odd = part(P, P), part(1)
    flag = part(1, 1).bitcast(i32)
    ident, later, iota = part(P, P), part(P, P), part(P)
    lo_hot, hi_hot, lo_hot_t, diag, same, hit = part(P), part(NW), part(P, P), part(P), part(P), part(NW)
    count, below, base = part(NW, P), part(NW, P), part(NW, P)
    now_f, now_i, now_d = part(2), part(2).bitcast(i32), part(1)
    rank, first, pos_i = part(1), part(1), part(1).bitcast(i32)

    def sorting_needed(eng):
        eng.wait_ge(order_known, 1)
        return eng.value_load(flag[0:1, 0:1], min_val=0, max_val=N_EDGES)

    @block.sync
    def _(sp):
        sp.wait_ge(limit_set, 1)
        by_part = dst.rearrange("(p t) -> p t", p=E)
        sp.dma_start(dst_next[:, 0:SORT_T], by_part).then_inc(dst_in, 16)
        with nc.allow_non_contiguous_dma(reason="one word per partition"):
            sp.dma_start(dst_next[0:E - 1, SORT_T:SORT_T + 1], by_part[1:E, 0:1]).then_inc(dst_in, 16)
        sp.wait_ge(pads_set, 2)
        sp.dma_start(flat_d[GE:GE + N_EDGES], dst).then_inc(edges_copied, 16)
        sp.dma_start(flat_s[GE:GE + N_EDGES], src).then_inc(edges_copied, 16)
        tail = (NG + 1) * GE - GE - N_EDGES
        sp.dma_start(flat_d[0:GE].unsqueeze(0), pads[0:1, 0:GE]).then_inc(edges_copied, 16)
        sp.dma_start(flat_d[GE + N_EDGES:(NG + 1) * GE].unsqueeze(0), pads[0:1, GE:GE + tail]).then_inc(edges_copied, 16)
        sp.dma_start(flat_s[0:GE].unsqueeze(0), pads[0:1, 0:GE]).then_inc(edges_copied, 16)
        sp.dma_start(flat_s[GE + N_EDGES:(NG + 1) * GE].unsqueeze(0), pads[0:1, 0:tail]).then_inc(edges_copied, 16)
        load_first_x(sp)
        sp.wait_ge(edges_copied, 96)
        with sp.If(sorting_needed(sp) > 0):
            sp.dma_start(src_raw, src.rearrange("(p t) -> p t", p=E)).then_inc(src_in, 16)

    @block.gpsimd
    def _(pool):
        pool.memset(pads[0:1, 0:GE], 0).then_inc(pads_set, 1)
        pool.memset(pads[0:1, GE:2 * GE], PAD_DST).then_inc(pads_set, 1)
        with pool.If(sorting_needed(pool) > 0):
            pool.memset(ident, 0.0).then_inc(sort_step, 1)
            pool.memset(later, 1.0).then_inc(sort_step, 1)
            pool.wait_ge(sort_step, 2)
            pool.affine_select(out=ident, in_=ident, compare_op=ALU.not_equal, fill=1.0,
                               base=0, pattern=[[-1, P]], channel_multiplier=1).then_inc(sort_consts, 1)
            pool.affine_select(out=later, in_=later, compare_op=ALU.is_ge, fill=0.0,
                               base=-1, pattern=[[1, P]], channel_multiplier=-1).then_inc(sort_consts, 1)
            pool.iota(iota, [[1, P]], base=0, channel_multiplier=0,
                      allow_small_or_imprecise_dtypes=True).then_inc(sort_consts, 1)
            pool.wait_ge(edges_copied, 96)
            pool.memset(pads[0:1, 0:1], 0).then_inc(sort_free, 1)
            with pool.Fori(0, SORT_T) as t:
                pool.wait_ge(sort_pos, t + 1)
                pool.nop(nofuse=True)
                for flat, c in ((flat_d, 0), (flat_s, 1)):
                    pool.indirect_dma_start(flat.unsqueeze(1), bass.IndirectOffsetOnAxis(ap=pos_i[:, 0:1], axis=0),
                                            now_i[:, c:c + 1], None).then_inc(sort_stored, 16)
                pool.wait_ge(sort_stored, t * 32 + 32)
                pool.nop(nofuse=True)
                pool.memset(pads[0:1, 0:1], 0).then_inc(sort_free, 1)

    @block.tensor
    def _(pe):
        pe.wait_ge(sort_ones, 1)
        pe.wait_ge(odd_count, 2)
        pe.matmul(bank[0][0:1, 0:1], odd, ones[0:E, 0:1], start=True, stop=True).then_inc(odd_sum, 1)
        with pe.If(sorting_needed(pe) > 0):
            pe.wait_ge(sort_consts, 3)
            with pe.Fori(0, SORT_T) as t:
                pe.wait_ge(sort_onehot, t + 1)
                pe.matmul(bank[2][:, 0:NW], lo_hot, hi_hot, start=True, stop=True).then_inc(sort_prod, 1)
            pe.wait_ge(sort_base, 1)
            pe.matmul(bank[4][:, 0:NW], ones, below, start=True, stop=False)
            pe.matmul(bank[4][:, 0:NW], later, count, start=False, stop=True).then_inc(sort_base, 1)
            with pe.Fori(0, SORT_T) as t:
                pe.wait_ge(sort_onehot, t + (SORT_T + 1))
                pe.transpose(bank[0][:, 0:E], lo_hot, ident[0:E, 0:E])
                pe.matmul(bank[1][0:E, 0:E], ones[0:E, 0:E], diag[:, 0:E], start=True, stop=True)
                pe.matmul(bank[2][:, 0:NW], lo_hot, hi_hot, start=True, stop=True).then_inc(sort_prod, 1)
                pe.wait_ge(sort_turned, t + 1)
                pe.matmul(bank[3][0:E, 0:NW], lo_hot_t[:, 0:E], base, start=True, stop=True).then_inc(sort_looked, 1)

    @block.vector
    def _(dve):
        dve.memset(dst_next[:, SORT_T:SORT_T + 1], PAD_DST).then_inc(limit_set, 1)
        dve.memset(ones, 1.0).then_inc(sort_ones, 1)
        dve.wait_ge(dst_in, 32)
        dve.tensor_tensor(temp, dst_next[:, 0:SORT_T], dst_next[:, 1:SORT_T + 1], ALU.is_gt).then_inc(odd_count, 1)
        dve.wait_ge(odd_count, 1)
        dve.tensor_reduce(odd, temp, AX.X, ALU.add).then_inc(odd_count, 1)
        dve.wait_ge(odd_sum, 1)
        dve.tensor_copy(flag[0:1, 0:1], bank[0][0:1, 0:1]).then_inc(order_known, 1)
        with dve.If(sorting_needed(dve) > 0):
            links = [2]

            def link(ins):
                links[0] += 1
                ins.then_inc(sort_step, 1)
                dve.wait_ge(sort_step, links[0])

            dve.wait_ge(sort_consts, 3)
            dve.wait_ge(src_in, 16)
            link(dve.tensor_copy(edge_i[:, :, 1:2], src_raw.unsqueeze(2)))
            link(dve.tensor_copy(edge_i[:, :, 0:1], dst_next[:, 0:SORT_T].unsqueeze(2)))
            link(dve.tensor_single_scalar(temp_i, dst_next[:, 0:SORT_T], 7, ALU.arith_shift_right))
            link(dve.tensor_copy(edge_f[:, :, 1:2], temp_i.unsqueeze(2)))
            link(dve.tensor_single_scalar(temp_i, dst_next[:, 0:SORT_T], P - 1, ALU.bitwise_and))
            link(dve.tensor_copy(edge_f[:, :, 0:1], temp_i.unsqueeze(2)))
            link(dve.memset(count, 0.0))

            def turn(t, at, links_per_turn):
                n = [0]

                def go(ins):
                    n[0] += 1
                    assert n[0] <= links_per_turn
                    ins.then_inc(sort_step, 1)
                    dve.wait_ge(sort_step, t * links_per_turn + (at + n[0]))
                return go

            def one_hots(t, go):
                go(dve.tensor_copy(now_f.unsqueeze(1), edge_f[:, bass.ds(t, 1), :]))
                go(dve.tensor_scalar(lo_hot, iota, now_f[:, 0:1], None, ALU.is_equal))
                go(dve.tensor_scalar(hi_hot, iota[:, 0:NW], now_f[:, 1:2], None, ALU.is_equal))

            start, COUNT_LINKS = links[0], 4
            with dve.Fori(0, SORT_T) as t:
                go = turn(t, start, COUNT_LINKS)
                one_hots(t, go)
                dve.memset(odd, 0.0).then_inc(sort_onehot, 1)
                dve.wait_ge(sort_prod, t + 1)
                go(dve.tensor_tensor(count, count, bank[2][:, 0:NW], ALU.add))
            links[0] += SORT_T * COUNT_LINKS
            link(dve.memset(below, 0.0))
            for j in range(1, NW):
                link(dve.tensor_tensor(below[:, j:j + 1], below[:, j - 1:j], count[:, j - 1:j], ALU.add))
            dve.memset(odd, 0.0).then_inc(sort_base, 1)
            dve.wait_ge(sort_base, 2)
            link(dve.tensor_copy(base, bank[4][:, 0:NW]))

            start, PLACE_LINKS = links[0], 14
            with dve.Fori(0, SORT_T) as t:
                go = turn(t, start, PLACE_LINKS)
                dve.wait_ge(sort_free, t + 1)
                go(dve.tensor_copy(now_i.unsqueeze(1), edge_i[:, bass.ds(t, 1), :]))
                go(dve.tensor_copy(now_d, now_i[:, 0:1]))
                one_hots(t, go)
                go(dve.tensor_scalar(diag, ident[0:E, :], now_d[:, 0:1], None, ALU.mult))
                dve.memset(odd, 0.0).then_inc(sort_onehot, 1)
                dve.wait_ge(sort_prod, t + (SORT_T + 1))
                go(dve.tensor_copy(lo_hot_t[:, 0:E], bank[0][:, 0:E]))
                dve.memset(odd, 0.0).then_inc(sort_turned, 1)
                go(dve.scalar_tensor_tensor(same[:, 0:E], bank[1][0:E, 0:E], now_d[:, 0:1], later[0:E, 0:E], ALU.is_equal, ALU.mult))
                go(dve.tensor_reduce(rank, same[:, 0:E], AX.X, ALU.add))
                dve.wait_ge(sort_looked, t + 1)
                go(dve.tensor_tensor(hit, bank[3][0:E, 0:NW], hi_hot, ALU.mult))
                go(dve.tensor_reduce(first, hit, AX.X, ALU.add))
                go(dve.tensor_tensor(first, first, rank, ALU.add))
                go(dve.tensor_single_scalar(pos_i, first, float(GE), ALU.add))
                dve.memset(odd, 0.0).then_inc(sort_pos, 1)
                go(dve.tensor_tensor(base, base, bank[2][:, 0:NW], ALU.add))


def gnn_moe_program(nc, x, src, dst, gat_w, att_src, att_dst, gat_bias, r_w1, r_b1, r_w2, r_b2,
                    e_w1, e_b1, e_w2, e_b2, e_w3, e_b3, out):
    f32, i32, bf16 = mybir.dt.float32, mybir.dt.int32, mybir.dt.bfloat16
    ALU, ACT, AX = mybir.AluOpType, mybir.ActivationFunctionType, mybir.AxisListType

    src_pad = nc.dram_tensor("src_pad", [NG + 1, GE], i32, kind="Internal").ap()
    dst_pad = nc.dram_tensor("dst_pad", [NG + 1, GE], i32, kind="Internal").ap()
    node_rows = nc.dram_tensor("node_rows", [NW * P, ROW], f32, kind="Internal").ap()
    flag_rows = nc.dram_tensor("flag_rows", [CHUNKS * P, TILES, HEADS, P], f32, kind="Internal").ap()
    window_list = nc.dram_tensor("window_list", [CHUNKS * P], i32, kind="Internal").ap()

    with ExitStack() as ctx:
        def sb(name, cols, dt=f32, parts=P):
            return ctx.enter_context(nc.sbuf_tensor(name, [parts, cols], dt))

        def sem(name):
            return ctx.enter_context(nc.semaphore(name))

        def sems(name, n):
            return [sem(f"{name}{i}") for i in range(n)]

        acc = sb("acc", NW * ROW)
        state = sb("state", NW * 8)
        parts3 = sb("parts3", NW * 24, bf16)
        ident = sb("ident", P)
        ident_b = sb("ident_b", P, bf16)
        iota_b = sb("iota_b", P, bf16)
        waug = sb("waug", 2 * (ROW + HEADS))
        ew1, ew2, ew3 = (sb(f"ew{i}", EXPERTS * 2 * 256) for i in (1, 2, 3))
        eb1, eb2 = (sb(f"eb{i}", EXPERTS * 2) for i in (1, 2))
        eb3 = sb("eb3", EXPERTS * DIM)
        rw1, rb1, rw2, rb2 = sb("rw1", 2 * ROUTER_H), sb("rb1", 1), sb("rw2", EXPERTS), sb("rb2", EXPERTS)
        gbias = sb("gbias", DIM)
        eps = sb("eps", 1)

        arena = sb("arena", UNROLL * (TILES * ROW + 2 * TILES * P))
        rows_at, oh_at = 0, UNROLL * TILES * ROW
        ohb_at = oh_at + UNROLL * TILES * P
        oht_at = ohb_at + UNROLL * TILES * P // 2
        column_data = sb("column_data", 3 * CHUNKS * P * TILES)
        columns = column_data[:, :].rearrange("p (s c) -> p s c", c=3 * TILES)
        flag_ring = sb("flag_ring", UNROLL * P, parts=16)
        scan_ring = sb("scan_ring", UNROLL * P, parts=16)
        idx_ring = sb("idx_ring", UNROLL * TILES, i32)
        col_ring = sb("col_ring", UNROLL * 2 * TILES)
        seg_ring = sb("seg_ring", UNROLL * 16, bf16)
        part_ring = sb("part_ring", UNROLL * 24, bf16)
        top = sb("top", HEADS)
        top_e = sb("top_e", HEADS)
        top_l = sb("top_l", HEADS)
        fall = sb("fall", UNROLL * HEADS)
        keep = sb("keep", UNROLL * HEADS)
        zsum = sb("zsum", 16)
        zlr = sb("zlr", 16)
        zexp = sb("zexp", UNROLL * 16)
        wexp = sb("wexp", UNROLL * 16)
        windows = sb("windows", CHUNKS * P, i32, parts=1)

        def rows(u):
            return arena[:, rows_at + u * TILES * ROW:rows_at + (u + 1) * TILES * ROW]

        def onehot32(u):
            return arena[:, oh_at + u * TILES * P:oh_at + (u + 1) * TILES * P]

        def onehot(u):
            return arena[:, ohb_at + u * TILES * P // 2:ohb_at + (u + 1) * TILES * P // 2].bitcast(bf16)

        def onehot_t(u):
            return arena[:, oht_at + u * TILES * P // 2:oht_at + (u + 1) * TILES * P // 2].bitcast(bf16)

        dst_i = arena[:, 0:2048].bitcast(i32)
        src_i = arena[:, 2048:4096].bitcast(i32)
        rel_q = arena[:, 4096:6144]
        change = arena[:, 6144:8192 + 4]
        end_q = arena[:, 8200:10248]
        src_f = arena[:, 10248:12296]
        before = column_data[:, 0:2048]
        iota_step = column_data[:, 2048:2560]
        tri = column_data[:, 2560:2688]
        ones = column_data[:, 2688:2816]
        small = sb("small", 96)
        step_no = small[:, 0:4]
        width = small[:, 4:12].rearrange("p (c two) -> p c two", two=2)
        shifted = small[:, 12:16]
        cum = small[:, 16:20]
        found = small[:, 20:28]
        win_f = small[:, 28:32]
        neg_w = small[:, 32:36]
        prev_f = small[:, 36:44]
        ints = sb("ints", 40, i32)
        prev_first, prev_last = ints[:, 0:4], ints[:, 4:8]
        prev_first_w, prev_last_w = ints[:, 8:12], ints[:, 12:16]
        group_no, win_i, first_w = ints[:, 16:20], ints[:, 20:24], ints[:, 24:28]
        pads = sb("pads", 2 * GE, i32, parts=1)

        xn0 = [arena[:, 4096 + i * BW * DIM:4096 + (i + 1) * BW * DIM] for i in (0, 1)]
        xnt0 = arena[:, 7680:8192]
        attb, att_prod = arena[:, 8192:8704], arena[:, 8704:8960]
        least = sb("least", 24)
        ad_rest = sb("ad_rest", 2 * NW * HEADS)
        ynt = [arena[:, i * 2 * BN:(i + 1) * 2 * BN] for i in (0, 1)]
        h1t = [arena[:, (2 + i) * 2 * BN:(3 + i) * 2 * BN] for i in (0, 1)]
        h2t = [arena[:, (4 + i) * 2 * BN:(5 + i) * 2 * BN] for i in (0, 1)]
        xblk = [column_data[:, i * BW * DIM:(i + 1) * BW * DIM] for i in (0, 1)]
        y = [sb(f"y{i}", BW * DIM) for i in (0, 1)]
        yn = column_data[:, 2 * BW * DIM:3 * BW * DIM]
        rht = arena[:, 12 * BN:13 * BN]
        stats3 = sb("stats3", BW * 6)
        mv3 = [sb(f"mv3_{i}", BW * 2) for i in (0, 1)]
        std = [sb(f"std{i}", BW) for i in (0, 1)]
        rstd = [sb(f"rstd{i}", BW) for i in (0, 1)]
        rsum28 = sb("rsum28", BW * HEADS)
        gate = [sb(f"gate{i}", BW * EXPERTS) for i in (0, 1)]
        rt = sb("rt", 12 * BW * EXPERTS)
        rev = sb("rev", BW * EXPERTS)

        bank = [ctx.enter_context(nc.psum_tensor(f"bank{i}", [P, 512], f32)) for i in range(8)]

        gat_in, bounds_ready = sem("gat_in"), sem("bounds_ready")
        weights_in, xblk_in = sem("weights_in"), sems("xblk_in", 2)
        consts = sem("consts")
        const_step = sem("const_step")
        dve_link, act_prep = sem("dve_link"), sem("act_prep")
        pads_set = sem("pads_set")
        edges_copied, bounds_in = sem("edges_copied"), sem("bounds_in")
        cum_ps, before_set, found_ps, groups_set = sem("cum_ps"), sem("before_set"), sem("found_ps"), sem("groups_set")
        group_rows_in = sem("group_rows_in")
        sched_set, flags_out, windows_out, windows_in = sem("sched_set"), sem("flags_out"), sem("windows_out"), sem("windows_in")
        col_ps, col_copied = sem("col_ps"), sem("col_copied")
        x_in = sems("x_in", 2)
        p1_stats, p1_var, p1_std, p1_rstd, p1_xn = (sem(f"p1_{n}") for n in ("stats", "var", "std", "rstd", "xn"))
        p1_xt_ps, p1_xt, p1_h, p1_acc, p1_ad = (sem(f"p1_{n}") for n in ("xt_ps", "xt", "h", "acc", "ad"))
        least_turn, least_ps, least_row, least_all = sem("least_turn"), sem("least_ps"), sem("least_row"), sem("least_all")
        shifted_set, self_fall, self_weight = sem("shifted_set"), sem("self_fall"), sem("self_weight")
        node_rows_out, waug_set, init_set = sem("node_rows_out"), sem("waug_set"), sem("init_set")

        idx_ready = sem("idx_ready")
        rows_in = sems("rows_in", UNROLL)
        flags_in = sems("flags_in", UNROLL)
        (cols_set, onehot_set, onehot32_set, oht_ps, oht_set, score_ps, scanned, scan_ps, seg_set, px_ps, parts_set,
         top_set, tope_set, lr_set, newmax_set, fall_set, keep_set, max_stored, ex_ps, zsum_set, zlr_set,
         z_set, wexp_set, w_set, msg_set, agg_ps, scaled, added) = (
            sem(n) for n in ("cols_set onehot_set onehot32_set oht_ps oht_set score_ps scanned scan_ps seg_set px_ps "
                             "parts_set top_set tope_set lr_set newmax_set fall_set keep_set max_stored "
                             "ex_ps zsum_set zlr_set z_set wexp_set w_set msg_set agg_ps scaled added").split())
        p3_y, p3_stats, p3_var, p3_std, p3_rstd, p3_yn, p3_yt_ps, p3_yt, p3_rh_ps, p3_rh, p3_lg_ps = (
            sem(f"p3_{n}") for n in ("y", "stats", "var", "std", "rstd", "yn", "yt_ps", "yt", "rh_ps", "rh", "lg_ps"))
        p3_ex_in, p3_ex_out, p3_e2_in, p3_e2_out, p3_route = (
            sem(f"p3_{n}") for n in ("ex_in", "ex_out", "e2_in", "e2_out", "route"))
        h1_ps, h1_set, h2_ps, h2_set = sem("h1_ps"), sem("h1_set"), sem("h2_ps"), sem("h2_set")
        o_ps, o_used, b3_used = sem("o_ps"), sem("o_used"), sem("b3_used")
        block_done, out_sem = sem("block_done"), sem("out_sem")

        N_BOUNDS = 8
        N_WEIGHTS = 4 + 3 * EXPERTS + 3 + 1

        def load_x(sp, b, to, done):
            last = P if b < NB - 1 else LAST_ROWS
            sp.dma_start(to[:, 0:(BW - 1) * DIM].rearrange("p (t d) -> p t d", d=DIM),
                         x[b * BN:b * BN + (BW - 1) * P, :].rearrange("(t p) d -> p t d", p=P)).then_inc(done, 16)
            sp.dma_start(to[0:last, (BW - 1) * DIM:BW * DIM],
                         x[b * BN + (BW - 1) * P:b * BN + (BW - 1) * P + last, :]).then_inc(done, 16)


        with nc.Block() as block:
            order_edges(nc, block, ctx, src, dst, src_pad, dst_pad, arena, pads, pads_set, edges_copied, bank,
                        lambda sp: (load_x(sp, 0, y[0], x_in[0]), load_x(sp, 1, y[1], x_in[1])))

        block = ctx.enter_context(nc.Block())

        @block.sync
        def _(sp):
            for k in range(2):
                o = k * (ROW + HEADS)
                sp.dma_start(waug[:, o:o + ROW].rearrange("p (h c) -> p h c", c=HC)[:, :, 0:HEAD_DIM],
                             gat_w[k * P:(k + 1) * P, :].rearrange("p (h c) -> p h c", c=HEAD_DIM)).then_inc(gat_in, 16)
            sp.dma_start(attb[:, 0:DIM], att_src.rearrange("h c -> (h c)").partition_broadcast(P)).then_inc(gat_in, 16)
            sp.dma_start(attb[:, DIM:2 * DIM], att_dst.rearrange("h c -> (h c)").partition_broadcast(P)).then_inc(gat_in, 16)
            sp.dma_start(gbias[:, :], gat_bias.partition_broadcast(P)).then_inc(gat_in, 16)
            sp.wait_ge(bounds_ready, 1)
            with nc.allow_non_contiguous_dma(reason="one word per group"):
                for c in range(CHUNKS):
                    n = min(P, NG - c * P)
                    sp.dma_start(prev_first[0:n, c:c + 1], dst_pad[c * P:c * P + n, 0:1]).then_inc(bounds_in, 16)
                    sp.dma_start(prev_last[0:n, c:c + 1], dst_pad[c * P:c * P + n, GE - 1:GE]).then_inc(bounds_in, 16)
            for b in range(2, NB):
                sp.wait_ge(p1_xn, BW * (b - 1))
                load_x(sp, b, y[b % 2], x_in[b % 2])
            for k in range(2):
                sp.dma_start(rw1[:, k * ROUTER_H:(k + 1) * ROUTER_H], r_w1[k * P:(k + 1) * P, :]).then_inc(weights_in, 16)
            sp.dma_start(rw2[:, :], r_w2).then_inc(weights_in, 16)
            sp.dma_start(rb2[:, :], r_b2.partition_broadcast(P)).then_inc(weights_in, 16)
            for w, d in ((ew1, e_w1), (ew2, e_w2), (ew3, e_w3)):
                for e in range(EXPERTS):
                    sp.dma_start(w[:, e * 512:(e + 1) * 512].rearrange("p (k n) -> p k n", k=2),
                                 d[e, :, :].rearrange("(k p) n -> p k n", p=P)).then_inc(weights_in, 16)
            with nc.allow_non_contiguous_dma(reason="biases one word per partition"):
                sp.dma_start(rb1[:, :], r_b1.rearrange("(p o) -> p o", o=1)).then_inc(weights_in, 16)
                sp.dma_start(eb1[:, :].rearrange("p (e m) -> p e m", m=2), e_b1.rearrange("e (m p) -> p e m", p=P)).then_inc(weights_in, 16)
                sp.dma_start(eb2[:, :].rearrange("p (e m) -> p e m", m=2), e_b2.rearrange("e (m p) -> p e m", p=P)).then_inc(weights_in, 16)
            sp.dma_start(eb3[:, :], e_b3.rearrange("e d -> (e d)").partition_broadcast(P)).then_inc(weights_in, 16)
            sp.wait_ge(shifted_set, 1)
            for b in range(NB):
                sp.dma_start(node_rows[b * BN:(b + 1) * BN, :].rearrange("(t p) c -> p t c", p=P),
                             acc[:, b * BW * ROW:(b + 1) * BW * ROW].rearrange("p (t c) -> p t c", c=ROW)).then_inc(node_rows_out, 16)
            sp.wait_ge(sched_set, 1)
            for q in range(CHUNKS):
                for h in range(HEADS):
                    sp.dma_start(flag_rows[q * P:(q + 1) * P, :, h, :],
                                 change[:, q * GE:(q + 1) * GE].rearrange("p (j e) -> p j e", j=TILES)).then_inc(flags_out, 16)
            with nc.allow_non_contiguous_dma(reason="one word per step"):
                sp.dma_start(window_list.rearrange("(q p) -> p q", p=P), win_i).then_inc(windows_out, 16)
            sp.wait_ge(windows_out, 16)
            sp.dma_start(windows[0:1, :], window_list.unsqueeze(0)).then_inc(windows_in, 16)
            sp.wait_ge(flags_out, 16 * CHUNKS * HEADS)

            def load_flags(s, u):
                sp.dma_start(flag_ring[:, u * P:(u + 1) * P],
                             flag_rows[bass.ds(s, 1), :, :, :].rearrange("s j h e -> (s j h) e")).then_inc(flags_in[u], 16)

            for s in range(UNROLL):
                load_flags(s, s)
            with sp.Fori(1, STEPS // UNROLL) as it:
                for u in range(UNROLL):
                    sp.wait_ge(scanned, it * UNROLL + (u - UNROLL + 1))
                    load_flags(it * UNROLL + u, u)

            sp.wait_ge(cols_set, STEPS)
            sp.wait_ge(idx_ready, STEPS)
            load_x(sp, 0, xblk[0], xblk_in[0])
            load_x(sp, 1, xblk[1], xblk_in[1])
            for b in range(NB):
                sp.wait_ge(block_done, b + 1)
                last = P if b < NB - 1 else LAST_ROWS
                sp.dma_start(out[b * BN:b * BN + (BW - 1) * P, :].rearrange("(t p) d -> p t d", p=P),
                             y[b % 2][:, 0:(BW - 1) * DIM].rearrange("p (t d) -> p t d", d=DIM)).then_inc(out_sem, 16)
                sp.dma_start(out[b * BN + (BW - 1) * P:b * BN + (BW - 1) * P + last, :],
                             y[b % 2][0:last, (BW - 1) * DIM:BW * DIM]).then_inc(out_sem, 16)
                sp.wait_ge(out_sem, 32 * (b + 1))
                if b + 2 < NB:
                    load_x(sp, b + 2, xblk[b % 2], xblk_in[b % 2])

        @block.gpsimd
        def _(pool):
            pool.memset(ident[:, :], 0.0).then_inc(const_step, 1)
            pool.memset(ident_b[:, :], 0.0).then_inc(const_step, 1)
            pool.memset(tri, 1.0).then_inc(const_step, 1)
            pool.wait_ge(const_step, 3)
            for m in (ident, ident_b):
                pool.affine_select(out=m[:, :], in_=m[:, :], compare_op=ALU.not_equal, fill=1.0,
                                   base=0, pattern=[[-1, P]], channel_multiplier=1).then_inc(consts, 1)
            pool.affine_select(out=tri, in_=tri, compare_op=ALU.is_ge, fill=0.0,
                               base=0, pattern=[[1, P]], channel_multiplier=-1).then_inc(consts, 1)
            pool.iota(iota_b[:, :], [[1, P]], base=0, channel_multiplier=0,
                      allow_small_or_imprecise_dtypes=True).then_inc(consts, 1)
            pool.iota(iota_step, [[1, CHUNKS * P]], base=1, channel_multiplier=0,
                      allow_small_or_imprecise_dtypes=True).then_inc(consts, 1)
            pool.iota(step_no, [[P, CHUNKS]], base=1, channel_multiplier=1,
                      allow_small_or_imprecise_dtypes=True).then_inc(consts, 1)
            pool.iota(rev[:, :], [[0, BW], [-1, EXPERTS]], base=EXPERTS, channel_multiplier=0,
                      allow_small_or_imprecise_dtypes=True).then_inc(consts, 1)
            pool.memset(ones, 1.0).then_inc(consts, 1)
            pool.memset(eps[:, :], LN_EPS).then_inc(consts, 1)
            pool.wait_ge(groups_set, 1)
            for q in range(CHUNKS):
                for to, table in ((dst_i, dst_pad), (src_i, src_pad)):
                    pool.indirect_dma_start(to[:, q * GE:(q + 1) * GE], None, table,
                                            bass.IndirectOffsetOnAxis(ap=group_no[:, q:q + 1], axis=0)).then_inc(group_rows_in, 16)
            pool.wait_ge(node_rows_out, 16 * NB)

            def gather(u):
                for j in range(TILES):
                    pool.indirect_dma_start(rows(u)[:, j * ROW:(j + 1) * ROW], None, node_rows,
                                            bass.IndirectOffsetOnAxis(ap=idx_ring[:, u * TILES + j:u * TILES + j + 1], axis=0)
                                            ).then_inc(rows_in[u], 16)

            for u in range(UNROLL):
                pool.wait_ge(idx_ready, u + 1)
                gather(u)
            with pool.Fori(1, STEPS // UNROLL) as it:
                for u in range(UNROLL):
                    pool.wait_ge(idx_ready, it * UNROLL + (u + 1))
                    pool.wait_ge(agg_ps, it * UNROLL + (u - UNROLL + 1))
                    pool.nop(nofuse=True)
                    gather(u)

        FIRST_IT, LAST_IT = 2, STEPS // UNROLL - 1

        def iterate(eng, body):
            for k in range(-1, FIRST_IT * UNROLL):
                body(k // UNROLL, k % UNROLL, lambda off: 0 <= k + off < STEPS)
            with eng.Fori(FIRST_IT, LAST_IT) as it:
                for u in range(UNROLL):
                    body(it, u, lambda off: True)
            for k in range(LAST_IT * UNROLL, STEPS + 2):
                body(k // UNROLL, k % UNROLL, lambda off: 0 <= k + off < STEPS)

        def iterate_blocks(eng, run):
            with eng.Fori(0, NB // 2) as it:
                for par in range(2):
                    run(it * 2 + par, par, True)
            run(NB - 1, (NB - 1) % 2, False)

        @block.scalar
        def _(act):
            act.wait_ge(consts, 9)

            def p1_std_of(b):
                act.wait_ge(p1_var, BW * (b + 1))
                act.activation(std[b % 2][:, :].unsqueeze(2), mv3[b % 2][:, :].rearrange("p (t two) -> p t two", two=2)[:, :, 1:2],
                               ACT.Sqrt, bias=eps[:, 0:1]).then_inc(p1_std, 1)

            p1_std_of(0)
            for b in range(NB):
                for i in range(BW):
                    t = b * BW + i
                    if i == 2 and b + 1 < NB:
                        p1_std_of(b + 1)
                    act.wait_ge(p1_xt_ps, t + 1)
                    act.activation(xnt0[:, t % 2 * DIM:(t % 2 + 1) * DIM], bank[t % 2][:, 0:DIM], ACT.Copy).then_inc(p1_xt, 1)
            act.wait_ge(self_fall, 1)
            act.activation(ad_rest[:, NW * HEADS:2 * NW * HEADS], ad_rest[:, 0:NW * HEADS], ACT.Exp).then_inc(self_weight, 1)
            n = 0
            for q in range(CHUNKS):
                for c in range(3):
                    act.wait_ge(col_ps, n + 1)
                    act.activation(columns[:, q * P:(q + 1) * P, c * TILES:(c + 1) * TILES].rearrange("p s j -> p j s"),
                                   bank[4 + n % 2][:, :].rearrange("p (j s) -> p j s", j=TILES), ACT.Copy).then_inc(col_copied, 1)
                    n += 1
            act.wait_ge(col_copied, n)
            act.wait_ge(flags_out, 16 * CHUNKS * HEADS)
            act.wait_ge(windows_in, 16)

            def stage_columns(it, u):
                at = columns[:, bass.ds(it * UNROLL + u, 1), :]
                act.activation(idx_ring[:, u * TILES:(u + 1) * TILES], at[:, :, 2 * TILES:3 * TILES].rearrange("p s c -> p (s c)"),
                               ACT.Copy).then_inc(idx_ready, 1)
                act.activation(col_ring[:, u * 8:u * 8 + 8], at[:, :, 0:2 * TILES].rearrange("p s c -> p (s c)"),
                               ACT.Copy).then_inc(cols_set, 1)

            for u in range(2):
                stage_columns(0, u)

            seen = {}

            def window_of(it, u):
                return act.value_load(windows[0:1, bass.ds(it * UNROLL + u, 1)], min_val=0, max_val=NW - 1)

            def act_iter(it, u, on):
                k = it * UNROLL + u
                v = (u - 1) % UNROLL
                if on(-1):
                    act.wait_ge(fall_set, k)
                    act.activation(keep[:, v * HEADS:(v + 1) * HEADS], fall[:, v * HEADS:(v + 1) * HEADS], ACT.Exp).then_inc(keep_set, 1)
                if on(-2):
                    u2 = (u - 2) % UNROLL
                    w = seen[u2] if u >= 3 else window_of(it + (u - 2) // UNROLL, u2)
                    act.wait_ge(keep_set, k - 1)
                    if on(-3):
                        act.wait_ge(added, k - 2)
                    act.nop(nofuse=True)
                    for h in range(HEADS):
                        part = acc[:, bass.ds(w * ROW + h * HC, HC)]
                        last = act.activation(part, part, ACT.Copy, scale=keep[:, u2 * HEADS + h:u2 * HEADS + h + 1])
                    last.then_inc(scaled, 1)
                if on(3):
                    it3, u3 = it + (u + 3) // UNROLL, (u + 3) % UNROLL
                    if not isinstance(it3, int) or it3 > 0:
                        act.wait_ge(rows_in[u3], it3 * (16 * TILES))
                        act.nop(nofuse=True)
                    stage_columns(it3, u3)
                if on(-1):
                    act.wait_ge(z_set, k)
                    act.activation(wexp[:, v * 16:v * 16 + 16], zexp[:, v * 16:v * 16 + 16], ACT.Exp).then_inc(wexp_set, 1)
                if on(1):
                    n = (u + 1) % UNROLL
                    act.wait_ge(onehot_set, k + 2)
                    act.activation(onehot32(n), onehot(n), ACT.Copy).then_inc(onehot32_set, 1)
                    act.wait_ge(oht_ps, k + 2)
                    act.activation(onehot_t(n), bank[n % 2][:, :].bitcast(bf16)[:, 0:TILES * P], ACT.Copy).then_inc(oht_set, 1)
                    w = seen[n] = window_of(it + (u + 1) // UNROLL, n)
                    act.activation(part_ring[:, n * 24:(n + 1) * 24], parts3[:, bass.ds(w * 24, 24)], ACT.Copy).then_inc(parts_set, 1)

            iterate(act, act_iter)

            act.wait_ge(weights_in, 16 * N_WEIGHTS)
            act.wait_ge(added, STEPS)

            def front_act(b, par, piece):
                if piece == "norm":
                    act.wait_ge(p3_var, (b + 1) * BW)
                    act.activation(std[par][:, :].unsqueeze(2), mv3[par][:, :].rearrange("p (t two) -> p t two", two=2)[:, :, 1:2],
                                   ACT.Sqrt, bias=eps[:, 0:1]).then_inc(p3_std, 1)
                elif piece == "turn":
                    for g in range(4):
                        nt = 2 if g < 3 else 1
                        act.wait_ge(p3_yt_ps, b * 4 + (g + 1))
                        act.activation(ynt[par][:, :].rearrange("p (k n) -> p k n", k=2)[:, :, 2 * g * P:(2 * g + nt) * P]
                                       .rearrange("p k (t n) -> p t k n", t=nt),
                                       bank[6 + g % 2][:, 0:nt * DIM].rearrange("p (t k n) -> p t k n", t=nt, k=2),
                                       ACT.Copy).then_inc(p3_yt, 1)
                    for half in range(2):
                        act.wait_ge(p3_rh_ps, b * 2 + (half + 1))
                        act.activation(rht[:, half * HALF:(half + 1) * HALF], bank[6 + half][:, 0:HALF], ACT.Relu,
                                       bias=rb1[:, 0:1]).then_inc(p3_rh, 1)
                elif piece == "route":
                    act.wait_ge(p3_ex_in, b + 1)
                    act.activation(rt[:, 42:84], rt[:, 0:42], ACT.Exp).then_inc(p3_ex_out, 1)
                    act.wait_ge(p3_e2_in, b + 1)
                    act.activation(rt[:, 7 * 42 + 7:7 * 42 + 14], rt[:, 7 * 42:7 * 42 + 7], ACT.Exp).then_inc(p3_e2_out, 1)

            def hidden_act(s, par, e, layer):
                to, bias, ready, done = ((h1t[par], eb1, h1_ps, h1_set), (h2t[par], eb2, h2_ps, h2_set))[layer]
                for m in range(2):
                    for half in range(2):
                        i = 2 * m + half
                        act.wait_ge(ready, s * 4 + (i + 1))
                        act.activation(to[:, m * BN + half * HALF:m * BN + (half + 1) * HALF], bank[i][:, 0:HALF],
                                       ACT.Relu, bias=bias[:, 2 * e + m:2 * e + m + 1]).then_inc(done, 1)

            for piece in ("norm", "turn", "route"):
                front_act(0, 0, piece)
            act.activation(eps[:, 0:1], eps[:, 0:1], ACT.Copy).then_inc(h2_set, 4)
            hidden_act(0, 0, 0, 0)

            def act_block(b, par, has_next):
                for kind, e in block_parts(has_next):
                    if kind in ("sum", "norm", "turn", "route"):
                        front_act(b + 1, 1 - par, kind)
                    elif kind == "h1":
                        hidden_act(b * EXPERTS + e, e % 2, e % EXPERTS, 0)
                    elif kind == "h2":
                        hidden_act(b * EXPERTS + e, e % 2, e, 1)

            iterate_blocks(act, act_block)

        @block.tensor
        def _(pe):
            pe.wait_ge(consts, 9)

            def p1_turn(t):
                pe.wait_ge(p1_xn, t + 1)
                if t >= 2:
                    pe.wait_ge(p1_xt, t - 1)
                b, i = t // BW, t % BW
                for kk in range(2):
                    last = pe.transpose(bank[t % 2][:, kk * P:(kk + 1) * P], xn0[b % 2][:, i * DIM + kk * P:i * DIM + (kk + 1) * P], ident[:, :])
                last.then_inc(p1_xt_ps, 1)

            def p1_project(t):
                s = t % 2
                pe.wait_ge(p1_xt, t + 1)
                if t >= 2:
                    pe.wait_ge(p1_ad, t - 1)
                for kk in range(2):
                    last = pe.matmul(bank[2 + s][:, 0:ROW + HEADS], xnt0[:, s * DIM + kk * P:s * DIM + (kk + 1) * P],
                                     waug[:, kk * (ROW + HEADS):(kk + 1) * (ROW + HEADS)], start=(kk == 0), stop=(kk == 1))
                last.then_inc(p1_h, 1)

            p1_turn(0)
            pe.wait_ge(waug_set, 1)
            for t in range(NW):
                if t + 1 < NW:
                    p1_turn(t + 1)
                p1_project(t)
                if t == 0:
                    pe.wait_ge(before_set, 1)
                    pe.matmul(bank[6][:, 0:CHUNKS], tri, width[:, :, 1:2].rearrange("p c o -> p (c o)"), start=True, stop=False)
                    pe.matmul(bank[6][:, 0:CHUNKS], ones, shifted, start=False, stop=True).then_inc(cum_ps, 1)
                    pe.wait_ge(before_set, 2)
                    for q in range(CHUNKS):
                        for c in range(CHUNKS):
                            last = pe.matmul(bank[7][:, 2 * q:2 * q + 2], before[:, c * 512 + q * P:c * 512 + (q + 1) * P],
                                             width[:, c, :], start=(c == 0), stop=(c == CHUNKS - 1))
                    last.then_inc(found_ps, 1)
            pe.wait_ge(least_turn, 1)
            pe.transpose(bank[6][0:HEADS, 0:P], least[:, 0:HEADS], ident[:, :]).then_inc(least_ps, 1)
            pe.wait_ge(least_row, 1)
            pe.matmul(bank[7][:, 0:HEADS], ones[0:HEADS, :], least[0:HEADS, 8:12], start=True, stop=True).then_inc(least_all, 1)
            pe.wait_ge(sched_set, 1)
            n = 0
            for q in range(CHUNKS):
                for of in (rel_q, end_q, src_f):
                    if n >= 2:
                        pe.wait_ge(col_copied, n - 1)
                    for j in range(TILES):
                        last = pe.transpose(bank[4 + n % 2][:, j * P:(j + 1) * P], of[:, q * GE + j * P:q * GE + (j + 1) * P], ident[:, :])
                    last.then_inc(col_ps, 1)
                    n += 1

            def pe_iter(it, u, on):
                k = it * UNROLL + u
                v = (u - 1) % UNROLL

                def sum_rows(tiles):
                    for j in tiles:
                        last = pe.matmul(bank[6 + v % 2][:, 0:ROW], onehot32(v)[:, j * P:(j + 1) * P],
                                         rows(v)[:, j * ROW:(j + 1) * ROW], start=(j == 0), stop=(j == TILES - 1))
                    return last

                if on(0):
                    pe.wait_ge(scanned, k + 1)
                    pe.nop(nofuse=True)
                    pe.transpose(bank[3][:, 0:16], scan_ring[:, u * P:(u + 1) * P], ident[0:16, 0:16]).then_inc(scan_ps, 1)
                if on(1):
                    n = (u + 1) % UNROLL
                    pe.wait_ge(onehot_set, k + 2)
                    if on(-1):
                        pe.wait_ge(oht_set, k)
                    for j in range(TILES):
                        last = pe.transpose(bank[n % 2][:, :].bitcast(bf16)[:, j * P:(j + 1) * P], onehot(n)[:, j * P:(j + 1) * P], ident_b[:, :])
                    last.then_inc(oht_ps, 1)
                if on(0):
                    pe.wait_ge(seg_set, k + 1)
                    for j in range(TILES):
                        last = pe.matmul(bank[4][:, j * 4:j * 4 + 4], onehot(u)[:, j * P:(j + 1) * P],
                                         seg_ring[:, u * 16 + j * 4:u * 16 + j * 4 + 4], start=True, stop=True)
                    last.then_inc(px_ps, 1)
                if on(-1):
                    if on(-3):
                        pe.wait_ge(added, k - 2)
                    for _ in range(FILL):
                        pe.matmul(bank[6 + v % 2][:, 0:512], ident_b[:, :], onehot(u)[:, 0:512], start=True, stop=True)
                    pe.wait_ge(onehot32_set, k)
                    pe.wait_ge(msg_set, (k - 1) * TILES + 2)
                    sum_rows(range(0, TILES // 2))
                if on(0):
                    pe.wait_ge(oht_set, k + 1)
                    pe.wait_ge(newmax_set, k + 1)
                    for j in range(TILES):
                        for part in range(3):
                            last = pe.matmul(bank[5][:, j * 8:j * 8 + 8], onehot_t(u)[:, j * P:(j + 1) * P],
                                             part_ring[:, u * 24 + part * 8:u * 24 + part * 8 + 8],
                                             start=(part == 0), stop=(part == 2))
                    last.then_inc(ex_ps, 1)
                if on(1):
                    n = (u + 1) % UNROLL
                    pe.wait_ge(rows_in[n], (it + (u + 1) // UNROLL + 1) * (16 * TILES))
                    scores = rows(n).rearrange("p (r c) -> p r c", c=HC)[:, :, HEAD_DIM:HC].rearrange("p r o -> p (r o)")
                    pe.transpose(bank[2][0:16, 0:P], scores, ident[:, :]).then_inc(score_ps, 1)
                if on(-1):
                    pe.wait_ge(msg_set, k * TILES)
                    sum_rows(range(TILES // 2, TILES)).then_inc(agg_ps, 1)

            iterate(pe, pe_iter)

            pe.wait_ge(weights_in, 16 * N_WEIGHTS)

            def front_pe(b, par, piece):
                if piece != "turn":
                    return
                pe.wait_ge(p3_yn, b + 1)
                for g in range(4):
                    nt = 2 if g < 3 else 1
                    if g >= 2:
                        pe.wait_ge(p3_yt, b * 4 + (g - 1))
                    for i in range(nt):
                        t = 2 * g + i
                        for kk in range(2):
                            last = pe.transpose(bank[6 + g % 2][:, (2 * i + kk) * P:(2 * i + kk + 1) * P],
                                                yn[:, t * DIM + kk * P:t * DIM + (kk + 1) * P], ident[:, :])
                    last.then_inc(p3_yt_ps, 1)
                pe.wait_ge(p3_yt, b * 4 + 4)
                for half in range(2):
                    for kk in range(2):
                        last = pe.matmul(bank[6 + half][:, 0:HALF], rw1[:, kk * ROUTER_H:(kk + 1) * ROUTER_H],
                                         ynt[par][:, kk * BN + half * HALF:kk * BN + (half + 1) * HALF],
                                         start=(kk == 0), stop=(kk == 1))
                    last.then_inc(p3_rh_ps, 1)
                pe.wait_ge(p3_rh, b * 2 + 2)
                for t in range(BW):
                    last = pe.matmul(bank[6][:, t * EXPERTS:(t + 1) * EXPERTS], rht[:, t * P:(t + 1) * P], rw2[:, :],
                                     start=True, stop=True)
                last.then_inc(p3_lg_ps, 1)

            def hidden_pe(s, par, e, ypar, layer, before):
                frm = ynt[ypar] if layer == 0 else h1t[par]
                w, done = ((ew1, h1_ps), (ew2, h2_ps))[layer]
                if layer == 1:
                    pe.wait_ge(h1_set, s * 4 + 4)
                for m in range(2):
                    for half in range(2):
                        i = 2 * m + half
                        if before == "h2 of s-2":
                            pe.wait_ge(h2_set, s * 4 + (i - 3))
                        elif before == "h1 of s+1":
                            pe.wait_ge(h1_set, s * 4 + (i + 5))
                        elif before == "h2 of s-1":
                            pe.wait_ge(h2_set, s * 4 + (i + 1))
                        for kk in range(2):
                            last = pe.matmul(bank[i][:, 0:HALF], w[:, e * 512 + kk * 256 + m * P:e * 512 + kk * 256 + (m + 1) * P],
                                             frm[:, kk * BN + half * HALF:kk * BN + (half + 1) * HALF],
                                             start=(kk == 0), stop=(kk == 1))
                        last.then_inc(done, 1)

            def out_pe(s, par, e):
                pe.wait_ge(h2_set, s * 4 + 8)
                for t in range(BW):
                    pe.wait_ge(o_used, s * BW + (t + 1))
                    for kk in range(2):
                        last = pe.matmul(bank[4 + (e + t) % 2][:, 0:DIM], h2t[par][:, kk * BN + t * P:kk * BN + (t + 1) * P],
                                         ew3[:, e * 512 + kk * 256:e * 512 + (kk + 1) * 256], start=(kk == 0), stop=(kk == 1))
                    last.then_inc(o_ps, 1)

            front_pe(0, 0, "turn")
            hidden_pe(0, 0, 0, 0, 0, None)
            pe.wait_ge(h1_set, 4)

            def pe_block(b, par, has_next):
                for kind, e in block_parts(has_next):
                    if kind in ("sum", "norm", "turn", "route"):
                        front_pe(b + 1, 1 - par, kind)
                    elif kind == "h1":
                        hidden_pe(b * EXPERTS + e, e % 2, e % EXPERTS, par if e < EXPERTS else 1 - par, 0, "h2 of s-2")
                    elif kind == "h2":
                        hidden_pe(b * EXPERTS + e, e % 2, e, par, 1,
                                  "h1 of s+1" if has_next or e + 1 < EXPERTS else "h2 of s-1")
                    else:
                        out_pe(b * EXPERTS + e, e % 2, e)

            iterate_blocks(pe, pe_block)

        @block.vector
        def _(dve):
            links = [0]

            def link(ins):
                links[0] += 1
                ins.then_inc(dve_link, 1)
                dve.wait_ge(dve_link, links[0])

            def p1_norm(b):
                xb, mv, n0 = y[b % 2], mv3[b % 2], b * BW
                dve.wait_ge(x_in[b % 2], 32 * (b // 2 + 1))
                if b >= 2:
                    dve.wait_ge(p1_h, n0 - BW)
                for i in range(BW):
                    dve.bn_stats(stats3[:, i * 6:(i + 1) * 6], xb[:, i * DIM:(i + 1) * DIM]).then_inc(p1_stats, 1)
                for i in range(BW):
                    dve.wait_ge(p1_stats, n0 + i + 1)
                    dve.bn_aggr(mv[:, 2 * i:2 * i + 2], stats3[:, i * 6:(i + 1) * 6]).then_inc(p1_var, 1)

            def p1_apply(b):
                xb, mv, n0 = y[b % 2], mv3[b % 2], b * BW
                dve.wait_ge(p1_std, b + 1)
                dve.reciprocal(rstd[b % 2][:, :], std[b % 2][:, :]).then_inc(p1_rstd, 1)
                dve.wait_ge(p1_rstd, b + 1)
                for i in range(BW):
                    dve.tensor_scalar(xn0[b % 2][:, i * DIM:(i + 1) * DIM], xb[:, i * DIM:(i + 1) * DIM],
                                      mv[:, 2 * i:2 * i + 1], rstd[b % 2][:, i:i + 1], ALU.subtract, ALU.mult).then_inc(p1_xn, 1)

            def p1_take(t):
                s = t % 2
                dve.wait_ge(p1_h, t + 1)
                dve.tensor_copy(acc[:, t * ROW:(t + 1) * ROW], bank[2 + s][:, 0:ROW]).then_inc(p1_acc, 1)
                dve.tensor_copy(state[:, t * 8 + 4:t * 8 + 8], bank[2 + s][:, ROW:ROW + HEADS]).then_inc(p1_ad, 1)

            link(dve.memset(ints[:, 3:4], 0))
            link(dve.memset(ints[:, 7:8], P * 1000))
            dve.memset(small[:, 60:61], 0.0).then_inc(bounds_ready, 1)
            p1_norm(0)
            dve.wait_ge(gat_in, 16 * 5)
            for kk in range(2):
                o = kk * (ROW + HEADS)
                feats = waug[:, o:o + ROW].rearrange("p (h c) -> p h c", c=HC)
                for which in range(2):
                    link(dve.tensor_tensor(att_prod.rearrange("p (h c) -> p h c", h=HEADS), feats[:, :, 0:HEAD_DIM],
                                           attb[:, which * DIM:(which + 1) * DIM].rearrange("p (h c) -> p h c", h=HEADS), ALU.mult))
                    to = feats[:, :, HEAD_DIM:HC] if which == 0 else waug[:, o + ROW:o + ROW + HEADS].unsqueeze(2)
                    link(dve.tensor_reduce(to, att_prod.rearrange("p (h c) -> p h c", h=HEADS), AX.X, ALU.add))
            dve.memset(small[:, 59:60], 0.0).then_inc(waug_set, 1)
            p1_apply(0)
            dve.wait_ge(consts, 9)
            dve.wait_ge(bounds_in, 16 * N_BOUNDS)
            link(dve.tensor_single_scalar(ints[:, 8:16], ints[:, 0:8], 7, ALU.arith_shift_right))
            link(dve.tensor_copy(prev_f, ints[:, 8:16]))
            link(dve.memset(width, 1.0))
            link(dve.scalar_tensor_tensor(width[:, :, 1:2].rearrange("p c o -> p (c o)"), prev_f[:, 4:8], 1.0, prev_f[:, 0:4], ALU.add, ALU.subtract))
            link(dve.memset(shifted, 0.0))
            for c in range(1, CHUNKS):
                link(dve.tensor_tensor(shifted[:, c:c + 1], shifted[:, c - 1:c], width[:, c - 1, 1:2], ALU.add))
            dve.memset(small[:, 61:62], 0.0).then_inc(before_set, 1)
            dve.wait_ge(cum_ps, 1)
            link(dve.tensor_copy(cum, bank[6][:, 0:CHUNKS]))
            for c in range(CHUNKS):
                link(dve.tensor_scalar(before[:, c * 512:(c + 1) * 512], iota_step, cum[:, c:c + 1], None, ALU.is_ge))
            dve.memset(small[:, 61:62], 0.0).then_inc(before_set, 1)
            dve.wait_ge(found_ps, 1)
            link(dve.tensor_copy(found, bank[7][:, 0:2 * CHUNKS]))
            counts = found.rearrange("p (q two) -> p q two", two=2)
            dve.tensor_copy(group_no, counts[:, :, 0:1].rearrange("p q o -> p (q o)")).then_inc(groups_set, 1)

            for b in range(NB):
                if b + 1 < NB:
                    p1_norm(b + 1)
                for i in range(BW):
                    p1_take(b * BW + i)
                    if i == 1 and b + 1 < NB:
                        p1_apply(b + 1)

            acc_all = acc[:, :].rearrange("p (t h c) -> p t h c", h=HEADS, c=HC)
            score_all = acc_all[:, :, :, HEAD_DIM:HC].rearrange("p t h o -> p t (h o)")
            st_all = state[:, :].rearrange("p (t c) -> p t c", c=8)
            dve.wait_ge(p1_acc, NW)
            dve.wait_ge(p1_ad, NW)
            dve.tensor_reduce(least[:, 0:HEADS].unsqueeze(2), score_all.rearrange("p t h -> p h t"), AX.X, ALU.min).then_inc(least_turn, 1)
            dve.wait_ge(least_ps, 1)
            link(dve.tensor_reduce(least[0:HEADS, 4:5], bank[6][0:HEADS, 0:P], AX.X, ALU.min))
            dve.tensor_scalar(least[0:HEADS, 8:12], ident[0:HEADS, 0:HEADS], least[0:HEADS, 4:5], None, ALU.mult).then_inc(least_row, 1)
            dve.wait_ge(least_all, 1)
            link(dve.tensor_copy(least[:, 12:16], bank[7][:, 0:HEADS]))
            least_w = least[:, 12:16].unsqueeze(1).to_broadcast([P, NW, HEADS])
            link(dve.tensor_tensor(score_all, score_all, least_w, ALU.subtract))
            dve.memset(small[:, 60:61], 0.0).then_inc(shifted_set, 1)
            link(dve.tensor_tensor(st_all[:, :, 4:8], st_all[:, :, 4:8], least_w, ALU.add))
            rest = [ad_rest[:, i * NW * HEADS:(i + 1) * NW * HEADS].rearrange("p (t h) -> p t h", h=HEADS) for i in (0, 1)]
            pr = parts3[:, :].rearrange("p (t c) -> p t c", c=24)
            link(dve.memset(parts3[:, :], 0.0))
            link(dve.tensor_copy(pr[:, :, 0:4], st_all[:, :, 4:8]))
            link(dve.tensor_tensor(rest[0], st_all[:, :, 4:8], pr[:, :, 0:4], ALU.subtract))
            link(dve.tensor_copy(pr[:, :, 8:12], rest[0]))
            link(dve.tensor_tensor(rest[1], rest[0], pr[:, :, 8:12], ALU.subtract))
            link(dve.tensor_copy(pr[:, :, 16:20], rest[1]))
            link(dve.tensor_tensor(rest[0], score_all, st_all[:, :, 4:8], ALU.add))
            link(dve.scalar_tensor_tensor(rest[1], rest[0], SLOPE, rest[0], ALU.mult, ALU.max))
            link(dve.tensor_copy(pr[:, :, 4:8], rest[1]))
            link(dve.tensor_copy(st_all[:, :, 0:4], pr[:, :, 4:8]))
            dve.tensor_tensor(rest[0], rest[1], st_all[:, :, 0:4], ALU.subtract).then_inc(self_fall, 1)

            dve.wait_ge(group_rows_in, 16 * 2 * CHUNKS)
            dst_q = dst_i.rearrange("p (q e) -> p q e", e=GE)
            link(dve.tensor_single_scalar(first_w, dst_q[:, :, 0:1].rearrange("p q o -> p (q o)"), 7, ALU.arith_shift_right))
            link(dve.tensor_copy(win_f, first_w))
            link(dve.tensor_tensor(win_f, win_f, step_no, ALU.add))
            link(dve.tensor_tensor(win_f, win_f, counts[:, :, 1:2].rearrange("p q o -> p (q o)"), ALU.subtract))
            link(dve.tensor_single_scalar(neg_w, win_f, -float(P), ALU.mult))
            link(dve.tensor_single_scalar(win_i, win_f, float(NW - 1), ALU.min))
            for q in range(CHUNKS):
                link(dve.tensor_scalar(rel_q[:, q * GE:(q + 1) * GE], dst_i[:, q * GE:(q + 1) * GE], neg_w[:, q:q + 1], None, ALU.add))
            rel3 = rel_q.rearrange("p (q e) -> p q e", e=GE)
            chg3 = change[:, 0:CHUNKS * GE].rearrange("p (q e) -> p q e", e=GE)
            link(dve.memset(chg3[:, :, 0:1], 0.0))
            link(dve.tensor_tensor(chg3[:, :, 1:GE], rel3[:, :, 1:GE], rel3[:, :, 0:GE - 1], ALU.not_equal))
            end3 = end_q.rearrange("p (r e) -> p r e", e=P)
            chr3 = change[:, 0:CHUNKS * GE].rearrange("p (r e) -> p r e", e=P)
            link(dve.tensor_copy(end3[:, :, 0:P - 1], chr3[:, :, 1:P]))
            link(dve.memset(end3[:, :, P - 1:P], 1.0))
            link(dve.tensor_single_scalar(change[:, 0:CHUNKS * GE], change[:, 0:CHUNKS * GE], -BIG, ALU.mult))
            link(dve.tensor_copy(src_f, src_i))
            dve.memset(small[:, 63:64], 0.0).then_inc(sched_set, 1)

            dve.wait_ge(self_weight, 1)
            dve.wait_ge(node_rows_out, 16 * NB)
            parts_all = acc[:, :].rearrange("p (r c) -> p r c", c=HC)
            link(dve.tensor_copy(parts_all[:, :, HEAD_DIM:HC], ad_rest[:, NW * HEADS:2 * NW * HEADS].unsqueeze(2)))
            link(dve.tensor_tensor(parts_all[:, :, 0:HEAD_DIM], parts_all[:, :, 0:HEAD_DIM],
                                   parts_all[:, :, HEAD_DIM:HC].to_broadcast([P, NW * HEADS, HEAD_DIM]), ALU.mult))

            dve.wait_ge(windows_in, 16)
            dve.wait_ge(col_copied, 3 * CHUNKS)
            dve.wait_ge(flags_out, 16 * CHUNKS * HEADS)

            wreg = {}

            def window_of(it, u):
                return dve.value_load(windows[0:1, bass.ds(it * UNROLL + u, 1)], min_val=0, max_val=NW - 1)

            def dve_iter(it, u, on):
                k = it * UNROLL + u
                v = (u - 1) % UNROLL
                scores = rows(v).rearrange("p (j h c) -> p j h c", h=HEADS, c=HC)[:, :, :, HEAD_DIM:HC].rearrange("p j h o -> p j (h o)")
                ex = bank[5][:, 0:32].rearrange("p (j c) -> p j c", c=8)

                def one_hot(tiles):
                    n = (u + 1) % UNROLL
                    for j in tiles:
                        last = dve.tensor_scalar(onehot(n)[:, j * P:(j + 1) * P], iota_b[:, :], col_ring[:, n * 8 + j:n * 8 + j + 1],
                                                 None, ALU.is_equal)
                    return last

                if on(0):
                    dve.wait_ge(flags_in[u], (it + 1) * 16)
                    dve.wait_ge(score_ps, k + 1)
                    dve.tensor_tensor_scan(scan_ring[:, u * P:(u + 1) * P], flag_ring[:, u * P:(u + 1) * P],
                                           bank[2][0:16, 0:P], -BIG, ALU.add, ALU.max).then_inc(scanned, 1)
                if on(-1):
                    dve.wait_ge(ex_ps, k)
                    dve.tensor_tensor(zsum[:, :].rearrange("p (j h) -> p j h", h=HEADS), scores, ex[:, :, 0:4], ALU.add).then_inc(zsum_set, 1)
                if on(1):
                    dve.wait_ge(cols_set, k + 2)
                    one_hot((0, 1))
                if on(-1):
                    dve.wait_ge(zsum_set, k)
                    dve.scalar_tensor_tensor(zlr[:, :], zsum[:, :], SLOPE, zsum[:, :], ALU.mult, ALU.max).then_inc(zlr_set, 1)
                if on(1):
                    one_hot((2,))
                if on(-1):
                    dve.wait_ge(zlr_set, k)
                    dve.tensor_tensor(zexp[:, v * 16:v * 16 + 16].rearrange("p (j h) -> p j h", h=HEADS),
                                      zlr[:, :].rearrange("p (j h) -> p j h", h=HEADS), ex[:, :, 4:8], ALU.subtract).then_inc(z_set, 1)
                if on(1):
                    one_hot((3,)).then_inc(onehot_set, 1)
                if on(0):
                    dve.wait_ge(scan_ps, k + 1)
                    dve.tensor_tensor(seg_ring[:, u * 16:u * 16 + 16].rearrange("p (j h) -> p j h", h=HEADS),
                                      bank[3][:, 0:16].rearrange("p (j h) -> p j h", h=HEADS),
                                      col_ring[:, u * 8 + 4:u * 8 + 8].unsqueeze(2).to_broadcast([P, TILES, HEADS]),
                                      ALU.mult).then_inc(seg_set, 1)
                if on(-1):
                    dve.wait_ge(wexp_set, k)
                    parts = rows(v).rearrange("p (r c) -> p r c", c=HC)
                    weight = wexp[:, v * 16:v * 16 + 16].unsqueeze(2)
                    dve.tensor_single_scalar(parts[:, :, HEAD_DIM:HC], weight, CAP, ALU.min).then_inc(w_set, 1)

                def weigh(j):
                    if on(-1):
                        r = slice(j * HEADS, (j + 1) * HEADS)
                        dve.scalar_tensor_tensor(parts[:, r, 0:HEAD_DIM], weight[:, r, :].to_broadcast([P, HEADS, HEAD_DIM]), CAP,
                                                 parts[:, r, 0:HEAD_DIM], ALU.min, ALU.mult).then_inc(msg_set, 1)

                weigh(0)
                weigh(1)
                if on(0):
                    w = wreg[u] = window_of(it, u)
                    new = part_ring[:, u * 24 + 4:u * 24 + 8]
                    dve.wait_ge(px_ps, k + 1)
                    dve.tensor_reduce(top[:, :].unsqueeze(2), bank[4][:, 0:16].rearrange("p (j h) -> p h j", h=HEADS), AX.X, ALU.max).then_inc(top_set, 1)
                weigh(2)
                if on(0):
                    dve.wait_ge(top_set, k + 1)
                    dve.tensor_tensor(top_e[:, :], top[:, :], state[:, bass.ds(w * 8 + 4, 4)], ALU.add).then_inc(tope_set, 1)
                weigh(3)
                if on(0):
                    dve.wait_ge(tope_set, k + 1)
                    dve.scalar_tensor_tensor(top_l[:, :], top_e[:, :], SLOPE, top_e[:, :], ALU.mult, ALU.max).then_inc(lr_set, 1)
                if on(-2):
                    u2 = (u - 2) % UNROLL
                    w2 = window_of(it + (u - 2) // UNROLL, u2) if u < 2 else wreg[u2]
                    here = acc[:, bass.ds(w2 * ROW, ROW)]
                    dve.wait_ge(scaled, k - 1)
                    dve.wait_ge(agg_ps, k - 1)
                    dve.tensor_tensor(here, here, bank[6 + u2 % 2][:, 0:ROW], ALU.add).then_inc(added, 1)
                if on(0):
                    dve.wait_ge(parts_set, k + 1)
                    if on(-1):
                        dve.wait_ge(max_stored, k)
                    dve.wait_ge(lr_set, k + 1)
                    dve.tensor_tensor(new, top_l[:, :], state[:, bass.ds(w * 8, 4)], ALU.max).then_inc(newmax_set, 1)
                    dve.wait_ge(newmax_set, k + 1)
                    dve.tensor_tensor(fall[:, u * HEADS:(u + 1) * HEADS], state[:, bass.ds(w * 8, 4)], new, ALU.subtract).then_inc(fall_set, 1)
                    dve.wait_ge(fall_set, k + 1)
                    dve.nop(nofuse=True)
                    dve.tensor_copy(state[:, bass.ds(w * 8, 4)], new).then_inc(max_stored, 1)

            iterate(dve, dve_iter)

            dve.wait_ge(weights_in, 16 * N_WEIGHTS)
            dve.wait_ge(added, STEPS)

            class Serial:
                per_block, n, base = 0, 0, 0

            def begin(b):
                Serial.n, Serial.base = 0, b * Serial.per_block

            def plink(ins):
                Serial.n += 1
                ins.then_inc(p3_y, 1)
                dve.wait_ge(p3_y, Serial.base + Serial.n)

            T = [rt[:, i * 42:(i + 1) * 42] for i in range(12)]
            C = [T[i].rearrange("p (t e) -> p t e", e=EXPERTS) for i in range(12)]
            REV = rev[:, :].rearrange("p (t e) -> p t e", e=EXPERTS)

            def one(i):
                return rt[:, 10 * 42 + i * 7:10 * 42 + (i + 1) * 7].unsqueeze(2)

            def wide(i):
                return one(i).to_broadcast([P, BW, EXPERTS])

            def front_dve(b, par, piece):
                yb, mv = y[par], mv3[par]
                if piece == "sum":
                    begin(b)
                    dve.wait_ge(xblk_in[par], (b + (2 - par)) * 16)
                    ab = acc[:, bass.ds(b * (BW * ROW), BW * ROW)].rearrange("p (r c) -> p r c", c=HC)
                    plink(dve.tensor_scalar_add(rsum28[:, :].unsqueeze(2), ab[:, :, HEAD_DIM:HC], SUM_EPS))
                    plink(dve.reciprocal(rsum28[:, :], rsum28[:, :]))
                    plink(dve.tensor_tensor(yb[:, :].rearrange("p (r c) -> p r c", c=HEAD_DIM), ab[:, :, 0:HEAD_DIM],
                                            rsum28[:, :].unsqueeze(2).to_broadcast([P, BW * HEADS, HEAD_DIM]), ALU.mult))
                    plink(dve.tensor_tensor(yb[:, :].rearrange("p (t d) -> p t d", d=DIM), yb[:, :].rearrange("p (t d) -> p t d", d=DIM),
                                            gbias[:, :].unsqueeze(1).to_broadcast([P, BW, DIM]), ALU.add))
                    plink(dve.tensor_tensor(yb[:, :], yb[:, :], xblk[par][:, :], ALU.add))
                elif piece == "norm":
                    for t in range(BW):
                        dve.bn_stats(stats3[:, t * 6:(t + 1) * 6], yb[:, t * DIM:(t + 1) * DIM]).then_inc(p3_stats, 1)
                    for t in range(BW):
                        dve.wait_ge(p3_stats, b * BW + (t + 1))
                        dve.nop(nofuse=True)
                        dve.bn_aggr(mv[:, 2 * t:2 * t + 2], stats3[:, t * 6:(t + 1) * 6]).then_inc(p3_var, 1)
                    dve.wait_ge(p3_std, b + 1)
                    dve.reciprocal(rstd[par][:, :], std[par][:, :]).then_inc(p3_rstd, 1)
                    dve.wait_ge(p3_rstd, b + 1)
                    for t in range(BW):
                        ins = dve.tensor_scalar(yn[:, t * DIM:(t + 1) * DIM], yb[:, t * DIM:(t + 1) * DIM], mv[:, 2 * t:2 * t + 1],
                                                rstd[par][:, t:t + 1], ALU.subtract, ALU.mult)
                    ins.then_inc(p3_yn, 1)
                elif piece == "route":
                    dve.wait_ge(p3_lg_ps, b + 1)
                    plink(dve.tensor_tensor(C[2], bank[6][:, 0:42].rearrange("p (t e) -> p t e", e=EXPERTS),
                                            rb2[:, :].unsqueeze(1).to_broadcast([P, BW, EXPERTS]), ALU.add))
                    plink(dve.tensor_reduce(one(0), C[2], AX.X, ALU.max))
                    dve.tensor_tensor(C[0], C[2], wide(0), ALU.subtract).then_inc(p3_ex_in, 1)
                    dve.wait_ge(p3_ex_out, b + 1)
                    plink(dve.tensor_reduce(one(1), C[1], AX.X, ALU.add))
                    plink(dve.reciprocal(one(2), one(1)))
                    plink(dve.tensor_tensor(C[3], C[1], wide(2), ALU.mult))
                    for r in range(2):
                        prob, hot = C[3 + r], C[5 + r]
                        plink(dve.tensor_reduce(one(3 + r), prob, AX.X, ALU.max))
                        plink(dve.tensor_tensor(C[8], prob, wide(3 + r), ALU.is_equal))
                        plink(dve.tensor_tensor(C[8], C[8], REV, ALU.mult))
                        plink(dve.tensor_reduce(one(5), C[8], AX.X, ALU.max))
                        plink(dve.tensor_tensor(hot, REV, wide(5), ALU.is_equal))
                        if r == 0:
                            plink(dve.scalar_tensor_tensor(T[4], T[5], -2.0, T[3], ALU.mult, ALU.add))
                    e2 = rt[:, 7 * 42 + 7:7 * 42 + 14]
                    dve.tensor_tensor(rt[:, 7 * 42:7 * 42 + 7].unsqueeze(2), one(4), one(3), ALU.subtract).then_inc(p3_e2_in, 1)
                    dve.wait_ge(p3_e2_out, b + 1)
                    plink(dve.tensor_scalar_add(one(6), e2.unsqueeze(2), 1.0))
                    plink(dve.reciprocal(one(7), one(6)))
                    plink(dve.tensor_tensor(one(8), one(7), e2.unsqueeze(2), ALU.mult))
                    plink(dve.tensor_tensor(C[5], C[5], wide(7), ALU.mult))
                    plink(dve.tensor_tensor(C[6], C[6], wide(8), ALU.mult))
                    plink(dve.tensor_tensor(gate[par][:, :].rearrange("p (t e) -> p t e", e=EXPERTS), C[5], C[6], ALU.add))

            def out_dve(s, par, e):
                yb = y[par]
                for t in range(BW):
                    part, g = yb[:, t * DIM:(t + 1) * DIM], gate[par][:, t * EXPERTS + e:t * EXPERTS + e + 1]
                    if e > 0:
                        dve.wait_ge(o_used, s * BW + (t - BW + 3))
                    dve.scalar_tensor_tensor(part, eb3[:, e * DIM:(e + 1) * DIM], g, part, ALU.mult, ALU.add).then_inc(b3_used, 1)
                for t in range(BW):
                    part, g = yb[:, t * DIM:(t + 1) * DIM], gate[par][:, t * EXPERTS + e:t * EXPERTS + e + 1]
                    dve.wait_ge(b3_used, s * BW + (t + 1))
                    dve.wait_ge(o_ps, s * BW + (t + 1))
                    dve.scalar_tensor_tensor(part, bank[4 + (e + t) % 2][:, 0:DIM], g, part, ALU.mult, ALU.add).then_inc(o_used, 1)
                if e == EXPERTS - 1:
                    dve.wait_ge(o_used, s * BW + (BW + 2))
                    dve.tensor_copy(small[:, 64:65], small[:, 60:61]).then_inc(block_done, 1)

            for piece in ("sum", "norm", "route"):
                front_dve(0, 0, piece)
            Serial.per_block = Serial.n
            dve.memset(small[:, 66:67], 0.0).then_inc(o_used, 2)

            def dve_block(b, par, has_next):
                for kind, e in block_parts(has_next):
                    if kind in ("sum", "norm", "turn", "route"):
                        front_dve(b + 1, 1 - par, kind)
                    elif kind == "out":
                        out_dve(b * EXPERTS + e, par, e)

            iterate_blocks(dve, dve_block)


_INS = ["x", "src", "dst", "L0_gnn_W", "L0_gnn_att_src", "L0_gnn_att_dst", "L0_gnn_bias", "L0_ffn_router_w1",
        "L0_ffn_router_b1", "L0_ffn_router_w2", "L0_ffn_router_b2", "L0_ffn_expert_w1", "L0_ffn_expert_b1",
        "L0_ffn_expert_w2", "L0_ffn_expert_b2", "L0_ffn_expert_w3", "L0_ffn_expert_b3"]


def kernel(**inputs):
    import numpy as _np
    import concourse.bacc as _bacc
    from concourse import mybir as _mybir
    from concourse.bass_utils import run_bass_kernel_spmd as _run

    nc = _bacc.Bacc("TRN2", target_bir_lowering=False, num_devices=1)
    arrays, args = {}, []
    for name in _INS:
        a = _np.ascontiguousarray(inputs[name])
        arrays[f"in_{name}"] = a
        args.append(nc.dram_tensor(f"in_{name}", a.shape, _mybir.dt.from_np(a.dtype), kind="ExternalInput").ap())
    args.append(nc.dram_tensor("out_dram", (N_NODES, DIM), _mybir.dt.float32, kind="ExternalOutput").ap())
    gnn_moe_program(nc, *args)
    r = _run(nc, [arrays], core_ids=[0])
    return r.results[0]["out_dram"]
```

```python
from contextlib import ExitStack

import concourse.bass as bass
from concourse import mybir

N_NODES, DIM, N_EDGES = 6250, 256, 200000
HEADS, HEAD_DIM = 4, 64
EXPERTS, ROUTER_H = 6, 128
SLOPE, LN_EPS, SUM_EPS = 0.2, 1e-5, 1e-16
P = 128

NW = -(-N_NODES // P)
LAST_ROWS = N_NODES - (NW - 1) * P
TILES = 4
GE = TILES * P
NG = -(-N_EDGES // GE)
UNROLL = 6
FILL = 2
STEPS = NG + NW - 1
CHUNKS = 4
assert STEPS <= CHUNKS * P and NG <= CHUNKS * P
SORT_P = 125
SORT_T = N_EDGES // SORT_P
assert SORT_P * SORT_T == N_EDGES
HC = HEAD_DIM + 1
ROW = HEADS * HC
BIG = 1.0e30
CAP = 1.0e18
PAD_DST = 1 << 20
BW = 7
NB = NW // BW
BN = BW * P
HALF = BN // 2
TT = 256
REGION = NW * P + TT
NT = (2 * NW * P + EXPERTS * (TT - 1)) // TT
assert NT % 2 == 0 and NT >= 8
SUM_LINKS, ROUTE_LINKS = 5, 35

def order_edges(nc, block, ctx, src, dst, src_pad, dst_pad, arena, pads, pads_set, edges_copied, bank, load_first_x):
    f32, i32 = mybir.dt.float32, mybir.dt.int32
    ALU, AX = mybir.AluOpType, mybir.AxisListType
    E = SORT_P
    flat_s = src_pad.rearrange("g e -> (g e)")
    flat_d = dst_pad.rearrange("g e -> (g e)")

    def sem(name):
        return ctx.enter_context(nc.semaphore(name))

    limit_set, dst_in, src_in, odd_count, odd_sum, order_known = (
        sem(n) for n in ("limit_set", "dst_in", "src_in", "odd_count", "odd_sum", "order_known"))
    sort_ones, sort_consts, sort_step, sort_onehot, sort_prod, sort_turned, sort_looked, sort_pos, sort_free, sort_stored, sort_base = (
        sem(f"sort_{n}") for n in ("ones", "consts", "step", "onehot", "prod", "turned", "looked", "pos", "free", "stored", "base"))

    used = [0]

    def part(cols, parts=E):
        at = used[0]
        used[0] += cols
        return arena[0:parts, at:at + cols]

    dst_next = part(SORT_T + 1).bitcast(i32)
    edge_i = part(2 * SORT_T).bitcast(i32).rearrange("p (t c) -> p t c", c=2)
    edge_f = part(2 * SORT_T).rearrange("p (t c) -> p t c", c=2)
    temp = part(SORT_T)
    temp_i = temp.bitcast(i32)
    src_raw = edge_f.rearrange("p t c -> p (t c)")[:, 0:SORT_T].bitcast(i32)
    ones, odd = part(P, P), part(1)
    flag = part(1, 1).bitcast(i32)
    ident, later, iota = part(P, P), part(P, P), part(P)
    lo_hot, hi_hot, lo_hot_t, diag, same, hit = part(P), part(NW), part(P, P), part(P), part(P), part(NW)
    count, below, base = part(NW, P), part(NW, P), part(NW, P)
    now_f, now_i, now_d = part(2), part(2).bitcast(i32), part(1)
    rank, first, pos_i = part(1), part(1), part(1).bitcast(i32)

    def sorting_needed(eng):
        eng.wait_ge(order_known, 1)
        return eng.value_load(flag[0:1, 0:1], min_val=0, max_val=N_EDGES)

    @block.sync
    def _(sp):
        sp.wait_ge(limit_set, 1)
        by_part = dst.rearrange("(p t) -> p t", p=E)
        sp.dma_start(dst_next[:, 0:SORT_T], by_part).then_inc(dst_in, 16)
        with nc.allow_non_contiguous_dma(reason="one word per partition"):
            sp.dma_start(dst_next[0:E - 1, SORT_T:SORT_T + 1], by_part[1:E, 0:1]).then_inc(dst_in, 16)
        sp.wait_ge(pads_set, 2)
        sp.dma_start(flat_d[GE:GE + N_EDGES], dst).then_inc(edges_copied, 16)
        sp.dma_start(flat_s[GE:GE + N_EDGES], src).then_inc(edges_copied, 16)
        tail = (NG + 1) * GE - GE - N_EDGES
        sp.dma_start(flat_d[0:GE].unsqueeze(0), pads[0:1, 0:GE]).then_inc(edges_copied, 16)
        sp.dma_start(flat_d[GE + N_EDGES:(NG + 1) * GE].unsqueeze(0), pads[0:1, GE:GE + tail]).then_inc(edges_copied, 16)
        sp.dma_start(flat_s[0:GE].unsqueeze(0), pads[0:1, 0:GE]).then_inc(edges_copied, 16)
        sp.dma_start(flat_s[GE + N_EDGES:(NG + 1) * GE].unsqueeze(0), pads[0:1, 0:tail]).then_inc(edges_copied, 16)
        load_first_x(sp)
        sp.wait_ge(edges_copied, 96)
        with sp.If(sorting_needed(sp) > 0):
            sp.dma_start(src_raw, src.rearrange("(p t) -> p t", p=E)).then_inc(src_in, 16)

    @block.gpsimd
    def _(pool):
        pool.memset(pads[0:1, 0:GE], 0).then_inc(pads_set, 1)
        pool.memset(pads[0:1, GE:2 * GE], PAD_DST).then_inc(pads_set, 1)
        with pool.If(sorting_needed(pool) > 0):
            pool.memset(ident, 0.0).then_inc(sort_step, 1)
            pool.memset(later, 1.0).then_inc(sort_step, 1)
            pool.wait_ge(sort_step, 2)
            pool.affine_select(out=ident, in_=ident, compare_op=ALU.not_equal, fill=1.0,
                               base=0, pattern=[[-1, P]], channel_multiplier=1).then_inc(sort_consts, 1)
            pool.affine_select(out=later, in_=later, compare_op=ALU.is_ge, fill=0.0,
                               base=-1, pattern=[[1, P]], channel_multiplier=-1).then_inc(sort_consts, 1)
            pool.iota(iota, [[1, P]], base=0, channel_multiplier=0,
                      allow_small_or_imprecise_dtypes=True).then_inc(sort_consts, 1)
            pool.wait_ge(edges_copied, 96)
            pool.memset(pads[0:1, 0:1], 0).then_inc(sort_free, 1)
            with pool.Fori(0, SORT_T) as t:
                pool.wait_ge(sort_pos, t + 1)
                pool.nop(nofuse=True)
                for flat, c in ((flat_d, 0), (flat_s, 1)):
                    pool.indirect_dma_start(flat.unsqueeze(1), bass.IndirectOffsetOnAxis(ap=pos_i[:, 0:1], axis=0),
                                            now_i[:, c:c + 1], None).then_inc(sort_stored, 16)
                pool.wait_ge(sort_stored, t * 32 + 32)
                pool.nop(nofuse=True)
                pool.memset(pads[0:1, 0:1], 0).then_inc(sort_free, 1)

    @block.tensor
    def _(pe):
        pe.wait_ge(sort_ones, 1)
        pe.wait_ge(odd_count, 2)
        pe.matmul(bank[0][0:1, 0:1], odd, ones[0:E, 0:1], start=True, stop=True).then_inc(odd_sum, 1)
        with pe.If(sorting_needed(pe) > 0):
            pe.wait_ge(sort_consts, 3)
            with pe.Fori(0, SORT_T) as t:
                pe.wait_ge(sort_onehot, t + 1)
                pe.matmul(bank[2][:, 0:NW], lo_hot, hi_hot, start=True, stop=True).then_inc(sort_prod, 1)
            pe.wait_ge(sort_base, 1)
            pe.matmul(bank[4][:, 0:NW], ones, below, start=True, stop=False)
            pe.matmul(bank[4][:, 0:NW], later, count, start=False, stop=True).then_inc(sort_base, 1)
            with pe.Fori(0, SORT_T) as t:
                pe.wait_ge(sort_onehot, t + (SORT_T + 1))
                pe.transpose(bank[0][:, 0:E], lo_hot, ident[0:E, 0:E])
                pe.matmul(bank[1][0:E, 0:E], ones[0:E, 0:E], diag[:, 0:E], start=True, stop=True)
                pe.matmul(bank[2][:, 0:NW], lo_hot, hi_hot, start=True, stop=True).then_inc(sort_prod, 1)
                pe.wait_ge(sort_turned, t + 1)
                pe.matmul(bank[3][0:E, 0:NW], lo_hot_t[:, 0:E], base, start=True, stop=True).then_inc(sort_looked, 1)

    @block.vector
    def _(dve):
        dve.memset(dst_next[:, SORT_T:SORT_T + 1], PAD_DST).then_inc(limit_set, 1)
        dve.memset(ones, 1.0).then_inc(sort_ones, 1)
        dve.wait_ge(dst_in, 32)
        dve.tensor_tensor(temp, dst_next[:, 0:SORT_T], dst_next[:, 1:SORT_T + 1], ALU.is_gt).then_inc(odd_count, 1)
        dve.wait_ge(odd_count, 1)
        dve.tensor_reduce(odd, temp, AX.X, ALU.add).then_inc(odd_count, 1)
        dve.wait_ge(odd_sum, 1)
        dve.tensor_copy(flag[0:1, 0:1], bank[0][0:1, 0:1]).then_inc(order_known, 1)
        with dve.If(sorting_needed(dve) > 0):
            links = [2]

            def link(ins):
                links[0] += 1
                ins.then_inc(sort_step, 1)
                dve.wait_ge(sort_step, links[0])

            dve.wait_ge(sort_consts, 3)
            dve.wait_ge(src_in, 16)
            link(dve.tensor_copy(edge_i[:, :, 1:2], src_raw.unsqueeze(2)))
            link(dve.tensor_copy(edge_i[:, :, 0:1], dst_next[:, 0:SORT_T].unsqueeze(2)))
            link(dve.tensor_single_scalar(temp_i, dst_next[:, 0:SORT_T], 7, ALU.arith_shift_right))
            link(dve.tensor_copy(edge_f[:, :, 1:2], temp_i.unsqueeze(2)))
            link(dve.tensor_single_scalar(temp_i, dst_next[:, 0:SORT_T], P - 1, ALU.bitwise_and))
            link(dve.tensor_copy(edge_f[:, :, 0:1], temp_i.unsqueeze(2)))
            link(dve.memset(count, 0.0))

            def turn(t, at, links_per_turn):
                n = [0]

                def go(ins):
                    n[0] += 1
                    assert n[0] <= links_per_turn
                    ins.then_inc(sort_step, 1)
                    dve.wait_ge(sort_step, t * links_per_turn + (at + n[0]))
                return go

            def one_hots(t, go):
                go(dve.tensor_copy(now_f.unsqueeze(1), edge_f[:, bass.ds(t, 1), :]))
                go(dve.tensor_scalar(lo_hot, iota, now_f[:, 0:1], None, ALU.is_equal))
                go(dve.tensor_scalar(hi_hot, iota[:, 0:NW], now_f[:, 1:2], None, ALU.is_equal))

            start, COUNT_LINKS = links[0], 4
            with dve.Fori(0, SORT_T) as t:
                go = turn(t, start, COUNT_LINKS)
                one_hots(t, go)
                dve.memset(odd, 0.0).then_inc(sort_onehot, 1)
                dve.wait_ge(sort_prod, t + 1)
                go(dve.tensor_tensor(count, count, bank[2][:, 0:NW], ALU.add))
            links[0] += SORT_T * COUNT_LINKS
            link(dve.memset(below, 0.0))
            for j in range(1, NW):
                link(dve.tensor_tensor(below[:, j:j + 1], below[:, j - 1:j], count[:, j - 1:j], ALU.add))
            dve.memset(odd, 0.0).then_inc(sort_base, 1)
            dve.wait_ge(sort_base, 2)
            link(dve.tensor_copy(base, bank[4][:, 0:NW]))

            start, PLACE_LINKS = links[0], 14
            with dve.Fori(0, SORT_T) as t:
                go = turn(t, start, PLACE_LINKS)
                dve.wait_ge(sort_free, t + 1)
                go(dve.tensor_copy(now_i.unsqueeze(1), edge_i[:, bass.ds(t, 1), :]))
                go(dve.tensor_copy(now_d, now_i[:, 0:1]))
                one_hots(t, go)
                go(dve.tensor_scalar(diag, ident[0:E, :], now_d[:, 0:1], None, ALU.mult))
                dve.memset(odd, 0.0).then_inc(sort_onehot, 1)
                dve.wait_ge(sort_prod, t + (SORT_T + 1))
                go(dve.tensor_copy(lo_hot_t[:, 0:E], bank[0][:, 0:E]))
                dve.memset(odd, 0.0).then_inc(sort_turned, 1)
                go(dve.scalar_tensor_tensor(same[:, 0:E], bank[1][0:E, 0:E], now_d[:, 0:1], later[0:E, 0:E], ALU.is_equal, ALU.mult))
                go(dve.tensor_reduce(rank, same[:, 0:E], AX.X, ALU.add))
                dve.wait_ge(sort_looked, t + 1)
                go(dve.tensor_tensor(hit, bank[3][0:E, 0:NW], hi_hot, ALU.mult))
                go(dve.tensor_reduce(first, hit, AX.X, ALU.add))
                go(dve.tensor_tensor(first, first, rank, ALU.add))
                go(dve.tensor_single_scalar(pos_i, first, float(GE), ALU.add))
                dve.memset(odd, 0.0).then_inc(sort_pos, 1)
                go(dve.tensor_tensor(base, base, bank[2][:, 0:NW], ALU.add))


def gnn_moe_program(nc, x, src, dst, gat_w, att_src, att_dst, gat_bias, r_w1, r_b1, r_w2, r_b2,
                    e_w1, e_b1, e_w2, e_b2, e_w3, e_b3, out):
    f32, i32, bf16 = mybir.dt.float32, mybir.dt.int32, mybir.dt.bfloat16
    ALU, ACT, AX = mybir.AluOpType, mybir.ActivationFunctionType, mybir.AxisListType

    src_pad = nc.dram_tensor("src_pad", [NG + 1, GE], i32, kind="Internal").ap()
    dst_pad = nc.dram_tensor("dst_pad", [NG + 1, GE], i32, kind="Internal").ap()
    node_rows = nc.dram_tensor("node_rows", [NW * P, ROW], f32, kind="Internal").ap()
    flag_rows = nc.dram_tensor("flag_rows", [CHUNKS * P, TILES, HEADS, P], f32, kind="Internal").ap()
    slot_rows = nc.dram_tensor("slot_rows", [EXPERTS * REGION, DIM], f32, kind="Internal").ap()
    expert_rows = nc.dram_tensor("expert_rows", [NT * TT, DIM], f32, kind="Internal").ap()
    window_list = nc.dram_tensor("window_list", [CHUNKS * P], i32, kind="Internal").ap()

    with ExitStack() as ctx:
        def sb(name, cols, dt=f32, parts=P):
            return ctx.enter_context(nc.sbuf_tensor(name, [parts, cols], dt))

        def sem(name):
            return ctx.enter_context(nc.semaphore(name))

        def sems(name, n):
            return [sem(f"{name}{i}") for i in range(n)]

        acc = sb("acc", NW * ROW)
        state = sb("state", NW * 8)
        parts3 = sb("parts3", NW * 24, bf16)
        ident = sb("ident", P)
        ident_b = sb("ident_b", P, bf16)
        iota_b = sb("iota_b", P, bf16)
        waug = sb("waug", 2 * (ROW + HEADS))
        ew1, ew2, ew3 = (sb(f"ew{i}", EXPERTS * 2 * 256) for i in (1, 2, 3))
        eb1, eb2 = (sb(f"eb{i}", EXPERTS * 2) for i in (1, 2))
        eb3 = sb("eb3", EXPERTS * DIM)
        rw1, rb1, rw2, rb2 = sb("rw1", 2 * ROUTER_H), sb("rb1", 1), sb("rw2", EXPERTS), sb("rb2", EXPERTS)
        gbias = sb("gbias", DIM)
        eps = sb("eps", 1)

        arena = sb("arena", UNROLL * (TILES * ROW + 2 * TILES * P))
        rows_at, oh_at = 0, UNROLL * TILES * ROW
        ohb_at = oh_at + UNROLL * TILES * P
        oht_at = ohb_at + UNROLL * TILES * P // 2
        column_data = sb("column_data", 3 * CHUNKS * P * TILES)
        columns = column_data[:, :].rearrange("p (s c) -> p s c", c=3 * TILES)
        flag_ring = sb("flag_ring", UNROLL * P, parts=16)
        scan_ring = sb("scan_ring", UNROLL * P, parts=16)
        idx_ring = sb("idx_ring", UNROLL * TILES, i32)
        col_ring = sb("col_ring", UNROLL * 2 * TILES)
        seg_ring = sb("seg_ring", UNROLL * 16, bf16)
        part_ring = sb("part_ring", UNROLL * 24, bf16)
        top = sb("top", HEADS)
        top_e = sb("top_e", HEADS)
        top_l = sb("top_l", HEADS)
        fall = sb("fall", UNROLL * HEADS)
        keep = sb("keep", UNROLL * HEADS)
        zsum = sb("zsum", 16)
        zlr = sb("zlr", 16)
        zexp = sb("zexp", UNROLL * 16)
        wexp = sb("wexp", UNROLL * 16)
        windows = sb("windows", CHUNKS * P, i32, parts=1)

        def rows(u):
            return arena[:, rows_at + u * TILES * ROW:rows_at + (u + 1) * TILES * ROW]

        def onehot32(u):
            return arena[:, oh_at + u * TILES * P:oh_at + (u + 1) * TILES * P]

        def onehot(u):
            return arena[:, ohb_at + u * TILES * P // 2:ohb_at + (u + 1) * TILES * P // 2].bitcast(bf16)

        def onehot_t(u):
            return arena[:, oht_at + u * TILES * P // 2:oht_at + (u + 1) * TILES * P // 2].bitcast(bf16)

        dst_i = arena[:, 0:2048].bitcast(i32)
        src_i = arena[:, 2048:4096].bitcast(i32)
        rel_q = arena[:, 4096:6144]
        change = arena[:, 6144:8192 + 4]
        end_q = arena[:, 8200:10248]
        src_f = arena[:, 10248:12296]
        before = column_data[:, 0:2048]
        iota_step = column_data[:, 2048:2560]
        tri = column_data[:, 2560:2688]
        ones = column_data[:, 2688:2816]
        small = sb("small", 96)
        step_no = small[:, 0:4]
        width = small[:, 4:12].rearrange("p (c two) -> p c two", two=2)
        shifted = small[:, 12:16]
        cum = small[:, 16:20]
        found = small[:, 20:28]
        win_f = small[:, 28:32]
        neg_w = small[:, 32:36]
        prev_f = small[:, 36:44]
        ints = sb("ints", 40, i32)
        prev_first, prev_last = ints[:, 0:4], ints[:, 4:8]
        prev_first_w, prev_last_w = ints[:, 8:12], ints[:, 12:16]
        group_no, win_i, first_w = ints[:, 16:20], ints[:, 20:24], ints[:, 24:28]
        pads = sb("pads", 2 * GE, i32, parts=1)

        xn0 = [arena[:, 4096 + i * BW * DIM:4096 + (i + 1) * BW * DIM] for i in (0, 1)]
        xnt0 = arena[:, 7680:8192]
        attb, att_prod = arena[:, 8192:8704], arena[:, 8704:8960]
        least = sb("least", 24)
        ad_rest = sb("ad_rest", 2 * NW * HEADS)
        ynt, rht = arena[:, 0:2 * BN], arena[:, 2 * BN:3 * BN]
        zeros = arena[:, 4736:5248]
        later, ones3 = arena[:, 4480:4608], arena[:, 4608:4736]
        xg, xt, h1t, h2t, og = ([arena[:, 5248 + (2 * n + i) * 512:5248 + (2 * n + i + 1) * 512] for i in (0, 1)] for n in range(5))
        w1_now, w2_now = ([column_data[:, (2 * n + i) * 512:(2 * n + i + 1) * 512] for i in (0, 1)] for n in range(2))
        picked = [arena[:, i * 2 * BW * DIM:(i + 1) * 2 * BW * DIM] for i in (0, 1)]
        at = [10400]

        def late(cols):
            at[0] += cols
            assert at[0] <= UNROLL * (TILES * ROW + 2 * TILES * P)
            return arena[:, at[0] - cols:at[0]]

        pos_all, picked_at, gate_all = late(NW * 2), late(NW * 2).bitcast(i32), late(NW * 2)
        pos_now, gate_now = [late(2 * BW).bitcast(i32) for i in (0, 1)], [late(2 * BW) for i in (0, 1)]
        row_count, region_base, both, pos_e, pos_f, hit = late((BW + 1) * EXPERTS), late(EXPERTS), late(42), late(42), late(2 * BW), late(42)
        tile_no, tile_end, tile_n, tile_e, tile_first, tile_hit = late(NT), late(EXPERTS), late(EXPERTS), late(NT), late(NT), late(NT * EXPERTS)
        tiles_i, expert_list, start_list, fill_list = (late(n).bitcast(i32) for n in (EXPERTS, NT, NT, EXPERTS))
        xblk = [column_data[:, i * BW * DIM:(i + 1) * BW * DIM] for i in (0, 1)]
        y = [sb(f"y{i}", BW * DIM) for i in (0, 1)]
        yn = [column_data[:, 2 * BW * DIM:3 * BW * DIM], arena[:, 3 * BN:3 * BN + BW * DIM]]
        stats3 = sb("stats3", BW * 6)
        mv3 = [sb(f"mv3_{i}", BW * 2) for i in (0, 1)]
        std = [sb(f"std{i}", BW) for i in (0, 1)]
        rstd = [sb(f"rstd{i}", BW) for i in (0, 1)]
        rsum28 = sb("rsum28", BW * HEADS)
        rt = sb("rt", 12 * BW * EXPERTS)
        rev = sb("rev", BW * EXPERTS)

        bank = [ctx.enter_context(nc.psum_tensor(f"bank{i}", [P, 512], f32)) for i in range(8)]

        gat_in, bounds_ready = sem("gat_in"), sem("bounds_ready")
        weights_in, xblk_in = sem("weights_in"), sems("xblk_in", 2)
        consts = sem("consts")
        const_step = sem("const_step")
        dve_link = sem("dve_link")
        pads_set = sem("pads_set")
        edges_copied, bounds_in = sem("edges_copied"), sem("bounds_in")
        cum_ps, before_set, found_ps, groups_set = sem("cum_ps"), sem("before_set"), sem("found_ps"), sem("groups_set")
        group_rows_in = sem("group_rows_in")
        sched_set, flags_out, windows_out, windows_in = sem("sched_set"), sem("flags_out"), sem("windows_out"), sem("windows_in")
        col_ps, col_copied = sem("col_ps"), sem("col_copied")
        x_in = sems("x_in", 2)
        p1_stats, p1_var, p1_std, p1_rstd, p1_xn = (sem(f"p1_{n}") for n in ("stats", "var", "std", "rstd", "xn"))
        p1_xt_ps, p1_xt, p1_h, p1_acc, p1_ad = (sem(f"p1_{n}") for n in ("xt_ps", "xt", "h", "acc", "ad"))
        least_turn, least_ps, least_row, least_all = sem("least_turn"), sem("least_ps"), sem("least_row"), sem("least_all")
        shifted_set, self_fall, self_weight = sem("shifted_set"), sem("self_fall"), sem("self_weight")
        node_rows_out, waug_set = sem("node_rows_out"), sem("waug_set")

        idx_ready = sem("idx_ready")
        rows_in = sems("rows_in", UNROLL)
        flags_in = sems("flags_in", UNROLL)
        (cols_set, onehot_set, onehot32_set, oht_ps, oht_set, score_ps, scanned, scan_ps, seg_set, px_ps, parts_set,
         top_set, tope_set, lr_set, newmax_set, fall_set, keep_set, max_stored, ex_ps, zsum_set, zlr_set,
         z_set, wexp_set, w_set, msg_set, agg_ps, scaled, added) = (
            sem(n) for n in ("cols_set onehot_set onehot32_set oht_ps oht_set score_ps scanned scan_ps seg_set px_ps "
                             "parts_set top_set tope_set lr_set newmax_set fall_set keep_set max_stored "
                             "ex_ps zsum_set zlr_set z_set wexp_set w_set msg_set agg_ps scaled added").split())
        p3_y, p3_stats, p3_var, p3_std, p3_rstd, p3_yn, p3_yt_ps, p3_yt, p3_rh_ps, p3_rh, p3_lg_ps = (
            sem(f"p3_{n}") for n in ("y", "stats", "var", "std", "rstd", "yn", "yt_ps", "yt", "rh_ps", "rh", "lg_ps"))
        p3_ex_in, p3_ex_out, p3_e2_in, p3_e2_out = (sem(f"p3_{n}") for n in ("ex_in", "ex_out", "e2_in", "e2_out"))
        moe_consts, moe_step, sums_set, res_saved, both_set, rank_ps, pos_set, route_link = (
            sem(n) for n in ("moe_consts", "moe_step", "sums_set", "res_saved", "both_set", "rank_ps", "pos_set", "route_link"))
        scattered, lists_set, filled, xg_in = sems("scattered", 2), sem("lists_set"), sem("filled"), sems("xg_in", 2)
        xt_ps, xt_set, h1_ps, h1_set, h2_ps, h2_set, o_ps, og_set, expert_out = (
            sem(n) for n in ("xt_ps", "xt_set", "h1_ps", "h1_set", "h2_ps", "h2_set", "o_ps", "og_set", "expert_out"))
        w1_set, w2_set, picks_set = sem("w1_set"), sem("w2_set"), sem("picks_set")
        pos_staged, gates_staged, first_added, gate_used = (
            sem(n) for n in ("pos_staged", "gates_staged", "first_added", "gate_used"))
        picked_in = sems("picked_in", 2)
        block_done, stored = sem("block_done"), sems("stored", 2)

        N_BOUNDS = 8
        N_WEIGHTS = 4 + 3 * EXPERTS + 3 + 1

        def load_x(sp, b, to, done):
            last = P if b < NB - 1 else LAST_ROWS
            sp.dma_start(to[:, 0:(BW - 1) * DIM].rearrange("p (t d) -> p t d", d=DIM),
                         x[b * BN:b * BN + (BW - 1) * P, :].rearrange("(t p) d -> p t d", p=P)).then_inc(done, 16)
            sp.dma_start(to[0:last, (BW - 1) * DIM:BW * DIM],
                         x[b * BN + (BW - 1) * P:b * BN + (BW - 1) * P + last, :]).then_inc(done, 16)


        with nc.Block() as block:
            order_edges(nc, block, ctx, src, dst, src_pad, dst_pad, arena, pads, pads_set, edges_copied, bank,
                        lambda sp: (load_x(sp, 0, y[0], x_in[0]), load_x(sp, 1, y[1], x_in[1])))

        block = ctx.enter_context(nc.Block())

        def iterate_blocks(eng, run):
            for b in range(2):
                run(b, b, True)
            with eng.Fori(1, NB // 2) as it:
                for par in range(2):
                    run(it * 2 + par, par, True)
            run(NB - 1, (NB - 1) % 2, False)

        def iterate_tiles(eng, first, last, body):
            lo, hi = 2, (NT - 4) // 2
            for k in range(first, 2 * lo):
                body(k // 2, k % 2, lambda off: 0 <= k + off < NT)
            with eng.Fori(lo, hi) as it:
                for u in range(2):
                    body(it, u, lambda off: True)
            for k in range(2 * hi, last):
                body(k // 2, k % 2, lambda off: 0 <= k + off < NT)

        @block.sync
        def _(sp):
            for k in range(2):
                o = k * (ROW + HEADS)
                sp.dma_start(waug[:, o:o + ROW].rearrange("p (h c) -> p h c", c=HC)[:, :, 0:HEAD_DIM],
                             gat_w[k * P:(k + 1) * P, :].rearrange("p (h c) -> p h c", c=HEAD_DIM)).then_inc(gat_in, 16)
            sp.dma_start(attb[:, 0:DIM], att_src.rearrange("h c -> (h c)").partition_broadcast(P)).then_inc(gat_in, 16)
            sp.dma_start(attb[:, DIM:2 * DIM], att_dst.rearrange("h c -> (h c)").partition_broadcast(P)).then_inc(gat_in, 16)
            sp.dma_start(gbias[:, :], gat_bias.partition_broadcast(P)).then_inc(gat_in, 16)
            sp.wait_ge(bounds_ready, 1)
            with nc.allow_non_contiguous_dma(reason="one word per group"):
                for c in range(CHUNKS):
                    n = min(P, NG - c * P)
                    sp.dma_start(prev_first[0:n, c:c + 1], dst_pad[c * P:c * P + n, 0:1]).then_inc(bounds_in, 16)
                    sp.dma_start(prev_last[0:n, c:c + 1], dst_pad[c * P:c * P + n, GE - 1:GE]).then_inc(bounds_in, 16)
            for b in range(2, NB):
                sp.wait_ge(p1_xn, BW * (b - 1))
                load_x(sp, b, y[b % 2], x_in[b % 2])
            for k in range(2):
                sp.dma_start(rw1[:, k * ROUTER_H:(k + 1) * ROUTER_H], r_w1[k * P:(k + 1) * P, :]).then_inc(weights_in, 16)
            sp.dma_start(rw2[:, :], r_w2).then_inc(weights_in, 16)
            sp.dma_start(rb2[:, :], r_b2.partition_broadcast(P)).then_inc(weights_in, 16)
            for w, d in ((ew1, e_w1), (ew2, e_w2), (ew3, e_w3)):
                for e in range(EXPERTS):
                    sp.dma_start(w[:, e * 512:(e + 1) * 512].rearrange("p (k n) -> p k n", k=2),
                                 d[e, :, :].rearrange("(k p) n -> p k n", p=P)).then_inc(weights_in, 16)
            with nc.allow_non_contiguous_dma(reason="biases one word per partition"):
                sp.dma_start(rb1[:, :], r_b1.rearrange("(p o) -> p o", o=1)).then_inc(weights_in, 16)
                sp.dma_start(eb1[:, :].rearrange("p (e m) -> p e m", m=2), e_b1.rearrange("e (m p) -> p e m", p=P)).then_inc(weights_in, 16)
                sp.dma_start(eb2[:, :].rearrange("p (e m) -> p e m", m=2), e_b2.rearrange("e (m p) -> p e m", p=P)).then_inc(weights_in, 16)
            sp.dma_start(eb3[:, :], e_b3.rearrange("e d -> (e d)").partition_broadcast(P)).then_inc(weights_in, 16)
            sp.wait_ge(shifted_set, 1)
            for b in range(NB):
                sp.dma_start(node_rows[b * BN:(b + 1) * BN, :].rearrange("(t p) c -> p t c", p=P),
                             acc[:, b * BW * ROW:(b + 1) * BW * ROW].rearrange("p (t c) -> p t c", c=ROW)).then_inc(node_rows_out, 16)
            sp.wait_ge(sched_set, 1)
            for q in range(CHUNKS):
                for h in range(HEADS):
                    sp.dma_start(flag_rows[q * P:(q + 1) * P, :, h, :],
                                 change[:, q * GE:(q + 1) * GE].rearrange("p (j e) -> p j e", j=TILES)).then_inc(flags_out, 16)
            with nc.allow_non_contiguous_dma(reason="one word per step"):
                sp.dma_start(window_list.rearrange("(q p) -> p q", p=P), win_i).then_inc(windows_out, 16)
            sp.wait_ge(windows_out, 16)
            sp.dma_start(windows[0:1, :], window_list.unsqueeze(0)).then_inc(windows_in, 16)
            sp.wait_ge(flags_out, 16 * CHUNKS * HEADS)

            def load_flags(s, u):
                sp.dma_start(flag_ring[:, u * P:(u + 1) * P],
                             flag_rows[bass.ds(s, 1), :, :, :].rearrange("s j h e -> (s j h) e")).then_inc(flags_in[u], 16)

            for s in range(UNROLL):
                load_flags(s, s)
            with sp.Fori(1, STEPS // UNROLL) as it:
                for u in range(UNROLL):
                    sp.wait_ge(scanned, it * UNROLL + (u - UNROLL + 1))
                    load_flags(it * UNROLL + u, u)
            for s in range(STEPS // UNROLL * UNROLL, STEPS):
                sp.wait_ge(scanned, s - UNROLL + 1)
                load_flags(s, s % UNROLL)

            sp.wait_ge(cols_set, STEPS)
            sp.wait_ge(idx_ready, STEPS)
            load_x(sp, 0, xblk[0], xblk_in[0])
            load_x(sp, 1, xblk[1], xblk_in[1])
            for b in range(2, NB):
                sp.wait_ge(sums_set, b - 1)
                load_x(sp, b, xblk[b % 2], xblk_in[b % 2])

            sp.wait_ge(moe_consts, 5)
            sp.wait_ge(lists_set, 1)
            for e in range(EXPERTS):
                row = sp.value_load(fill_list[0:1, e:e + 1], min_val=e * REGION, max_val=(e + 1) * REGION - TT)
                sp.dma_start(slot_rows[bass.ds(row, TT), :].rearrange("(p s) d -> p (s d)", s=2), zeros).then_inc(filled, 16)
            sp.wait_ge(filled, 16 * EXPERTS)
            for par in (0, 1):
                sp.wait_ge(scattered[par], 16 * 2 * BW * ((NB + 1 - par) // 2))

            def start_of(j):
                return sp.value_load(start_list[0:1, bass.ds(j, 1)], min_val=0, max_val=EXPERTS * REGION - TT)

            def sp_tile(it, u, on):
                k = it * 2 + u
                if on(4):
                    if on(2):
                        sp.wait_ge(xt_ps, k + 3)
                        sp.nop(nofuse=True)
                    sp.dma_start(xg[u], slot_rows[bass.ds(start_of(k + 4), TT), :].rearrange("(p s) d -> p (s d)", s=2)).then_inc(xg_in[u], 16)
                if on(0):
                    sp.wait_ge(og_set, k + 1)
                    sp.nop(nofuse=True)
                    if on(-1):
                        sp.wait_ge(expert_out, 16 * k)
                    sp.nop(nofuse=True)
                    sp.dma_start(expert_rows[bass.ds(k * TT, TT), :].rearrange("(p s) d -> p (s d)", s=2), og[u]).then_inc(expert_out, 16)

            iterate_tiles(sp, -4, NT, sp_tile)

            for b in range(NB):
                sp.wait_ge(block_done, b + 1)
                last = P if b < NB - 1 else LAST_ROWS
                sp.dma_start(out[b * BN:b * BN + (BW - 1) * P, :].rearrange("(t p) d -> p t d", p=P),
                             y[b % 2][:, 0:(BW - 1) * DIM].rearrange("p (t d) -> p t d", d=DIM)).then_inc(stored[b % 2], 16)
                sp.dma_start(out[b * BN + (BW - 1) * P:b * BN + (BW - 1) * P + last, :],
                             y[b % 2][0:last, (BW - 1) * DIM:BW * DIM]).then_inc(stored[b % 2], 16)
            for par in range(2):
                sp.wait_ge(stored[par], 32 * ((NB + 1 - par) // 2))

        @block.gpsimd
        def _(pool):
            pool.memset(ident[:, :], 0.0).then_inc(const_step, 1)
            pool.memset(ident_b[:, :], 0.0).then_inc(const_step, 1)
            pool.memset(tri, 1.0).then_inc(const_step, 1)
            pool.wait_ge(const_step, 3)
            for m in (ident, ident_b):
                pool.affine_select(out=m[:, :], in_=m[:, :], compare_op=ALU.not_equal, fill=1.0,
                                   base=0, pattern=[[-1, P]], channel_multiplier=1).then_inc(consts, 1)
            pool.affine_select(out=tri, in_=tri, compare_op=ALU.is_ge, fill=0.0,
                               base=0, pattern=[[1, P]], channel_multiplier=-1).then_inc(consts, 1)
            pool.iota(iota_b[:, :], [[1, P]], base=0, channel_multiplier=0,
                      allow_small_or_imprecise_dtypes=True).then_inc(consts, 1)
            pool.iota(iota_step, [[1, CHUNKS * P]], base=1, channel_multiplier=0,
                      allow_small_or_imprecise_dtypes=True).then_inc(consts, 1)
            pool.iota(step_no, [[P, CHUNKS]], base=1, channel_multiplier=1,
                      allow_small_or_imprecise_dtypes=True).then_inc(consts, 1)
            pool.iota(rev[:, :], [[0, BW], [-1, EXPERTS]], base=EXPERTS, channel_multiplier=0,
                      allow_small_or_imprecise_dtypes=True).then_inc(consts, 1)
            pool.memset(ones, 1.0).then_inc(consts, 1)
            pool.memset(eps[:, :], LN_EPS).then_inc(consts, 1)
            pool.wait_ge(groups_set, 1)
            for q in range(CHUNKS):
                for to, table in ((dst_i, dst_pad), (src_i, src_pad)):
                    pool.indirect_dma_start(to[:, q * GE:(q + 1) * GE], None, table,
                                            bass.IndirectOffsetOnAxis(ap=group_no[:, q:q + 1], axis=0)).then_inc(group_rows_in, 16)
            pool.wait_ge(node_rows_out, 16 * NB)

            def gather(u):
                for j in range(TILES):
                    pool.indirect_dma_start(rows(u)[:, j * ROW:(j + 1) * ROW], None, node_rows,
                                            bass.IndirectOffsetOnAxis(ap=idx_ring[:, u * TILES + j:u * TILES + j + 1], axis=0)
                                            ).then_inc(rows_in[u], 16)

            for u in range(UNROLL):
                pool.wait_ge(idx_ready, u + 1)
                gather(u)
            with pool.Fori(1, STEPS // UNROLL) as it:
                for u in range(UNROLL):
                    pool.wait_ge(idx_ready, it * UNROLL + (u + 1))
                    pool.wait_ge(agg_ps, it * UNROLL + (u - UNROLL + 1))
                    pool.nop(nofuse=True)
                    gather(u)
            for s in range(STEPS // UNROLL * UNROLL, STEPS):
                pool.wait_ge(idx_ready, s + 1)
                pool.wait_ge(agg_ps, s - UNROLL + 1)
                gather(s % UNROLL)

            pool.wait_ge(added, STEPS)
            pool.memset(later, 1.0).then_inc(moe_step, 1)
            pool.wait_ge(moe_step, 1)
            pool.affine_select(out=later, in_=later, compare_op=ALU.is_ge, fill=0.0,
                               base=-1, pattern=[[1, P]], channel_multiplier=-1).then_inc(moe_consts, 1)
            pool.memset(ones3, 1.0).then_inc(moe_consts, 1)
            pool.memset(zeros, 0.0).then_inc(moe_consts, 1)
            pool.iota(region_base, [[REGION, EXPERTS]], base=0, channel_multiplier=0,
                      allow_small_or_imprecise_dtypes=True).then_inc(moe_consts, 1)
            pool.iota(tile_no, [[1, NT]], base=0, channel_multiplier=0,
                      allow_small_or_imprecise_dtypes=True).then_inc(moe_consts, 1)

            def scatter_rows(b, par, has_next):
                pool.wait_ge(pos_set, b + 1)
                pool.nop(nofuse=True)
                for r in range(2):
                    for t in range(BW):
                        pool.indirect_dma_start(slot_rows, bass.IndirectOffsetOnAxis(ap=pos_now[par][:, r * BW + t:r * BW + t + 1], axis=0),
                                                yn[par][:, t * DIM:(t + 1) * DIM], None).then_inc(scattered[par], 16)

            iterate_blocks(pool, scatter_rows)
            pool.wait_ge(expert_out, 16 * NT)

            def pick_rows(b, par, has_next):
                pool.wait_ge(pos_staged, b + 1)
                pool.nop(nofuse=True)
                for t in range(BW):
                    for r in range(2):
                        pool.indirect_dma_start(picked[par][:, (r * BW + t) * DIM:(r * BW + t + 1) * DIM], None, expert_rows,
                                                bass.IndirectOffsetOnAxis(ap=pos_now[par][:, r * BW + t:r * BW + t + 1], axis=0)
                                                ).then_inc(picked_in[par], 16)

            iterate_blocks(pool, pick_rows)

        FIRST_IT, LAST_IT = 2, STEPS // UNROLL - 1

        def iterate(eng, body):
            for k in range(-1, FIRST_IT * UNROLL):
                body(k // UNROLL, k % UNROLL, lambda off: 0 <= k + off < STEPS)
            with eng.Fori(FIRST_IT, LAST_IT) as it:
                for u in range(UNROLL):
                    body(it, u, lambda off: True)
            for k in range(LAST_IT * UNROLL, STEPS + 2):
                body(k // UNROLL, k % UNROLL, lambda off: 0 <= k + off < STEPS)

        @block.scalar
        def _(act):
            act.wait_ge(consts, 9)

            def p1_take(t):
                s = t % 2
                act.wait_ge(p1_h, t + 1)
                act.activation(acc[:, t * ROW:(t + 1) * ROW], bank[2 + s][:, 0:ROW], ACT.Copy).then_inc(p1_acc, 1)
                act.activation(state[:, t * 8 + 4:t * 8 + 8], bank[2 + s][:, ROW:ROW + HEADS], ACT.Copy).then_inc(p1_ad, 1)

            def p1_std_of(b):
                act.wait_ge(p1_var, BW * (b + 1))
                act.activation(std[b % 2][:, :].unsqueeze(2), mv3[b % 2][:, :].rearrange("p (t two) -> p t two", two=2)[:, :, 1:2],
                               ACT.Sqrt, bias=eps[:, 0:1]).then_inc(p1_std, 1)

            p1_std_of(0)
            for b in range(NB):
                for i in range(BW):
                    t = b * BW + i
                    if i == 2 and b + 1 < NB:
                        p1_std_of(b + 1)
                    act.wait_ge(p1_xt_ps, t + 1)
                    act.activation(xnt0[:, t % 2 * DIM:(t % 2 + 1) * DIM], bank[t % 2][:, 0:DIM], ACT.Copy).then_inc(p1_xt, 1)
                    if t:
                        p1_take(t - 1)
            p1_take(NW - 1)
            act.wait_ge(self_fall, 1)
            act.activation(ad_rest[:, NW * HEADS:2 * NW * HEADS], ad_rest[:, 0:NW * HEADS], ACT.Exp).then_inc(self_weight, 1)
            n = 0
            for q in range(CHUNKS):
                for c in range(3):
                    act.wait_ge(col_ps, n + 1)
                    act.activation(columns[:, q * P:(q + 1) * P, c * TILES:(c + 1) * TILES].rearrange("p s j -> p j s"),
                                   bank[4 + n % 2][:, :].rearrange("p (j s) -> p j s", j=TILES), ACT.Copy).then_inc(col_copied, 1)
                    n += 1
            act.wait_ge(col_copied, n)
            act.wait_ge(flags_out, 16 * CHUNKS * HEADS)
            act.wait_ge(windows_in, 16)

            def stage_columns(it, u):
                at = columns[:, bass.ds(it * UNROLL + u, 1), :]
                act.activation(idx_ring[:, u * TILES:(u + 1) * TILES], at[:, :, 2 * TILES:3 * TILES].rearrange("p s c -> p (s c)"),
                               ACT.Copy).then_inc(idx_ready, 1)
                act.activation(col_ring[:, u * 8:u * 8 + 8], at[:, :, 0:2 * TILES].rearrange("p s c -> p (s c)"),
                               ACT.Copy).then_inc(cols_set, 1)

            for u in range(2):
                stage_columns(0, u)

            seen = {}

            def window_of(it, u):
                return act.value_load(windows[0:1, bass.ds(it * UNROLL + u, 1)], min_val=0, max_val=NW - 1)

            def act_iter(it, u, on):
                k = it * UNROLL + u
                v = (u - 1) % UNROLL
                if on(-1):
                    act.wait_ge(fall_set, k)
                    act.activation(keep[:, v * HEADS:(v + 1) * HEADS], fall[:, v * HEADS:(v + 1) * HEADS], ACT.Exp).then_inc(keep_set, 1)
                if on(-2):
                    u2 = (u - 2) % UNROLL
                    w = seen[u2] if u >= 3 else window_of(it + (u - 2) // UNROLL, u2)
                    act.wait_ge(keep_set, k - 1)
                    if on(-3):
                        act.wait_ge(added, k - 2)
                    act.nop(nofuse=True)
                    for h in range(HEADS):
                        part = acc[:, bass.ds(w * ROW + h * HC, HC)]
                        last = act.activation(part, part, ACT.Copy, scale=keep[:, u2 * HEADS + h:u2 * HEADS + h + 1])
                    last.then_inc(scaled, 1)
                if on(3):
                    it3, u3 = it + (u + 3) // UNROLL, (u + 3) % UNROLL
                    if not isinstance(it3, int) or it3 > 0:
                        act.wait_ge(rows_in[u3], it3 * (16 * TILES))
                        act.nop(nofuse=True)
                    stage_columns(it3, u3)
                if on(-1):
                    act.wait_ge(z_set, k)
                    act.activation(wexp[:, v * 16:v * 16 + 16], zexp[:, v * 16:v * 16 + 16], ACT.Exp).then_inc(wexp_set, 1)
                if on(1):
                    n = (u + 1) % UNROLL
                    act.wait_ge(onehot_set, k + 2)
                    act.activation(onehot32(n), onehot(n), ACT.Copy).then_inc(onehot32_set, 1)
                    act.wait_ge(oht_ps, k + 2)
                    act.activation(onehot_t(n), bank[n % 2][:, :].bitcast(bf16)[:, 0:TILES * P], ACT.Copy).then_inc(oht_set, 1)
                    w = seen[n] = window_of(it + (u + 1) // UNROLL, n)
                    act.activation(part_ring[:, n * 24:(n + 1) * 24], parts3[:, bass.ds(w * 24, 24)], ACT.Copy).then_inc(parts_set, 1)

            iterate(act, act_iter)

            act.wait_ge(weights_in, 16 * N_WEIGHTS)
            act.wait_ge(added, STEPS)

            def norm_act(b, par):
                act.wait_ge(p3_var, (b + 1) * BW)
                act.activation(std[par][:, :].unsqueeze(2), mv3[par][:, :].rearrange("p (t two) -> p t two", two=2)[:, :, 1:2],
                               ACT.Sqrt, bias=eps[:, 0:1]).then_inc(p3_std, 1)

            def turn_act(b, par):
                for g in range(4):
                    nt = 2 if g < 3 else 1
                    act.wait_ge(p3_yt_ps, b * 4 + (g + 1))
                    act.activation(ynt.rearrange("p (k n) -> p k n", k=2)[:, :, 2 * g * P:(2 * g + nt) * P]
                                   .rearrange("p k (t n) -> p t k n", t=nt),
                                   bank[6 + g % 2][:, 0:nt * DIM].rearrange("p (t k n) -> p t k n", t=nt, k=2),
                                   ACT.Copy).then_inc(p3_yt, 1)

            def router_act(b, par):
                act.wait_ge(sums_set, b + 1)
                act.nop(nofuse=True)
                act.activation(acc[:, bass.ds(b * (BW * ROW), BW * ROW)].rearrange("p (t c) -> p t c", c=ROW)[:, :, 0:DIM],
                               y[par][:, :].rearrange("p (t d) -> p t d", d=DIM), ACT.Copy).then_inc(res_saved, 1)
                for half in range(2):
                    act.wait_ge(p3_rh_ps, b * 2 + (half + 1))
                    act.activation(rht[:, half * HALF:(half + 1) * HALF], bank[6 + half][:, 0:HALF], ACT.Relu,
                                   bias=rb1[:, 0:1]).then_inc(p3_rh, 1)

            def act_block(b, par, has_next):
                if has_next:
                    norm_act(b + 1, 1 - par)
                act.wait_ge(p3_ex_in, b + 1)
                act.activation(rt[:, 42:84], rt[:, 0:42], ACT.Exp).then_inc(p3_ex_out, 1)
                act.wait_ge(p3_e2_in, b + 1)
                act.activation(rt[:, 7 * 42 + 7:7 * 42 + 14], rt[:, 7 * 42:7 * 42 + 7], ACT.Exp).then_inc(p3_e2_out, 1)
                if has_next:
                    turn_act(b + 1, 1 - par)
                    router_act(b + 1, 1 - par)

            norm_act(0, 0)
            turn_act(0, 0)
            router_act(0, 0)
            iterate_blocks(act, act_block)

            act.wait_ge(lists_set, 1)

            def expert_of(j):
                return act.value_load(expert_list[0:1, bass.ds(j, 1)], min_val=0, max_val=EXPERTS - 1)

            def hidden_act(j, par, first, to, bias, from_bank, ready, free, done):
                e = expert_of(j)
                act.wait_ge(ready, j + 1)
                if not first:
                    act.wait_ge(free, j - 1)
                act.nop(nofuse=True)
                for m in range(2):
                    act.activation(to[par][:, m * TT:(m + 1) * TT], from_bank[:, m * TT:(m + 1) * TT], ACT.Relu,
                                   bias=bias[:, bass.ds(e * 2 + m, 1)]).then_inc(done, 1)

            def act_tile(it, u, on):
                k = it * 2 + u
                if on(2):
                    act.wait_ge(xt_ps, k + 3)
                    if on(0):
                        act.wait_ge(h1_ps, k + 1)
                        act.nop(nofuse=True)
                    act.activation(xt[u], bank[u][:, :], ACT.Copy).then_inc(xt_set, 1)
                if on(1):
                    hidden_act(k + 1, 1 - u, not on(-1), h1t, eb1, bank[3 - u], h1_ps, h2_ps, h1_set)
                if on(0):
                    hidden_act(k, u, not on(-2), h2t, eb2, bank[4 + u], h2_ps, o_ps, h2_set)

            iterate_tiles(act, -2, NT, act_tile)

            def stage_block(b, par, has_next):
                if isinstance(b, int) and b < 2:
                    act.wait_ge(picks_set, 1)
                act.wait_ge(gate_used, b + 1)
                act.activation(pos_now[par], picked_at[:, bass.ds(b * 2 * BW, 2 * BW)], ACT.Copy).then_inc(pos_staged, 1)
                act.activation(gate_now[par], gate_all[:, bass.ds(b * 2 * BW, 2 * BW)], ACT.Copy).then_inc(gates_staged, 1)

            iterate_blocks(act, stage_block)

        @block.tensor
        def _(pe):
            pe.wait_ge(consts, 9)

            def p1_turn(t):
                pe.wait_ge(p1_xn, t + 1)
                if t >= 2:
                    pe.wait_ge(p1_xt, t - 1)
                b, i = t // BW, t % BW
                for kk in range(2):
                    last = pe.transpose(bank[t % 2][:, kk * P:(kk + 1) * P], xn0[b % 2][:, i * DIM + kk * P:i * DIM + (kk + 1) * P], ident[:, :])
                last.then_inc(p1_xt_ps, 1)

            def p1_project(t):
                s = t % 2
                pe.wait_ge(p1_xt, t + 1)
                if t >= 2:
                    pe.wait_ge(p1_ad, t - 1)
                for kk in range(2):
                    last = pe.matmul(bank[2 + s][:, 0:ROW + HEADS], xnt0[:, s * DIM + kk * P:s * DIM + (kk + 1) * P],
                                     waug[:, kk * (ROW + HEADS):(kk + 1) * (ROW + HEADS)], start=(kk == 0), stop=(kk == 1))
                last.then_inc(p1_h, 1)

            p1_turn(0)
            pe.wait_ge(waug_set, 1)
            for t in range(NW):
                if t + 1 < NW:
                    p1_turn(t + 1)
                p1_project(t)
                if t == 0:
                    pe.wait_ge(before_set, 1)
                    pe.matmul(bank[6][:, 0:CHUNKS], tri, width[:, :, 1:2].rearrange("p c o -> p (c o)"), start=True, stop=False)
                    pe.matmul(bank[6][:, 0:CHUNKS], ones, shifted, start=False, stop=True).then_inc(cum_ps, 1)
                    pe.wait_ge(before_set, 2)
                    for q in range(CHUNKS):
                        for c in range(CHUNKS):
                            last = pe.matmul(bank[7][:, 2 * q:2 * q + 2], before[:, c * 512 + q * P:c * 512 + (q + 1) * P],
                                             width[:, c, :], start=(c == 0), stop=(c == CHUNKS - 1))
                    last.then_inc(found_ps, 1)
            pe.wait_ge(least_turn, 1)
            pe.transpose(bank[6][0:HEADS, 0:P], least[:, 0:HEADS], ident[:, :]).then_inc(least_ps, 1)
            pe.wait_ge(least_row, 1)
            pe.matmul(bank[7][:, 0:HEADS], ones[0:HEADS, :], least[0:HEADS, 8:12], start=True, stop=True).then_inc(least_all, 1)
            pe.wait_ge(sched_set, 1)
            n = 0
            for q in range(CHUNKS):
                for of in (rel_q, end_q, src_f):
                    if n >= 2:
                        pe.wait_ge(col_copied, n - 1)
                    for j in range(TILES):
                        last = pe.transpose(bank[4 + n % 2][:, j * P:(j + 1) * P], of[:, q * GE + j * P:q * GE + (j + 1) * P], ident[:, :])
                    last.then_inc(col_ps, 1)
                    n += 1

            def pe_iter(it, u, on):
                k = it * UNROLL + u
                v = (u - 1) % UNROLL

                def sum_rows(tiles):
                    for j in tiles:
                        last = pe.matmul(bank[6 + v % 2][:, 0:ROW], onehot32(v)[:, j * P:(j + 1) * P],
                                         rows(v)[:, j * ROW:(j + 1) * ROW], start=(j == 0), stop=(j == TILES - 1))
                    return last

                if on(0):
                    pe.wait_ge(scanned, k + 1)
                    pe.nop(nofuse=True)
                    pe.transpose(bank[3][:, 0:16], scan_ring[:, u * P:(u + 1) * P], ident[0:16, 0:16]).then_inc(scan_ps, 1)
                if on(1):
                    n = (u + 1) % UNROLL
                    pe.wait_ge(onehot_set, k + 2)
                    if on(-1):
                        pe.wait_ge(oht_set, k)
                    for j in range(TILES):
                        last = pe.transpose(bank[n % 2][:, :].bitcast(bf16)[:, j * P:(j + 1) * P], onehot(n)[:, j * P:(j + 1) * P], ident_b[:, :])
                    last.then_inc(oht_ps, 1)
                if on(0):
                    pe.wait_ge(seg_set, k + 1)
                    for j in range(TILES):
                        last = pe.matmul(bank[4][:, j * 4:j * 4 + 4], onehot(u)[:, j * P:(j + 1) * P],
                                         seg_ring[:, u * 16 + j * 4:u * 16 + j * 4 + 4], start=True, stop=True)
                    last.then_inc(px_ps, 1)
                if on(-1):
                    if on(-3):
                        pe.wait_ge(added, k - 2)
                    for _ in range(FILL):
                        pe.matmul(bank[6 + v % 2][:, 0:512], ident_b[:, :], onehot(u)[:, 0:512], start=True, stop=True)
                    pe.wait_ge(onehot32_set, k)
                    pe.wait_ge(msg_set, (k - 1) * TILES + 2)
                    sum_rows(range(0, TILES // 2))
                if on(0):
                    pe.wait_ge(oht_set, k + 1)
                    pe.wait_ge(newmax_set, k + 1)
                    for j in range(TILES):
                        for part in range(3):
                            last = pe.matmul(bank[5][:, j * 8:j * 8 + 8], onehot_t(u)[:, j * P:(j + 1) * P],
                                             part_ring[:, u * 24 + part * 8:u * 24 + part * 8 + 8],
                                             start=(part == 0), stop=(part == 2))
                    last.then_inc(ex_ps, 1)
                if on(1):
                    n = (u + 1) % UNROLL
                    pe.wait_ge(rows_in[n], (it + (u + 1) // UNROLL + 1) * (16 * TILES))
                    scores = rows(n).rearrange("p (r c) -> p r c", c=HC)[:, :, HEAD_DIM:HC].rearrange("p r o -> p (r o)")
                    pe.transpose(bank[2][0:16, 0:P], scores, ident[:, :]).then_inc(score_ps, 1)
                if on(-1):
                    pe.wait_ge(msg_set, k * TILES)
                    sum_rows(range(TILES // 2, TILES)).then_inc(agg_ps, 1)

            iterate(pe, pe_iter)

            pe.wait_ge(weights_in, 16 * N_WEIGHTS)

            pe.wait_ge(moe_consts, 5)

            def turn_pe(b, par):
                pe.wait_ge(p3_yn, b + 1)
                for g in range(4):
                    nt = 2 if g < 3 else 1
                    if g >= 2:
                        pe.wait_ge(p3_yt, b * 4 + (g - 1))
                    for i in range(nt):
                        t = 2 * g + i
                        for kk in range(2):
                            last = pe.transpose(bank[6 + g % 2][:, (2 * i + kk) * P:(2 * i + kk + 1) * P],
                                                yn[par][:, t * DIM + kk * P:t * DIM + (kk + 1) * P], ident[:, :])
                    last.then_inc(p3_yt_ps, 1)

            def router_pe(b, par):
                pe.wait_ge(p3_yt, b * 4 + 4)
                for half in range(2):
                    for kk in range(2):
                        last = pe.matmul(bank[6 + half][:, 0:HALF], rw1[:, kk * ROUTER_H:(kk + 1) * ROUTER_H],
                                         ynt[:, kk * BN + half * HALF:kk * BN + (half + 1) * HALF],
                                         start=(kk == 0), stop=(kk == 1))
                    last.then_inc(p3_rh_ps, 1)
                pe.wait_ge(p3_rh, b * 2 + 2)
                for t in range(BW):
                    last = pe.matmul(bank[3 + par][:, t * EXPERTS:(t + 1) * EXPERTS], rht[:, t * P:(t + 1) * P], rw2[:, :],
                                     start=True, stop=True)
                last.then_inc(p3_lg_ps, 1)

            def pe_block(b, par, has_next):
                pe.wait_ge(both_set, b + 1)
                pe.matmul(bank[5][:, 0:42], later, both, start=True, stop=True)
                pe.matmul(bank[5][:, 42:84], ones3, both, start=True, stop=True).then_inc(rank_ps, 1)
                if has_next:
                    turn_pe(b + 1, 1 - par)
                    router_pe(b + 1, 1 - par)

            turn_pe(0, 0)
            router_pe(0, 0)
            iterate_blocks(pe, pe_block)

            pe.wait_ge(lists_set, 1)

            def expert_of(j):
                return pe.value_load(expert_list[0:1, bass.ds(j, 1)], min_val=0, max_val=EXPERTS - 1)

            def hidden_pe(j, w, w_ready, frm, to_bank, ready, done):
                pe.wait_ge(w_ready, j + 1)
                pe.wait_ge(*ready)
                pe.nop(nofuse=True)
                for m in range(2):
                    for kk in range(2):
                        last = pe.matmul(to_bank[:, m * TT:(m + 1) * TT], w[:, kk * 256 + m * P:kk * 256 + (m + 1) * P],
                                         frm[:, kk * TT:(kk + 1) * TT], start=(kk == 0), stop=(kk == 1))
                last.then_inc(done, 1)

            def pe_tile(it, u, on):
                k = it * 2 + u
                if on(2):
                    pe.wait_ge(xg_in[u], it * 16 + 32)
                    if on(0):
                        pe.wait_ge(xt_set, k + 1)
                        pe.nop(nofuse=True)
                    for s in range(2):
                        for kk in range(2):
                            last = pe.transpose(bank[u][:, kk * TT + s * P:kk * TT + (s + 1) * P],
                                                xg[u][:, s * DIM + kk * P:s * DIM + (kk + 1) * P], ident[:, :])
                    last.then_inc(xt_ps, 1)
                if on(1):
                    if on(-1):
                        pe.wait_ge(h1_set, k * 2)
                    hidden_pe(k + 1, w1_now[1 - u], w1_set, xt[1 - u], bank[3 - u], (xt_set, k + 2), h1_ps)
                if on(0):
                    if on(-2):
                        pe.wait_ge(h2_set, k * 2 - 2)
                    hidden_pe(k, w2_now[u], w2_set, h1t[u], bank[4 + u], (h1_set, k * 2 + 2), h2_ps)
                if on(-1):
                    e = expert_of(k - 1)
                    if on(-3):
                        pe.wait_ge(og_set, k - 2)
                    pe.wait_ge(h2_set, k * 2)
                    pe.nop(nofuse=True)
                    for s in range(2):
                        for kk in range(2):
                            last = pe.matmul(bank[7 - u][:, s * DIM:(s + 1) * DIM], h2t[1 - u][:, kk * TT + s * P:kk * TT + (s + 1) * P],
                                             ew3[:, bass.ds(e * 512 + kk * 256, 256)], start=(kk == 0), stop=(kk == 1))
                    last.then_inc(o_ps, 1)

            iterate_tiles(pe, -2, NT + 1, pe_tile)

        @block.vector
        def _(dve):
            links = [0]

            def link(ins):
                links[0] += 1
                ins.then_inc(dve_link, 1)
                dve.wait_ge(dve_link, links[0])

            def p1_norm(b):
                xb, mv, n0 = y[b % 2], mv3[b % 2], b * BW
                dve.wait_ge(x_in[b % 2], 32 * (b // 2 + 1))
                if b >= 2:
                    dve.wait_ge(p1_h, n0 - BW)
                for i in range(BW):
                    dve.bn_stats(stats3[:, i * 6:(i + 1) * 6], xb[:, i * DIM:(i + 1) * DIM]).then_inc(p1_stats, 1)
                for i in range(BW):
                    dve.wait_ge(p1_stats, n0 + i + 1)
                    dve.bn_aggr(mv[:, 2 * i:2 * i + 2], stats3[:, i * 6:(i + 1) * 6]).then_inc(p1_var, 1)

            def p1_apply(b):
                xb, mv, n0 = y[b % 2], mv3[b % 2], b * BW
                dve.wait_ge(p1_std, b + 1)
                dve.reciprocal(rstd[b % 2][:, :], std[b % 2][:, :]).then_inc(p1_rstd, 1)
                dve.wait_ge(p1_rstd, b + 1)
                for i in range(BW):
                    dve.tensor_scalar(xn0[b % 2][:, i * DIM:(i + 1) * DIM], xb[:, i * DIM:(i + 1) * DIM],
                                      mv[:, 2 * i:2 * i + 1], rstd[b % 2][:, i:i + 1], ALU.subtract, ALU.mult).then_inc(p1_xn, 1)

            link(dve.memset(ints[:, 3:4], 0))
            link(dve.memset(ints[:, 7:8], P * 1000))
            dve.memset(small[:, 60:61], 0.0).then_inc(bounds_ready, 1)
            p1_norm(0)
            dve.wait_ge(gat_in, 16 * 5)
            for kk in range(2):
                o = kk * (ROW + HEADS)
                feats = waug[:, o:o + ROW].rearrange("p (h c) -> p h c", c=HC)
                for which in range(2):
                    link(dve.tensor_tensor(att_prod.rearrange("p (h c) -> p h c", h=HEADS), feats[:, :, 0:HEAD_DIM],
                                           attb[:, which * DIM:(which + 1) * DIM].rearrange("p (h c) -> p h c", h=HEADS), ALU.mult))
                    to = feats[:, :, HEAD_DIM:HC] if which == 0 else waug[:, o + ROW:o + ROW + HEADS].unsqueeze(2)
                    link(dve.tensor_reduce(to, att_prod.rearrange("p (h c) -> p h c", h=HEADS), AX.X, ALU.add))
            dve.memset(small[:, 59:60], 0.0).then_inc(waug_set, 1)
            p1_apply(0)
            dve.wait_ge(consts, 9)
            dve.wait_ge(bounds_in, 16 * N_BOUNDS)
            link(dve.tensor_single_scalar(ints[:, 8:16], ints[:, 0:8], 7, ALU.arith_shift_right))
            link(dve.tensor_copy(prev_f, ints[:, 8:16]))
            link(dve.memset(width, 1.0))
            link(dve.scalar_tensor_tensor(width[:, :, 1:2].rearrange("p c o -> p (c o)"), prev_f[:, 4:8], 1.0, prev_f[:, 0:4], ALU.add, ALU.subtract))
            link(dve.memset(shifted, 0.0))
            for c in range(1, CHUNKS):
                link(dve.tensor_tensor(shifted[:, c:c + 1], shifted[:, c - 1:c], width[:, c - 1, 1:2], ALU.add))
            dve.memset(small[:, 61:62], 0.0).then_inc(before_set, 1)
            dve.wait_ge(cum_ps, 1)
            link(dve.tensor_copy(cum, bank[6][:, 0:CHUNKS]))
            for c in range(CHUNKS):
                link(dve.tensor_scalar(before[:, c * 512:(c + 1) * 512], iota_step, cum[:, c:c + 1], None, ALU.is_ge))
            dve.memset(small[:, 61:62], 0.0).then_inc(before_set, 1)
            dve.wait_ge(found_ps, 1)
            link(dve.tensor_copy(found, bank[7][:, 0:2 * CHUNKS]))
            counts = found.rearrange("p (q two) -> p q two", two=2)
            dve.tensor_copy(group_no, counts[:, :, 0:1].rearrange("p q o -> p (q o)")).then_inc(groups_set, 1)

            for b in range(1, NB):
                p1_norm(b)
                p1_apply(b)

            acc_all = acc[:, :].rearrange("p (t h c) -> p t h c", h=HEADS, c=HC)
            score_all = acc_all[:, :, :, HEAD_DIM:HC].rearrange("p t h o -> p t (h o)")
            st_all = state[:, :].rearrange("p (t c) -> p t c", c=8)
            dve.wait_ge(p1_acc, NW)
            dve.wait_ge(p1_ad, NW)
            dve.tensor_reduce(least[:, 0:HEADS].unsqueeze(2), score_all.rearrange("p t h -> p h t"), AX.X, ALU.min).then_inc(least_turn, 1)
            dve.wait_ge(least_ps, 1)
            link(dve.tensor_reduce(least[0:HEADS, 4:5], bank[6][0:HEADS, 0:P], AX.X, ALU.min))
            dve.tensor_scalar(least[0:HEADS, 8:12], ident[0:HEADS, 0:HEADS], least[0:HEADS, 4:5], None, ALU.mult).then_inc(least_row, 1)
            dve.wait_ge(least_all, 1)
            link(dve.tensor_copy(least[:, 12:16], bank[7][:, 0:HEADS]))
            least_w = least[:, 12:16].unsqueeze(1).to_broadcast([P, NW, HEADS])
            link(dve.tensor_tensor(score_all, score_all, least_w, ALU.subtract))
            dve.memset(small[:, 60:61], 0.0).then_inc(shifted_set, 1)
            link(dve.tensor_tensor(st_all[:, :, 4:8], st_all[:, :, 4:8], least_w, ALU.add))
            rest = [ad_rest[:, i * NW * HEADS:(i + 1) * NW * HEADS].rearrange("p (t h) -> p t h", h=HEADS) for i in (0, 1)]
            pr = parts3[:, :].rearrange("p (t c) -> p t c", c=24)
            link(dve.memset(parts3[:, :], 0.0))
            link(dve.tensor_copy(pr[:, :, 0:4], st_all[:, :, 4:8]))
            link(dve.tensor_tensor(rest[0], st_all[:, :, 4:8], pr[:, :, 0:4], ALU.subtract))
            link(dve.tensor_copy(pr[:, :, 8:12], rest[0]))
            link(dve.tensor_tensor(rest[1], rest[0], pr[:, :, 8:12], ALU.subtract))
            link(dve.tensor_copy(pr[:, :, 16:20], rest[1]))
            link(dve.tensor_tensor(rest[0], score_all, st_all[:, :, 4:8], ALU.add))
            link(dve.scalar_tensor_tensor(rest[1], rest[0], SLOPE, rest[0], ALU.mult, ALU.max))
            link(dve.tensor_copy(pr[:, :, 4:8], rest[1]))
            link(dve.tensor_copy(st_all[:, :, 0:4], pr[:, :, 4:8]))
            dve.tensor_tensor(rest[0], rest[1], st_all[:, :, 0:4], ALU.subtract).then_inc(self_fall, 1)

            dve.wait_ge(group_rows_in, 16 * 2 * CHUNKS)
            dst_q = dst_i.rearrange("p (q e) -> p q e", e=GE)
            link(dve.tensor_single_scalar(first_w, dst_q[:, :, 0:1].rearrange("p q o -> p (q o)"), 7, ALU.arith_shift_right))
            link(dve.tensor_copy(win_f, first_w))
            link(dve.tensor_tensor(win_f, win_f, step_no, ALU.add))
            link(dve.tensor_tensor(win_f, win_f, counts[:, :, 1:2].rearrange("p q o -> p (q o)"), ALU.subtract))
            link(dve.tensor_single_scalar(neg_w, win_f, -float(P), ALU.mult))
            link(dve.tensor_single_scalar(win_i, win_f, float(NW - 1), ALU.min))
            for q in range(CHUNKS):
                link(dve.tensor_scalar(rel_q[:, q * GE:(q + 1) * GE], dst_i[:, q * GE:(q + 1) * GE], neg_w[:, q:q + 1], None, ALU.add))
            rel3 = rel_q.rearrange("p (q e) -> p q e", e=GE)
            chg3 = change[:, 0:CHUNKS * GE].rearrange("p (q e) -> p q e", e=GE)
            link(dve.memset(chg3[:, :, 0:1], 0.0))
            link(dve.tensor_tensor(chg3[:, :, 1:GE], rel3[:, :, 1:GE], rel3[:, :, 0:GE - 1], ALU.not_equal))
            end3 = end_q.rearrange("p (r e) -> p r e", e=P)
            chr3 = change[:, 0:CHUNKS * GE].rearrange("p (r e) -> p r e", e=P)
            link(dve.tensor_copy(end3[:, :, 0:P - 1], chr3[:, :, 1:P]))
            link(dve.memset(end3[:, :, P - 1:P], 1.0))
            link(dve.tensor_single_scalar(change[:, 0:CHUNKS * GE], change[:, 0:CHUNKS * GE], -BIG, ALU.mult))
            link(dve.tensor_copy(src_f, src_i))
            dve.memset(small[:, 63:64], 0.0).then_inc(sched_set, 1)

            dve.wait_ge(self_weight, 1)
            dve.wait_ge(node_rows_out, 16 * NB)
            parts_all = acc[:, :].rearrange("p (r c) -> p r c", c=HC)
            link(dve.tensor_copy(parts_all[:, :, HEAD_DIM:HC], ad_rest[:, NW * HEADS:2 * NW * HEADS].unsqueeze(2)))
            link(dve.tensor_tensor(parts_all[:, :, 0:HEAD_DIM], parts_all[:, :, 0:HEAD_DIM],
                                   parts_all[:, :, HEAD_DIM:HC].to_broadcast([P, NW * HEADS, HEAD_DIM]), ALU.mult))

            dve.wait_ge(windows_in, 16)
            dve.wait_ge(col_copied, 3 * CHUNKS)
            dve.wait_ge(flags_out, 16 * CHUNKS * HEADS)

            wreg = {}

            def window_of(it, u):
                return dve.value_load(windows[0:1, bass.ds(it * UNROLL + u, 1)], min_val=0, max_val=NW - 1)

            def dve_iter(it, u, on):
                k = it * UNROLL + u
                v = (u - 1) % UNROLL
                scores = rows(v).rearrange("p (j h c) -> p j h c", h=HEADS, c=HC)[:, :, :, HEAD_DIM:HC].rearrange("p j h o -> p j (h o)")
                ex = bank[5][:, 0:32].rearrange("p (j c) -> p j c", c=8)

                def one_hot(tiles):
                    n = (u + 1) % UNROLL
                    for j in tiles:
                        last = dve.tensor_scalar(onehot(n)[:, j * P:(j + 1) * P], iota_b[:, :], col_ring[:, n * 8 + j:n * 8 + j + 1],
                                                 None, ALU.is_equal)
                    return last

                if on(0):
                    dve.wait_ge(flags_in[u], (it + 1) * 16)
                    dve.wait_ge(score_ps, k + 1)
                    dve.tensor_tensor_scan(scan_ring[:, u * P:(u + 1) * P], flag_ring[:, u * P:(u + 1) * P],
                                           bank[2][0:16, 0:P], -BIG, ALU.add, ALU.max).then_inc(scanned, 1)
                if on(-1):
                    dve.wait_ge(ex_ps, k)
                    dve.tensor_tensor(zsum[:, :].rearrange("p (j h) -> p j h", h=HEADS), scores, ex[:, :, 0:4], ALU.add).then_inc(zsum_set, 1)
                if on(1):
                    dve.wait_ge(cols_set, k + 2)
                    one_hot((0, 1))
                if on(-1):
                    dve.wait_ge(zsum_set, k)
                    dve.scalar_tensor_tensor(zlr[:, :], zsum[:, :], SLOPE, zsum[:, :], ALU.mult, ALU.max).then_inc(zlr_set, 1)
                if on(1):
                    one_hot((2,))
                if on(-1):
                    dve.wait_ge(zlr_set, k)
                    dve.tensor_tensor(zexp[:, v * 16:v * 16 + 16].rearrange("p (j h) -> p j h", h=HEADS),
                                      zlr[:, :].rearrange("p (j h) -> p j h", h=HEADS), ex[:, :, 4:8], ALU.subtract).then_inc(z_set, 1)
                if on(1):
                    one_hot((3,)).then_inc(onehot_set, 1)
                if on(0):
                    dve.wait_ge(scan_ps, k + 1)
                    dve.tensor_tensor(seg_ring[:, u * 16:u * 16 + 16].rearrange("p (j h) -> p j h", h=HEADS),
                                      bank[3][:, 0:16].rearrange("p (j h) -> p j h", h=HEADS),
                                      col_ring[:, u * 8 + 4:u * 8 + 8].unsqueeze(2).to_broadcast([P, TILES, HEADS]),
                                      ALU.mult).then_inc(seg_set, 1)
                if on(-1):
                    dve.wait_ge(wexp_set, k)
                    parts = rows(v).rearrange("p (r c) -> p r c", c=HC)
                    weight = wexp[:, v * 16:v * 16 + 16].unsqueeze(2)
                    dve.tensor_single_scalar(parts[:, :, HEAD_DIM:HC], weight, CAP, ALU.min).then_inc(w_set, 1)

                def weigh(j):
                    if on(-1):
                        r = slice(j * HEADS, (j + 1) * HEADS)
                        dve.scalar_tensor_tensor(parts[:, r, 0:HEAD_DIM], weight[:, r, :].to_broadcast([P, HEADS, HEAD_DIM]), CAP,
                                                 parts[:, r, 0:HEAD_DIM], ALU.min, ALU.mult).then_inc(msg_set, 1)

                weigh(0)
                weigh(1)
                if on(0):
                    w = wreg[u] = window_of(it, u)
                    new = part_ring[:, u * 24 + 4:u * 24 + 8]
                    dve.wait_ge(px_ps, k + 1)
                    dve.tensor_reduce(top[:, :].unsqueeze(2), bank[4][:, 0:16].rearrange("p (j h) -> p h j", h=HEADS), AX.X, ALU.max).then_inc(top_set, 1)
                weigh(2)
                if on(0):
                    dve.wait_ge(top_set, k + 1)
                    dve.tensor_tensor(top_e[:, :], top[:, :], state[:, bass.ds(w * 8 + 4, 4)], ALU.add).then_inc(tope_set, 1)
                weigh(3)
                if on(0):
                    dve.wait_ge(tope_set, k + 1)
                    dve.scalar_tensor_tensor(top_l[:, :], top_e[:, :], SLOPE, top_e[:, :], ALU.mult, ALU.max).then_inc(lr_set, 1)
                if on(-2):
                    u2 = (u - 2) % UNROLL
                    w2 = window_of(it + (u - 2) // UNROLL, u2) if u < 2 else wreg[u2]
                    here = acc[:, bass.ds(w2 * ROW, ROW)]
                    dve.wait_ge(scaled, k - 1)
                    dve.wait_ge(agg_ps, k - 1)
                    dve.tensor_tensor(here, here, bank[6 + u2 % 2][:, 0:ROW], ALU.add).then_inc(added, 1)
                if on(0):
                    dve.wait_ge(parts_set, k + 1)
                    if on(-1):
                        dve.wait_ge(max_stored, k)
                    dve.wait_ge(lr_set, k + 1)
                    dve.tensor_tensor(new, top_l[:, :], state[:, bass.ds(w * 8, 4)], ALU.max).then_inc(newmax_set, 1)
                    dve.wait_ge(newmax_set, k + 1)
                    dve.tensor_tensor(fall[:, u * HEADS:(u + 1) * HEADS], state[:, bass.ds(w * 8, 4)], new, ALU.subtract).then_inc(fall_set, 1)
                    dve.wait_ge(fall_set, k + 1)
                    dve.nop(nofuse=True)
                    dve.tensor_copy(state[:, bass.ds(w * 8, 4)], new).then_inc(max_stored, 1)

            iterate(dve, dve_iter)

            dve.wait_ge(weights_in, 16 * N_WEIGHTS)
            dve.wait_ge(added, STEPS)

            dve.wait_ge(moe_consts, 5)

            def block_links(signal, b, per_block):
                n = [0]

                def go(ins):
                    n[0] += 1
                    assert n[0] <= per_block, n
                    ins.then_inc(signal, 1)
                    dve.wait_ge(signal, b * per_block + n[0])
                    return n
                return go

            T = [rt[:, i * 42:(i + 1) * 42] for i in range(12)]
            C = [T[i].rearrange("p (t e) -> p t e", e=EXPERTS) for i in range(12)]
            REV = rev[:, :].rearrange("p (t e) -> p t e", e=EXPERTS)

            def one(i):
                return rt[:, 10 * 42 + i * 7:10 * 42 + (i + 1) * 7].unsqueeze(2)

            def wide(i):
                return one(i).to_broadcast([P, BW, EXPERTS])

            def sum_dve(b, par):
                yb, go = y[par], block_links(p3_y, b, SUM_LINKS)
                dve.wait_ge(xblk_in[par], (b + (2 - par)) * 16)
                if not isinstance(b, int) or b >= 2:
                    dve.wait_ge(res_saved, b - 1)
                    dve.nop(nofuse=True)
                ab = acc[:, bass.ds(b * (BW * ROW), BW * ROW)].rearrange("p (r c) -> p r c", c=HC)
                go(dve.tensor_scalar_add(rsum28[:, :].unsqueeze(2), ab[:, :, HEAD_DIM:HC], SUM_EPS))
                go(dve.reciprocal(rsum28[:, :], rsum28[:, :]))
                go(dve.tensor_tensor(yb[:, :].rearrange("p (r c) -> p r c", c=HEAD_DIM), ab[:, :, 0:HEAD_DIM],
                                     rsum28[:, :].unsqueeze(2).to_broadcast([P, BW * HEADS, HEAD_DIM]), ALU.mult))
                go(dve.tensor_tensor(yb[:, :].rearrange("p (t d) -> p t d", d=DIM), yb[:, :].rearrange("p (t d) -> p t d", d=DIM),
                                     gbias[:, :].unsqueeze(1).to_broadcast([P, BW, DIM]), ALU.add))
                go(dve.tensor_tensor(yb[:, :], yb[:, :], xblk[par][:, :], ALU.add))
                dve.memset(small[:, 60:61], 0.0).then_inc(sums_set, 1)

            def stats_dve(b, par):
                yb, mv = y[par], mv3[par]
                for t in range(BW):
                    dve.bn_stats(stats3[:, t * 6:(t + 1) * 6], yb[:, t * DIM:(t + 1) * DIM]).then_inc(p3_stats, 1)
                for t in range(BW):
                    dve.wait_ge(p3_stats, b * BW + (t + 1))
                    dve.nop(nofuse=True)
                    dve.bn_aggr(mv[:, 2 * t:2 * t + 2], stats3[:, t * 6:(t + 1) * 6]).then_inc(p3_var, 1)

            def norm_dve(b, par):
                yb, mv = y[par], mv3[par]
                dve.wait_ge(p3_std, b + 1)
                dve.reciprocal(rstd[par][:, :], std[par][:, :]).then_inc(p3_rstd, 1)
                dve.wait_ge(p3_rstd, b + 1)
                if not isinstance(b, int) or b >= 2:
                    dve.wait_ge(scattered[par], (b - par) * (16 * BW))
                    dve.nop(nofuse=True)
                for t in range(BW):
                    ins = dve.tensor_scalar(yn[par][:, t * DIM:(t + 1) * DIM], yb[:, t * DIM:(t + 1) * DIM], mv[:, 2 * t:2 * t + 1],
                                            rstd[par][:, t:t + 1], ALU.subtract, ALU.mult)
                ins.then_inc(p3_yn, 1)

            def route_dve(b, par):
                go = block_links(route_link, b, ROUTE_LINKS)
                dve.wait_ge(p3_lg_ps, b + 1)
                go(dve.tensor_tensor(C[2], bank[3 + par][:, 0:42].rearrange("p (t e) -> p t e", e=EXPERTS),
                                     rb2[:, :].unsqueeze(1).to_broadcast([P, BW, EXPERTS]), ALU.add))
                go(dve.tensor_reduce(one(0), C[2], AX.X, ALU.max))
                dve.tensor_tensor(C[0], C[2], wide(0), ALU.subtract).then_inc(p3_ex_in, 1)
                dve.wait_ge(p3_ex_out, b + 1)
                go(dve.tensor_reduce(one(1), C[1], AX.X, ALU.add))
                go(dve.reciprocal(one(2), one(1)))
                go(dve.tensor_tensor(C[3], C[1], wide(2), ALU.mult))
                for r in range(2):
                    prob, hot = C[3 + r], C[5 + r]
                    go(dve.tensor_reduce(one(3 + r), prob, AX.X, ALU.max))
                    go(dve.tensor_tensor(C[8], prob, wide(3 + r), ALU.is_equal))
                    go(dve.tensor_tensor(C[8], C[8], REV, ALU.mult))
                    go(dve.tensor_reduce(one(5), C[8], AX.X, ALU.max))
                    go(dve.tensor_tensor(hot, REV, wide(5), ALU.is_equal))
                    if r == 0:
                        go(dve.scalar_tensor_tensor(T[4], T[5], -2.0, T[3], ALU.mult, ALU.add))
                e2 = rt[:, 7 * 42 + 7:7 * 42 + 14]
                dve.tensor_tensor(rt[:, 7 * 42:7 * 42 + 7].unsqueeze(2), one(4), one(3), ALU.subtract).then_inc(p3_e2_in, 1)
                dve.tensor_tensor(both, T[5], T[6], ALU.add).then_inc(both_set, 1)
                dve.wait_ge(p3_e2_out, b + 1)
                gates = gate_now[par].rearrange("p (r t) -> p r t", r=2)
                go(dve.tensor_scalar_add(one(6), e2.unsqueeze(2), 1.0))
                go(dve.reciprocal(gates[:, 0, :].unsqueeze(2), one(6)))
                go(dve.tensor_tensor(gates[:, 1, :].unsqueeze(2), gates[:, 0, :].unsqueeze(2), e2.unsqueeze(2), ALU.mult))
                go(dve.tensor_copy(gate_all[:, bass.ds(b * 2 * BW, 2 * BW)], gate_now[par]))
                dve.wait_ge(rank_ps, b + 1)
                for t in range(BW):
                    go(dve.tensor_tensor(row_count[:, (t + 1) * EXPERTS:(t + 2) * EXPERTS], row_count[:, t * EXPERTS:(t + 1) * EXPERTS],
                                         bank[5][:, 42 + t * EXPERTS:42 + (t + 1) * EXPERTS], ALU.add))
                go(dve.tensor_tensor(pos_e, row_count[:, 0:42], bank[5][:, 0:42], ALU.add))
                go(dve.tensor_copy(row_count[:, 0:EXPERTS], row_count[:, 42:48]))
                if not isinstance(b, int) or b >= 2:
                    dve.wait_ge(scattered[par], (b - par) * (16 * BW))
                    dve.nop(nofuse=True)
                for r in range(2):
                    go(dve.tensor_tensor(hit, T[5 + r], pos_e, ALU.mult))
                    go(dve.tensor_reduce(pos_f[:, r * BW:(r + 1) * BW].unsqueeze(2), hit.rearrange("p (t e) -> p t e", e=EXPERTS), AX.X, ALU.add))
                go(dve.tensor_copy(pos_now[par], pos_f))
                n = go(dve.tensor_copy(pos_all[:, bass.ds(b * 2 * BW, 2 * BW)], pos_f))
                assert n[0] == ROUTE_LINKS, n
                dve.memset(small[:, 62:63], 0.0).then_inc(pos_set, 1)

            def dve_block(b, par, has_next):
                if has_next:
                    sum_dve(b + 1, 1 - par)
                    stats_dve(b + 1, 1 - par)
                route_dve(b, par)
                if has_next:
                    norm_dve(b + 1, 1 - par)

            link(dve.tensor_copy(row_count[:, 0:EXPERTS], region_base))
            sum_dve(0, 0)
            stats_dve(0, 0)
            norm_dve(0, 0)
            iterate_blocks(dve, dve_block)

            link(dve.tensor_copy(fill_list, row_count[:, 0:EXPERTS]))
            link(dve.tensor_tensor(tile_n, row_count[:, 0:EXPERTS], region_base, ALU.subtract))
            link(dve.tensor_scalar_add(tile_n, tile_n, float(TT - 1)))
            link(dve.tensor_copy(tiles_i, tile_n))
            link(dve.tensor_single_scalar(tiles_i, tiles_i, 8, ALU.arith_shift_right))
            link(dve.tensor_copy(tile_n, tiles_i))
            link(dve.tensor_copy(tile_end, tile_n))
            for e in range(1, EXPERTS):
                link(dve.tensor_tensor(tile_end[:, e:e + 1], tile_end[:, e:e + 1], tile_end[:, e - 1:e], ALU.add))
            E1 = EXPERTS - 1
            beyond = tile_hit[:, 0:NT * E1].rearrange("p (i e) -> p i e", e=E1)
            link(dve.tensor_tensor(beyond, tile_no.unsqueeze(2).to_broadcast([P, NT, E1]),
                                   tile_end[:, 0:E1].unsqueeze(1).to_broadcast([P, NT, E1]), ALU.is_ge))
            link(dve.tensor_reduce(tile_e.unsqueeze(2), beyond, AX.X, ALU.add))
            link(dve.tensor_tensor(beyond, beyond, tile_n[:, 0:E1].unsqueeze(1).to_broadcast([P, NT, E1]), ALU.mult))
            link(dve.tensor_reduce(tile_first.unsqueeze(2), beyond, AX.X, ALU.add))
            link(dve.tensor_tensor(tile_first, tile_no, tile_first, ALU.subtract))
            link(dve.tensor_single_scalar(tile_first, tile_first, float(TT), ALU.mult))
            link(dve.scalar_tensor_tensor(tile_first, tile_e, float(REGION), tile_first, ALU.mult, ALU.add))
            link(dve.tensor_scalar(tile_first, tile_first, row_count[:, E1:EXPERTS], None, ALU.min))
            link(dve.tensor_copy(expert_list, tile_e))
            link(dve.tensor_copy(start_list, tile_first))
            dve.memset(small[:, 63:64], 0.0).then_inc(lists_set, 1)
            link(dve.tensor_scalar(tile_n, tile_n, -float(TT), float(REGION), ALU.mult, ALU.add))
            shift = tile_hit[:, 0:2 * NW]
            total = tile_hit[:, 2 * NW:4 * NW]
            link(dve.memset(total, 0.0))
            for e in range(1, EXPERTS):
                link(dve.tensor_scalar(shift, pos_all, float(e * REGION), tile_n[:, e - 1:e], ALU.is_ge, ALU.mult))
                link(dve.tensor_tensor(total, total, shift, ALU.add))
            link(dve.tensor_tensor(total, pos_all, total, ALU.subtract))
            dve.tensor_copy(picked_at, total).then_inc(picks_set, 1)

            def take_weights(j, to, w, free, last_use, done):
                e = dve.value_load(expert_list[0:1, bass.ds(j, 1)], min_val=0, max_val=EXPERTS - 1)
                if last_use:
                    dve.wait_ge(free, j - 1)
                dve.nop(nofuse=True)
                dve.tensor_copy(to, w[:, bass.ds(e * 512, 512)]).then_inc(done, 1)

            def dve_tile(it, u, on):
                k = it * 2 + u
                if on(2):
                    take_weights(k + 2, w1_now[u], ew1, h1_ps, on(0), w1_set)
                if on(1):
                    take_weights(k + 1, w2_now[1 - u], ew2, h2_ps, on(-1), w2_set)
                if on(-1):
                    e = dve.value_load(expert_list[0:1, bass.ds(k - 1, 1)], min_val=0, max_val=EXPERTS - 1)
                    dve.wait_ge(o_ps, k)
                    if on(-3):
                        dve.wait_ge(expert_out, 16 * k - 32)
                    dve.nop(nofuse=True)
                    dve.tensor_tensor(og[1 - u].rearrange("p (s d) -> p s d", s=2), bank[7 - u][:, :].rearrange("p (s d) -> p s d", s=2),
                                      eb3[:, bass.ds(e * DIM, DIM)].unsqueeze(1).to_broadcast([P, 2, DIM]), ALU.add).then_inc(og_set, 1)

            iterate_tiles(dve, -2, NT + 1, dve_tile)
            dve.memset(small[:, 64:65], 0.0).then_inc(gate_used, 2)

            def add_block(b, par, has_next):
                dve.wait_ge(gates_staged, b + 1)
                dve.wait_ge(picked_in[par], (b + (2 - par)) * (16 * BW))
                if not isinstance(b, int) or b >= 2:
                    dve.wait_ge(stored[par], (b - par) * 16)
                for r in range(2):
                    for t in range(BW):
                        w = y[par][:, t * DIM:(t + 1) * DIM]
                        g, more = gate_now[par][:, r * BW + t:r * BW + t + 1], picked[par][:, (r * BW + t) * DIM:(r * BW + t + 1) * DIM]
                        if r == 0:
                            res = acc[:, bass.ds((b * BW + t) * ROW, DIM)]
                            dve.scalar_tensor_tensor(w, more, g, res, ALU.mult, ALU.add).then_inc(first_added, 1)
                        else:
                            dve.wait_ge(first_added, b * BW + (t + 1))
                            ins = dve.scalar_tensor_tensor(w, more, g, w, ALU.mult, ALU.add)
                ins.then_inc(block_done, 1)
                dve.memset(small[:, 65:66], 0.0).then_inc(gate_used, 1)

            iterate_blocks(dve, add_block)


_INS = ["x", "src", "dst", "L0_gnn_W", "L0_gnn_att_src", "L0_gnn_att_dst", "L0_gnn_bias", "L0_ffn_router_w1",
        "L0_ffn_router_b1", "L0_ffn_router_w2", "L0_ffn_router_b2", "L0_ffn_expert_w1", "L0_ffn_expert_b1",
        "L0_ffn_expert_w2", "L0_ffn_expert_b2", "L0_ffn_expert_w3", "L0_ffn_expert_b3"]


def kernel(**inputs):
    import numpy as _np
    import concourse.bacc as _bacc
    from concourse import mybir as _mybir
    from concourse.bass_utils import run_bass_kernel_spmd as _run

    nc = _bacc.Bacc("TRN2", target_bir_lowering=False, num_devices=1)
    arrays, args = {}, []
    for name in _INS:
        a = _np.ascontiguousarray(inputs[name])
        arrays[f"in_{name}"] = a
        args.append(nc.dram_tensor(f"in_{name}", a.shape, _mybir.dt.from_np(a.dtype), kind="ExternalInput").ap())
    args.append(nc.dram_tensor("out_dram", (N_NODES, DIM), _mybir.dt.float32, kind="ExternalOutput").ap())
    gnn_moe_program(nc, *args)
    r = _run(nc, [arrays], core_ids=[0])
    return r.results[0]["out_dram"]
```
